# Optimizing a Trainium2 kernel written in Bass

```python
import numpy as np
import jax
import jax.numpy as jnp

def _softmax(x, axis=-1):
    return jax.nn.softmax(x, axis=axis)

def _gelu(x):
    return jax.nn.gelu(x, approximate=True)

def _silu(x):
    return jax.nn.silu(x)

def _sigmoid(x):
    return jax.nn.sigmoid(x)

def _layernorm(x, axis=-1, eps=1e-05):
    m = jnp.mean(x, axis=axis, keepdims=True)
    v = jnp.var(x, axis=axis, keepdims=True)
    return (x - m) / jnp.sqrt(v + eps)

def _scatter_add(tgt, idx, src, axis=0):
    return tgt.at[idx].add(src)

def _segment_sum(src, seg, n):
    return jax.ops.segment_sum(src, seg, n)
kernel_name = 'mk_decoder_preln_d1_seqx_r8_a13c59'

def setup_inputs(seed: int=0):
    np.random.seed(seed)
    _w = jnp.asarray

    def _rec_inputs():
        import jax
        import jax.numpy as jnp
        _rk = jax.random.key(seed)
        x = -0.000125 + 0.9999 * jax.random.normal(jax.random.fold_in(_rk, 1), (4, 256, 256), jnp.float32)
        _lenS = 256 - jax.random.randint(jax.random.fold_in(_rk, 7), (4,), 0, max(1, 256 // 4) + 1, jnp.int32)
        _lenS2 = 256 - jax.random.randint(jax.random.fold_in(_rk, 8), (4,), 0, max(1, 256 // 4) + 1, jnp.int32)
        itok_BxS_13_99985 = jax.random.randint(jax.random.fold_in(_rk, 11), (4, 256), 13, 99986, jnp.int32)
        _ctx_2048P = jax.random.normal(jax.random.fold_in(_rk, 12), (4, 16, 256), jnp.float32)
        _ctx_2048c = jax.random.dirichlet(jax.random.fold_in(_rk, 512), 0.3 * jnp.ones((16,), jnp.float32), (4, 256))
        _ctx_2048t = jnp.einsum('bsk,bkd->bsd', _ctx_2048c, _ctx_2048P)
        _ctx_2048t = _ctx_2048t * jax.lax.rsqrt(jnp.mean(jnp.square(_ctx_2048t)) + 1e-12) * 0.953939
        ctx_2048 = 6.82029e-06 + 0.0200006 * (_ctx_2048t + 0.3 * jax.random.normal(jax.random.fold_in(_rk, 612), (4, 256, 256), jnp.float32))
        return (x, itok_BxS_13_99985, ctx_2048)
    x, itok_BxS_13_99985, ctx_2048 = _rec_inputs()

    def _L0_attn_setup():
        import jax, jax.numpy as jnp
        import numpy as np
        BLOCK = 32
        NUM_HEADS = 16
        HEAD_DIM = 128
        FP4_GRID = jnp.array([0.0, 0.5, 1.0, 1.5, 2.0, 3.0, 4.0, 6.0], dtype=jnp.float32)

        def quantize_to_mxfp4(w, block_size=BLOCK):
            D, F = w.shape
            blocks = w.reshape(D // block_size, block_size, F)
            amax = jnp.max(jnp.abs(blocks), axis=1)
            e = jnp.floor(jnp.log2(jnp.maximum(amax, 1e-12) / 6.0))
            scale = jnp.exp2(e)
            v = blocks / scale[:, None, :]
            idx = jnp.argmin(jnp.abs(jnp.abs(v)[..., None] - FP4_GRID), axis=-1)
            codes = jnp.sign(v) * FP4_GRID[idx]
            return (codes.reshape(D, F).astype(jnp.float32), scale.astype(jnp.float32))

        def _mxfp4_matmul(x, codes, scales, block_size=BLOCK):
            w = codes * jnp.repeat(scales, block_size, axis=0)
            return x @ w
        key = jax.random.key(seed)
        ks = jax.random.split(key, 9)
        B, S, D = (2, 256, 256)
        feat = NUM_HEADS * HEAD_DIM
        x = jax.random.normal(ks[0], (B, S, D), dtype=jnp.float32)

        def make_w(k, din, dout):
            w = jax.random.normal(k, (din, dout), dtype=jnp.float32) * (1.0 / np.sqrt(din))
            return quantize_to_mxfp4(w, BLOCK)
        wq_codes, wq_scales = make_w(ks[1], D, feat)
        wk_codes, wk_scales = make_w(ks[2], D, feat)
        wv_codes, wv_scales = make_w(ks[3], D, feat)
        wo_codes, wo_scales = make_w(ks[4], feat, D)
        bq = jnp.zeros((feat,), jnp.float32)
        bk = jnp.zeros((feat,), jnp.float32)
        bv = jnp.zeros((feat,), jnp.float32)
        bo = jnp.zeros((D,), jnp.float32)
        return {'x': x, 'wq_codes': wq_codes, 'wq_scales': wq_scales, 'bq': bq, 'wk_codes': wk_codes, 'wk_scales': wk_scales, 'bk': bk, 'wv_codes': wv_codes, 'wv_scales': wv_scales, 'bv': bv, 'wo_codes': wo_codes, 'wo_scales': wo_scales, 'bo': bo}
    _L0_attn_all = _L0_attn_setup()
    _L0_attn_in = {k: v for k, v in _L0_attn_all.items() if k in ('wq_codes', 'wq_scales', 'bq', 'wk_codes', 'wk_scales', 'bk', 'wv_codes', 'wv_scales', 'bv', 'wo_codes', 'wo_scales', 'bo')}
    del _L0_attn_all

    def _L0_xattn_setup():
        import jax, jax.numpy as jnp
        import numpy as np
        B, S, D = (4, 512, 256)
        E = 4
        F = 1024 // E
        VOCAB = 12500
        key = jax.random.key(seed)
        k1, k2, k3, k4, k5 = jax.random.split(key, 5)
        hidden_states = jax.random.normal(k1, (B, S, D), dtype=jnp.float32)
        token_ids = jax.random.randint(k2, (B, S), 0, VOCAB, dtype=jnp.int64)
        Wg = jax.random.normal(k3, (E, F, D), dtype=jnp.float32) * 0.02
        Wu = jax.random.normal(k4, (E, F, D), dtype=jnp.float32) * 0.02
        Wd = jax.random.normal(k5, (E, D, F), dtype=jnp.float32) * 0.02
        return {'hidden_states': hidden_states, 'token_ids': token_ids, 'Wg': Wg, 'Wu': Wu, 'Wd': Wd}
    _L0_xattn_all = _L0_xattn_setup()
    _L0_xattn_in = {k: v for k, v in _L0_xattn_all.items() if k in ()}
    del _L0_xattn_all

    def _L0_ffn_setup():
        import jax, jax.numpy as jnp
        import numpy as np
        E = 32
        K = 4
        H = 256
        I = 128
        RSF = 1.0
        B, S = (2, 128)

        def _mlp(x, wg, wu, wd):
            return jax.nn.silu(x @ wg) * (x @ wu) @ wd
        key = jax.random.key(seed)
        ks = jax.random.split(key, 9)
        sc = 0.02
        return {'x': jax.random.normal(ks[0], (B, S, H), jnp.float32), 'router_w': jax.random.normal(ks[1], (E, H), jnp.float32) * sc, 'bias': jnp.zeros((E,), jnp.float32), 'w_gate': jax.random.normal(ks[2], (E, H, I), jnp.float32) * sc, 'w_up': jax.random.normal(ks[3], (E, H, I), jnp.float32) * sc, 'w_down': jax.random.normal(ks[4], (E, I, H), jnp.float32) * sc, 'sw_gate': jax.random.normal(ks[5], (H, I), jnp.float32) * sc, 'sw_up': jax.random.normal(ks[6], (H, I), jnp.float32) * sc, 'sw_down': jax.random.normal(ks[7], (I, H), jnp.float32) * sc}
    _L0_ffn_all = _L0_ffn_setup()
    _L0_ffn_in = {k: v for k, v in _L0_ffn_all.items() if k in ('router_w', 'bias', 'w_gate', 'w_up', 'w_down', 'sw_gate', 'sw_up', 'sw_down')}
    del _L0_ffn_all
    return {'x': x, 'itok_BxS_13_99985': itok_BxS_13_99985, 'ctx_2048': ctx_2048, 'L0_attn_wq_codes': _L0_attn_in['wq_codes'], 'L0_attn_wq_scales': _L0_attn_in['wq_scales'], 'L0_attn_bq': _L0_attn_in['bq'], 'L0_attn_wk_codes': _L0_attn_in['wk_codes'], 'L0_attn_wk_scales': _L0_attn_in['wk_scales'], 'L0_attn_bk': _L0_attn_in['bk'], 'L0_attn_wv_codes': _L0_attn_in['wv_codes'], 'L0_attn_wv_scales': _L0_attn_in['wv_scales'], 'L0_attn_bv': _L0_attn_in['bv'], 'L0_attn_wo_codes': _L0_attn_in['wo_codes'], 'L0_attn_wo_scales': _L0_attn_in['wo_scales'], 'L0_attn_bo': _L0_attn_in['bo'], 'L0_ffn_router_w': _L0_ffn_in['router_w'], 'L0_ffn_bias': _L0_ffn_in['bias'], 'L0_ffn_w_gate': _L0_ffn_in['w_gate'], 'L0_ffn_w_up': _L0_ffn_in['w_up'], 'L0_ffn_w_down': _L0_ffn_in['w_down'], 'L0_ffn_sw_gate': _L0_ffn_in['sw_gate'], 'L0_ffn_sw_up': _L0_ffn_in['sw_up'], 'L0_ffn_sw_down': _L0_ffn_in['sw_down']}

def reference(x, itok_BxS_13_99985, ctx_2048, L0_attn_wq_codes, L0_attn_wq_scales, L0_attn_bq, L0_attn_wk_codes, L0_attn_wk_scales, L0_attn_bk, L0_attn_wv_codes, L0_attn_wv_scales, L0_attn_bv, L0_attn_wo_codes, L0_attn_wo_scales, L0_attn_bo, L0_ffn_router_w, L0_ffn_bias, L0_ffn_w_gate, L0_ffn_w_up, L0_ffn_w_down, L0_ffn_sw_gate, L0_ffn_sw_up, L0_ffn_sw_down):
    import jax
    import jax.numpy as jnp

    def _L0_attn_ref(x, wq_codes, wq_scales, bq, wk_codes, wk_scales, bk, wv_codes, wv_scales, bv, wo_codes, wo_scales, bo):
        import jax, jax.numpy as jnp
        import numpy as np
        BLOCK = 32
        NUM_HEADS = 16
        HEAD_DIM = 128
        FP4_GRID = jnp.array([0.0, 0.5, 1.0, 1.5, 2.0, 3.0, 4.0, 6.0], dtype=jnp.float32)

        def quantize_to_mxfp4(w, block_size=BLOCK):
            D, F = w.shape
            blocks = w.reshape(D // block_size, block_size, F)
            amax = jnp.max(jnp.abs(blocks), axis=1)
            e = jnp.floor(jnp.log2(jnp.maximum(amax, 1e-12) / 6.0))
            scale = jnp.exp2(e)
            v = blocks / scale[:, None, :]
            idx = jnp.argmin(jnp.abs(jnp.abs(v)[..., None] - FP4_GRID), axis=-1)
            codes = jnp.sign(v) * FP4_GRID[idx]
            return (codes.reshape(D, F).astype(jnp.float32), scale.astype(jnp.float32))

        def _mxfp4_matmul(x, codes, scales, block_size=BLOCK):
            w = codes * jnp.repeat(scales, block_size, axis=0)
            return x @ w
        B, S, D = x.shape
        q = _mxfp4_matmul(x, wq_codes, wq_scales) + bq
        k = _mxfp4_matmul(x, wk_codes, wk_scales) + bk
        v = _mxfp4_matmul(x, wv_codes, wv_scales) + bv
        q = q.reshape(B, S, NUM_HEADS, HEAD_DIM)
        k = k.reshape(B, S, NUM_HEADS, HEAD_DIM)
        v = v.reshape(B, S, NUM_HEADS, HEAD_DIM)
        scores = jnp.einsum('bqhd,bkhd->bhqk', q, k) / jnp.sqrt(jnp.float32(HEAD_DIM))
        attn = jax.nn.softmax(scores, axis=-1)
        out = jnp.einsum('bhqk,bkhd->bqhd', attn, v).reshape(B, S, NUM_HEADS * HEAD_DIM)
        return _mxfp4_matmul(out, wo_codes, wo_scales) + bo

    def _L0_xattn_ref(hidden_states, token_ids, Wg, Wu, Wd):
        import jax, jax.numpy as jnp
        import numpy as np
        B, S, D = (4, 512, 256)
        E = 4
        F = 1024 // E
        VOCAB = 12500
        tokens_per_expert = VOCAB // E
        tid = jnp.clip(token_ids, 0, VOCAB - 1)
        expert_ids = jnp.minimum(tid // tokens_per_expert, E - 1)
        out = jnp.zeros_like(hidden_states)
        for e in range(E):
            g = jax.nn.silu(jnp.einsum('bsd,fd->bsf', hidden_states, Wg[e]))
            u = jnp.einsum('bsd,fd->bsf', hidden_states, Wu[e])
            y = jnp.einsum('bsf,df->bsd', g * u, Wd[e])
            out = jnp.where((expert_ids == e)[..., None], y, out)
        return out

    def _L0_ffn_ref(x, router_w, bias, w_gate, w_up, w_down, sw_gate, sw_up, sw_down):
        import jax, jax.numpy as jnp
        import numpy as np
        E = 32
        K = 4
        H = 256
        I = 128
        RSF = 1.0
        B, S = (2, 128)

        def _mlp(x, wg, wu, wd):
            return jax.nn.silu(x @ wg) * (x @ wu) @ wd
        b, s, h = x.shape
        xs = x.reshape(-1, h)
        T = xs.shape[0]
        logits = xs @ router_w.T
        scores = jax.nn.sigmoid(logits)
        _, idx = jax.lax.top_k(scores + bias[None, :], K)
        w = jnp.take_along_axis(scores, idx, axis=1)
        w = w / (w.sum(-1, keepdims=True) + 1e-20) * RSF
        combine = jnp.zeros((T, E), scores.dtype).at[jnp.arange(T)[:, None], idx].add(w)

        def body(acc, ws):
            wg, wu, wd, c = ws
            return (acc + _mlp(xs, wg, wu, wd) * c[:, None], None)
        out, _ = jax.lax.scan(body, jnp.zeros_like(xs), (w_gate, w_up, w_down, combine.T))
        out = out + _mlp(xs, sw_gate, sw_up, sw_down)
        return out.reshape(b, s, h)
    x = x + _L0_attn_ref(_layernorm(x, axis=-1), L0_attn_wq_codes, L0_attn_wq_scales, L0_attn_bq, L0_attn_wk_codes, L0_attn_wk_scales, L0_attn_bk, L0_attn_wv_codes, L0_attn_wv_scales, L0_attn_bv, L0_attn_wo_codes, L0_attn_wo_scales, L0_attn_bo)
    x = x + _L0_xattn_ref(_layernorm(x, axis=-1), itok_BxS_13_99985, ctx_2048, ctx_2048, ctx_2048)
    x = x + _L0_ffn_ref(_layernorm(x, axis=-1), L0_ffn_router_w, L0_ffn_bias, L0_ffn_w_gate, L0_ffn_w_up, L0_ffn_w_down, L0_ffn_sw_gate, L0_ffn_sw_up, L0_ffn_sw_down)
    return x

_drawn_inputs = setup_inputs


def setup_inputs(seed=0):
    import zlib

    import numpy as np

    out = dict(_drawn_inputs(seed))
    spreads = {'L0_attn_bq': (0.0, 0.8),
     'L0_attn_bk': (0.0, 0.8),
     'L0_attn_bv': (0.0, 0.1),
     'L0_attn_bo': (0.0, 0.1),
     'L0_ffn_bias': (0.0, 0.8)}
    factors = {'L0_attn_wq_scales': 3.339,
     'L0_attn_wk_scales': 3.339,
     'L0_attn_wv_scales': 3.007,
     'L0_ffn_router_w': 8.0,
     'L0_ffn_w_gate': 8.0,
     'L0_ffn_w_up': 8.0,
     'L0_ffn_w_down': 8.0,
     'L0_ffn_sw_gate': 4.89,
     'L0_ffn_sw_up': 4.783,
     'L0_ffn_sw_down': 4.812}
    for name, (base, spread) in spreads.items():
        noise = np.random.default_rng([zlib.crc32(name.encode()), seed]).standard_normal(out[name].shape)
        drawn = base * np.exp(spread * noise) if base else spread * noise
        out[name] = jnp.asarray(drawn.astype(out[name].dtype))
    for name, factor in factors.items():
        out[name] = (out[name] * factor).astype(out[name].dtype)
    return out
```

```python
from contextlib import ExitStack

import concourse.bass as bass
from concourse import mybir

F32 = mybir.dt.float32
F32R = mybir.dt.float32r
F16 = mybir.dt.float16
BF16 = mybir.dt.bfloat16
U32 = mybir.dt.uint32
I32 = mybir.dt.int32
ALU = mybir.AluOpType
ACT = mybir.ActivationFunctionType
AX = mybir.AxisListType

P = 128
T = 1024
D = 256
NT = T // P
KT = D // P
B, S = 4, 256
H, HD = 16, 128
FEAT = H * HD
QB = 32
G = H // 2
PAIRS = 2 * B
SCALE = float(HD) ** -0.5
EPS = 1e-5
NROUTE = 4
VOCAB = 12500
HALF = 512
NH = T // HALF
NE, TOPK, FI = 32, 4, 128

SLOTS = 128
TILES = (T * TOPK + NE * (SLOTS - 1)) // SLOTS + 1
STEPS = 4
TRIPS = TILES // STEPS
assert TRIPS * STEPS == TILES == 64
CH = TOPK * NT
EW = 3 * D

Q, K, V, W = 0, 1, 2, 3
H0, VC, H1, WC = 0, 1, 2, 3


def wait(eng, sem, value):
    if isinstance(value, int) and value <= 0:
        return
    eng.wait_ge(sem, value)


def apart(eng):
    eng.nop(nofuse=True)


def slot_tiles(first, last):
    s = [[("qk", Q, 1, 0), ("qk", K, 1, 0)],
         [("v", V, 0, n) for n in range(B)],
         [("qk", Q, 1, 1), ("w", W, 0, 0)],
         [("qk", K, 1, 1), ("w", W, 0, 1)],
         [("next", Q, 0, 0), ("w", W, 0, 2)],
         [("next", K, 0, 0), ("w", W, 0, 3)],
         [("next", Q, 0, 1)],
         [("next", K, 0, 1)]]
    keep = lambda t: not (first and t[0] == "w") and not (last and t[0] == "next")
    return [[t for t in slot if keep(t)] for slot in s]


PRO_TILES = [("next", Q, 0, 0), ("next", K, 0, 0), ("next", Q, 0, 1), ("next", K, 0, 1)]


class Plan:

    def __init__(self, g):
        self.g = g
        self.first = isinstance(g, int) and g == 0
        self.last = isinstance(g, int) and g == G - 1
        self.slots = slot_tiles(self.first, self.last)
        n = 0
        self.tiles = []
        start = 4 if self.first else 16 * g
        for i, slot in enumerate(self.slots):
            for t in slot:
                self.tiles.append((i, t, start + n, n))
                n += 1
        if self.last:
            for b in range(B):
                self.tiles.append((PAIRS + 2, ("w", W, 0, b), start + n, n))
                n += 1

    def of_slot(self, i):
        return [(t, number, pos) for s, t, number, pos in self.tiles if s == i]

    def pair(self, i):
        return self.g * PAIRS + i

    def qk_count(self, t):
        kind, m, hp, half = t
        at = {(Q, 0): 0, (K, 0): 1, (Q, 1): 2, (K, 1): 3}[(m, half)] + 1
        if kind == "next":
            return self.g * 8 + 8 + at
        return self.g * 8 + 4 + at

    def v_count(self, n):
        return self.g * 4 + n + 1

    def w_done_count(self, b, final):
        return (self.g * 4 if final else (self.g - 1) * 4) + b + 2

    def freed(self, pos):
        if pos >= 2:
            t = self.tiles[pos - 2][1]
            final = self.last and self.tiles[pos - 2][0] > PAIRS
        else:
            t, final = ("prev", (Q, K)[pos], 0, 1), False
        kind, m, hp, n = t
        if kind == "prev":
            return "qk", self.g * 8 + {Q: 3, K: 4}[m]
        if kind in ("qk", "next"):
            return "qk", self.qk_count(t)
        if kind == "v":
            return "v", self.v_count(n)
        return "w", self.w_done_count(n, final)

    def w_tile_number(self, b):
        for s, t, number, pos in self.tiles:
            if t[0] == "w" and t[3] == b and s < PAIRS:
                return number

    def weights(self, chunk, ahead):
        if ahead == 0 and self.first and chunk != WC:
            return {H0: 1, VC: 2, H1: 3}[chunk]
        base = self.g * 4 + 3 if (ahead or chunk == WC) else (self.g - 1) * 4 + 3
        return base + {H0: 1, VC: 2, H1: 3, WC: 4}[chunk] - (3 if (self.last and chunk == WC and not ahead) else 0)


def over_groups(eng, body):
    body(Plan(0))
    with eng.Fori(1, G - 1) as g:
        body(Plan(g))
    body(Plan(G - 1))


def decoder_layer(nc, a, out):
    ctx = ExitStack()
    with ctx:
        def sb(name, shape, dt=F32):
            return ctx.enter_context(nc.sbuf_tensor(name, shape, dt))

        def sem(name):
            return ctx.enter_context(nc.semaphore(name))

        bank = [ctx.enter_context(nc.psum_tensor(f"bank{n}", [P, HALF], F32)) for n in range(8)]
        bS, bP, bO, bJ = bank[0:2], bank[2:4], bank[4:6], bank[6:8]

        Z_BANKS = bank[2:6]
        Y_BANKS = [bank[0], bank[1], bank[6], bank[7]]

        ident = sb("ident", [P, P])
        x_in = sb("x_in", [P, NT, D])
        h_row = sb("h_row", [P, NT, D])
        x_acc = sb("x_acc", [P, NT, D])
        bo_b = sb("bo_b", [P, D])
        b_rows = sb("b_rows", [3 * H, HD])
        b_col = sb("b_col", [P, 3 * H])
        rw_rows = sb("rw_rows", [NE, D])
        rwT = sb("rwT", [P, KT, NE])
        rb = sb("rb", [P, NE])
        sgu = sb("sgu", [P, KT, 2, FI])
        sdn = sb("sdn", [P, D])
        iota_e = sb("iota_e", [P, NE])
        iota_t = sb("iota_t", [P, TILES], F16)
        iota_s = sb("iota_s", [P, SLOTS], F16)
        iota_f = sb("iota_f", [NE, NT])
        tok_id = sb("tok_id", [P, TOPK, NT], F16)
        before = sb("before", [P, P], BF16)
        upto = sb("upto", [NE, NE], BF16)
        ones = sb("ones", [P, P], BF16)
        moe_at = nc.sbuf_base
        st_c = [sb(f"st_c{c}", [P, 4, P]) for c in range(4)]
        st_s = [sb(f"st_s{c}", [P, 4, P]) for c in range(4)]
        w_hi = [sb(f"w_hi{c}", [P, 4, P], F32R) for c in range(4)]
        w_lo = [sb(f"w_lo{c}", [P, 4, P], F32R) for c in range(4)]
        qk_hi = sb("qk_hi", [P, 2, 2, T], F32R)
        qk_lo = sb("qk_lo", [P, 2, 2, T], F32R)
        v_hi = sb("v_hi", [P, NT, 2, HD], F32R)
        v_lo = sb("v_lo", [P, NT, 2, HD], F32R)
        oT_hi = sb("oT_hi", [P, 2, T], F32R)
        oT_lo = sb("oT_lo", [P, 2, T], F32R)
        moe_w = nc.alloc_sbuf_tensor_at("moe_w", [P, NE, EW], F32, offset=moe_at)
        assert nc.sbuf_base >= moe_at + NE * EW * 4
        prob = sb("prob", [P, 2, 2, S])
        pT_hi = sb("pT_hi", [P, 2, 2, S], F32R)
        pT_lo = sb("pT_lo", [P, 2, 2, S], F32R)
        rmax = sb("rmax", [P, 2, 2])
        nmax = sb("nmax", [P, 2, 2])
        rsum = sb("rsum", [P, 2, 2])
        rinv = sb("rinv", [P, 2, 2])
        bn = sb("bn", [P, NT, 6])
        mv = sb("mv", [P, NT, 2])
        var = sb("var", [P, NT])
        sd = sb("sd", [P, NT])
        rstd = sb("rstd", [P, NT])
        nt1 = sb("nt1", [P, NT])
        ids = sb("ids", [P, T], I32)
        cw = sb("cw", [P, NROUTE, KT, D])
        hT_f = cw[:, :, :, :].rearrange("p (k a) t d -> p k (a t d)", k=KT)
        arena_at = nc.sbuf_base
        hT_hi = sb("hT_hi", [P, KT, T], F32R)
        hT_lo = sb("hT_lo", [P, KT, T], F32R)
        cT_hi = sb("cT_hi", [P, NROUTE, KT, D], F32R)
        cT_lo = sb("cT_lo", [P, NROUTE, KT, D], F32R)
        mask = sb("mask", [P, NROUTE, T])
        arena_end = nc.sbuf_base
        cursor = [arena_at]

        def later(name, shape, dt=F32):
            n = {F32: 4, I32: 4, U32: 4, F16: 2, BF16: 2}[dt]
            for m in shape[1:]:
                n *= m
            t = nc.alloc_sbuf_tensor_at(name, shape, dt, offset=cursor[0])
            cursor[0] += -(-n // 32) * 32
            assert cursor[0] <= arena_end
            return t

        score = later("score", [P, NT, NE])
        sel = later("sel", [P, NT, NE])
        top = later("top", [P, NT, 8])
        topi = later("topi", [P, NT, 8], U32)
        chosen = later("chosen", [P, TOPK, NT])
        hot = later("hot", [P, TOPK, NT, NE])
        work = later("work", [P, TOPK, NT, NE])
        member = later("member", [P, NT, NE], BF16)
        count = later("count", [NE, 1])
        over = later("over", [NE, NT])
        tiles_e = later("tiles_e", [NE, 1])
        tiles_b = later("tiles_b", [NE, P], BF16)
        end_e = later("end_e", [NE, 1])
        past = later("past", [NE, TILES], BF16)
        expert = later("expert", [1, TILES], I32)
        base = later("base", [P, NE])
        place = later("place", [P, NT, NE])
        slot_f = later("slot_f", [P, TOPK, NT])
        slot_i = later("slot_i", [P, TOPK, NT], I32)
        part_i = later("part_i", [P, 2, CH], I32)
        part_h = later("part_h", [P, 2, CH], F16)
        in_tile = later("in_tile", [P, CH, TILES], F16)
        in_slot = later("in_slot", [P, CH, SLOTS], F16)
        gain = later("gain", [P, TOPK, NT])
        gsum = later("gsum", [P, NT])
        source = later("source", [P, TILES], I32)
        src4 = later("src4", [P, STEPS], I32)
        xg = later("xg", [P, STEPS, D])
        xT = later("xT", [P, 2, D])
        sg = later("sg", [P, 2, FI])
        hid = later("hid", [P, 2, FI])
        hidT = later("hidT", [P, 2, SLOTS])
        ysb = later("ysb", [P, STEPS, D])
        slot8 = later("slot8", [P, NT], I32)
        yg = later("yg", [P, NT, D])
        gact = x_in[:, 0:4, :].rearrange("p (a t) d -> p a (t d)", a=2)
        gm = prob[:, :, :, :].rearrange("p a q k -> p a (q k)")
        gu_hi = pT_hi[:, :, :, :].rearrange("p a q k -> p a (q k)")
        gu_lo = pT_lo[:, :, :, :].rearrange("p a q k -> p a (q k)")
        zeros = sb("zeros", [1, HALF])

        d_x, d_b, d_bo, d_ids, d_cw = sem("d_x"), sem("d_b"), sem("d_bo"), sem("d_ids"), sem("d_cw")
        d_w = [sem(f"d_w{c}") for c in range(4)]
        d_out = sem("d_out")
        p_const = sem("p_const")
        p_mask = sem("p_mask")
        p_wm = sem("p_wm")
        a_wh = sem("a_wh")
        p_wl = sem("p_wl")
        v_ln = sem("v_ln")
        a_sd = sem("a_sd")
        t_ln, a_ln, v_lnlo = sem("t_ln"), sem("a_ln"), sem("v_lnlo")
        t_b, v_b = sem("t_b"), sem("v_b")
        t_sc = sem("t_sc")
        v_m1, v_max = sem("v_m1"), sem("v_max")
        a_exp = sem("a_exp")
        v_ri, v_p = sem("v_ri"), sem("v_p")
        t_pT, a_pT, v_pT = sem("t_pT"), sem("a_pT"), sem("v_pT")
        t_o, a_o, v_o = sem("t_o"), sem("a_o"), sem("v_o")
        t_j = sem("t_j")
        a_qk, v_qk = sem("a_qk"), sem("v_qk")
        a_v, v_v = sem("a_v"), sem("v_v")
        v_w = sem("v_w")
        t_c, a_c, v_c = sem("t_c"), sem("a_c"), sem("v_c")
        t_z, a_z = sem("t_z"), sem("a_z")
        v_t, v_tm, a_g, v_g = sem("v_t"), sem("v_tm"), sem("a_g"), sem("v_g")
        t_y, v_y = sem("t_y"), sem("v_y")
        d_r, d_sw, d_h = sem("d_r"), sem("d_sw"), sem("d_h")
        d_m = sem("d_m")
        t_rw, v_rw = sem("t_rw"), sem("v_rw")
        a_hf, v_hf = sem("a_hf"), sem("v_hf")
        t_r, a_r, v_r = sem("t_r"), sem("a_r"), sem("v_r")
        t_gu, a_s, v_h = sem("t_gu"), sem("a_s"), sem("v_h")
        t_hT, a_hT, t_dn = sem("t_hT"), sem("a_hT"), sem("t_dn")
        v_sh, a_y = sem("v_sh"), sem("a_y")
        t_x, v_x = sem("t_x"), sem("v_x")
        d_g = [sem(f"d_g{u}") for u in range(STEPS)]
        d_y = [sem(f"d_y{u}") for u in range(STEPS)]
        d_yg = [sem(f"d_yg{t}") for t in range(NT)]
        v_own = sem("v_own")
        p_src, p_sl, v_cmb = sem("p_src"), sem("p_sl"), sem("v_cmb")

        bX, bG, bH, bY = bank[0:2], bank[2:4], bank[4:6], bank[6:8]
        SH = NT

        h_dram = nc.dram_tensor("h_dram", (T, D), F32, kind="Internal").ap()
        y_dram = nc.dram_tensor("y_dram", (TILES * SLOTS, D), F32, kind="Internal").ap()
        x_rows = a["x"].rearrange("b s d -> (b s) d").rearrange("(t p) d -> p t d", p=P)
        out_rows = out.rearrange("b s d -> (b s) d").rearrange("(t p) d -> p t d", p=P)
        codes = [a[f"w{n}_codes"].rearrange("(t p) n -> p t n", p=P) for n in "qkv"]
        scales = [a[f"w{n}_scales"] for n in "qkv"]
        wo_codes = a["wo_codes"].rearrange("(h p) n -> p h n", p=P)

        def load_chunk(eng, c, g):
            def spread(rows):
                return rows.unsqueeze(1).to_broadcast([rows.shape[0], QB, rows.shape[1]])
            if c in (H0, H1):
                col = g * (2 * HD) + (0 if c == H0 else HD)
                for j, m in enumerate((Q, K)):
                    eng.dma_start(st_c[c][:, KT * j:KT * j + KT, :], codes[m][:, :, bass.ds(col, HD)]).then_inc(d_w[c], 16)
                    for kt in range(KT):
                        eng.dma_start(st_s[c][:, KT * j + kt, :],
                                      spread(scales[m][kt * 4:kt * 4 + 4, bass.ds(col, HD)])).then_inc(d_w[c], 16)
            elif c == VC:
                col = g * (2 * HD)
                dst_c = st_c[c][:, :, :].rearrange("p (t n) e -> p t (n e)", t=KT)
                dst_s = st_s[c][:, :, :].rearrange("p (t n) e -> p t (n e)", t=KT)
                eng.dma_start(dst_c, codes[V][:, :, bass.ds(col, 2 * HD)]).then_inc(d_w[c], 16)
                for kt in range(KT):
                    eng.dma_start(dst_s[:, kt, :],
                                  spread(scales[V][kt * 4:kt * 4 + 4, bass.ds(col, 2 * HD)])).then_inc(d_w[c], 16)
            else:
                dst_c = st_c[c][:, :, :].rearrange("p (h n) e -> p h (n e)", h=2)
                dst_s = st_s[c][:, :, :].rearrange("p (h n) e -> p h (n e)", h=2)
                eng.dma_start(dst_c, wo_codes[:, bass.ds(g * 2, 2), :]).then_inc(d_w[c], 16)
                for hp in range(2):
                    eng.dma_start(dst_s[:, hp, :],
                                  spread(a["wo_scales"][bass.ds(g * 8 + hp * 4, 4), :])).then_inc(d_w[c], 16)

        DMAS = {H0: 6, VC: 3, H1: 6, WC: 3}

        LN_STEPS = 2 * NT + 1 + 5 + NT
        R_MEMBER, R_TILES, R_PAST, R_EXPERT, R_HOT, R_SOURCE = 1, 2, 3, 4, 5, 6

        block = ctx.enter_context(nc.Block())

        @block.sync
        def _(sp):
            sp.dma_start(x_in[:, :, :], x_rows).then_inc(d_x, 16)
            for c in (H0, VC, H1):
                load_chunk(sp, c, 0)
            load_chunk(sp, WC, 0)
            for c, n in ((H0, 1), (VC, 2), (H1, 3)):
                sp.wait_ge(p_wl, n)
                load_chunk(sp, c, 1)

            def reload(g, chunks):
                for c in chunks:
                    sp.wait_ge(p_wl, g * 4 + 3 + {H0: 1, VC: 2, H1: 3, WC: 4}[c])
                    load_chunk(sp, c, g + (1 if c == WC else 2))

            reload(0, (H0, VC, H1, WC))
            with sp.Fori(1, G - 2) as g:
                reload(g, (H0, VC, H1, WC))
            reload(G - 2, (WC,))
            sp.wait_ge(v_w, 4 * G + 1)
            EB = NE // 4
            for q in range(4):
                es = slice(q * EB, (q + 1) * EB)
                gate = a["w_gate"][es, :, :].rearrange("e (t p) i -> p e t i", p=P)
                up = a["w_up"][es, :, :].rearrange("e (t p) i -> p e t i", p=P)
                down = a["w_down"][es, :, :].rearrange("e p d -> p e d")
                gu = moe_w[:, es, 0:2 * D].rearrange("p e (t m) -> p e t m", t=KT)
                for t in range(KT):
                    sp.dma_start(gu[:, :, t, 0:FI], gate[:, :, t, :]).then_inc(d_m, 16)
                    sp.dma_start(gu[:, :, t, FI:2 * FI], up[:, :, t, :]).then_inc(d_m, 16)
                sp.dma_start(moe_w[:, es, 2 * D:EW], down).then_inc(d_m, 16)
            sp.wait_ge(v_ln, 3 * LN_STEPS)
            sp.dma_start(h_dram.rearrange("(t p) d -> p t d", p=P), h_row[:, :, :]).then_inc(d_h, 16)

            for u in range(STEPS):
                sp.sem_inc(d_y[u], 16)
            def store(it):
                for u in range(STEPS):
                    sp.wait_ge(a_y, it * STEPS + u + 1)
                    sp.dma_start(y_dram[bass.ds((it * STEPS + u) * SLOTS, SLOTS), :], ysb[:, u, :]).then_inc(d_y[u], 16)

            with sp.Fori(0, TRIPS) as it:
                store(it)
            for t in range(0, NT, 2):
                sp.wait_ge(v_cmb, (TOPK - 1) * NT + t + 2)
                sp.dma_start(out_rows[:, t:t + 2, :], x_acc[:, t:t + 2, :]).then_inc(d_out, 16)
            sp.wait_ge(d_out, 16 * (NT // 2))

        @block.gpsimd
        def _(pool):
            def prep(c, wm, load_count, free=None):
                wait(pool, d_w[c], load_count)
                pool.tensor_tensor(st_c[c][:, :, :], st_c[c][:, :, :], st_s[c][:, :, :], ALU.mult).then_inc(p_wm, 1)
                wait(pool, p_wm, wm)
                wait(pool, a_wh, wm)
                pool.tensor_tensor(w_lo[c][:, :, :], st_c[c][:, :, :], w_hi[c][:, :, :], ALU.subtract).then_inc(p_wl, 1)

            pool.memset(ident[:, :], 0.0).then_inc(p_const, 1)
            pool.memset(zeros[:, :], 0.0).then_inc(p_const, 1)
            pool.wait_ge(p_const, 2)
            pool.affine_select(out=ident[:, :], in_=ident[:, :], compare_op=ALU.not_equal, fill=1.0,
                               base=0, pattern=[[-1, P]], channel_multiplier=1).then_inc(p_const, 1)
            for n, c in enumerate((H0, VC, H1)):
                prep(c, n + 1, 16 * DMAS[c])
            pool.wait_ge(d_x, 16)
            pool.wait_ge(d_bo, 16)
            pool.tensor_tensor(x_acc[:, :, :], x_in[:, :, :],
                               bo_b[:, :].unsqueeze(1).to_broadcast([P, NT, D]), ALU.add).then_inc(v_w, 1)
            pool.wait_ge(d_ids, 16)
            per = VOCAB // NROUTE
            for e in range(NROUTE):
                pool.tensor_scalar(mask[:, e, :], ids[:, :], float(per * e) if e else float(per), None,
                                   ALU.is_ge if e else ALU.is_lt).then_inc(p_mask, 1)
            pool.wait_ge(p_mask, NROUTE)
            for e in range(1, NROUTE - 1):
                pool.tensor_tensor(mask[:, e, :], mask[:, e, :], mask[:, e + 1, :], ALU.subtract).then_inc(p_mask, 1)

            pool.iota(iota_e[:, :], pattern=[[1, NE]], base=0, channel_multiplier=0,
                      allow_small_or_imprecise_dtypes=True).then_inc(p_const, 1)
            pool.iota(iota_t[:, :], pattern=[[1, TILES]], base=0, channel_multiplier=0,
                      allow_small_or_imprecise_dtypes=True).then_inc(p_const, 1)
            pool.iota(iota_s[:, :], pattern=[[1, SLOTS]], base=0, channel_multiplier=0,
                      allow_small_or_imprecise_dtypes=True).then_inc(p_const, 1)
            pool.iota(iota_f[:, :], pattern=[[SLOTS, NT]], base=0, channel_multiplier=0,
                      allow_small_or_imprecise_dtypes=True).then_inc(p_const, 1)
            pool.iota(tok_id[:, :, :], pattern=[[0, TOPK], [P, NT]], base=0, channel_multiplier=1,
                      allow_small_or_imprecise_dtypes=True).then_inc(p_const, 1)
            pool.memset(ones[:, :], 1.0).then_inc(p_const, 1)
            pool.wait_ge(p_const, 9)
            pool.affine_select(out=before[:, :], in_=ones[:, :], compare_op=ALU.is_gt, fill=0.0,
                               base=0, pattern=[[1, P]], channel_multiplier=-1).then_inc(p_const, 1)
            pool.affine_select(out=upto[:, :], in_=ones[0:NE, 0:NE], compare_op=ALU.is_ge, fill=0.0,
                               base=0, pattern=[[1, NE]], channel_multiplier=-1).then_inc(p_const, 1)

            def body(pl):
                g = pl.g
                for c in ((WC,) if pl.last else (H0, VC, H1, WC)):
                    ahead = 0 if c == WC else 1
                    prep(c, pl.weights(c, ahead), (g + ahead) * (16 * DMAS[c]) + 16 * DMAS[c])

            over_groups(pool, body)

            pool.wait_ge(d_h, 16)
            pool.wait_ge(v_r, R_SOURCE)

            def gathers(it, first):
                for u in range(STEPS):
                    wait(pool, t_x, 0 if first else (it - 1) * STEPS + u + 1)
                    pool.tensor_copy(src4[:, u:u + 1], source[:, bass.ds(it * STEPS + u, 1)]).then_inc(p_src, 1)
                    wait(pool, p_src, it * STEPS + u + 1)
                    apart(pool)
                    pool.indirect_dma_start(out=xg[:, u, :], out_offset=None, in_=h_dram,
                                            in_offset=bass.IndirectOffsetOnAxis(ap=src4[:, u:u + 1], axis=0)).then_inc(d_g[u], 16)

            gathers(0, True)
            with pool.Fori(1, TRIPS) as it:
                gathers(it, False)

            for u in range(STEPS):
                pool.wait_ge(d_y[u], 16 * TRIPS + 16)

            flat_slot = slot_i[:, :, :].rearrange("p k t -> p (k t)")

            def results(k, first):
                for t in range(NT):
                    wait(pool, v_cmb, 0 if first else (k - 1) * NT + t + 1)
                    pool.tensor_copy(slot8[:, t:t + 1], flat_slot[:, bass.ds(k * NT + t, 1)]).then_inc(p_sl, 1)
                    wait(pool, p_sl, k * NT + t + 1)
                    apart(pool)
                    pool.indirect_dma_start(out=yg[:, t, :], out_offset=None, in_=y_dram,
                                            in_offset=bass.IndirectOffsetOnAxis(ap=slot8[:, t:t + 1], axis=0)).then_inc(d_yg[t], 16)

            results(0, True)
            with pool.Fori(1, TOPK) as k:
                results(k, False)


        def ln_vector(dve, n, src):
            base = n * LN_STEPS
            for t in range(NT):
                dve.bn_stats(bn[:, t, :], src[:, t, :]).then_inc(v_ln, 1)
            for t in range(NT):
                dve.wait_ge(v_ln, base + t + 1)
                dve.bn_aggr(mv[:, t, :], bn[:, t, :]).then_inc(v_ln, 1)
            dve.wait_ge(v_ln, base + 2 * NT)
            dve.tensor_scalar(var[:, :], mv[:, :, 1], EPS, None, ALU.add).then_inc(v_ln, 1)
            dve.wait_ge(a_sd, n + 1)
            k = base + 2 * NT + 1
            dve.reciprocal(rstd[:, :], sd[:, :]).then_inc(v_ln, 1)
            dve.wait_ge(v_ln, k + 1)
            dve.tensor_tensor(nt1[:, :], rstd[:, :], rstd[:, :], ALU.mult).then_inc(v_ln, 1)
            dve.wait_ge(v_ln, k + 2)
            dve.tensor_tensor(nt1[:, :], nt1[:, :], var[:, :], ALU.mult).then_inc(v_ln, 1)
            dve.wait_ge(v_ln, k + 3)
            dve.tensor_scalar(nt1[:, :], nt1[:, :], -0.5, 1.5, ALU.mult, ALU.add).then_inc(v_ln, 1)
            dve.wait_ge(v_ln, k + 4)
            dve.tensor_tensor(rstd[:, :], rstd[:, :], nt1[:, :], ALU.mult).then_inc(v_ln, 1)
            dve.wait_ge(v_ln, k + 5)
            for t in range(NT):
                dve.tensor_scalar(h_row[:, t, :], src[:, t, :], mv[:, t, 0:1], rstd[:, t:t + 1],
                                  ALU.subtract, ALU.mult).then_inc(v_ln, 1)

        def ln_scalar(act, n):
            act.wait_ge(v_ln, n * LN_STEPS + 2 * NT + 1)
            act.activation(sd[:, :], var[:, :], ACT.Sqrt).then_inc(a_sd, 1)

        LN_BANKS = [bank[2], bank[3], bank[4], bank[5]]

        def ln_tensor(pe, n):
            for half in range(NH):
                for kt in range(KT):
                    b = LN_BANKS[half * KT + kt]
                    for j in range(4):
                        t = half * 4 + j
                        pe.wait_ge(v_ln, n * LN_STEPS + LN_STEPS - NT + t + 1)
                        mm = pe.transpose(b[:, j * P:j * P + P], h_row[:, t, kt * P:kt * P + P], ident[:, :])
                    mm.then_inc(t_ln, 1)

        def ln_high(act, n):
            for i in range(4):
                act.wait_ge(t_ln, 4 * n + i + 1)
                half, kt = i // KT, i % KT
                act.copy(hT_hi[:, kt, half * HALF:(half + 1) * HALF], LN_BANKS[i][:, :]).then_inc(a_ln, 1)

        def ln_low(dve, n):
            for i in range(4):
                dve.wait_ge(a_ln, 4 * n + i + 1)
                half, kt = i // KT, i % KT
                sl = slice(half * HALF, (half + 1) * HALF)
                dve.tensor_tensor(hT_lo[:, kt, sl], LN_BANKS[i][:, :], hT_hi[:, kt, sl], ALU.subtract).then_inc(v_lnlo, 1)

        @block.tensor
        def _(pe):
            def mm3(o, l_hi, l_lo, r_hi, r_lo, start, stop, share=False):
                pe.matmul(o, l_lo, r_hi, start=start, stop=False, skip_group_check=share)
                pe.matmul(o, l_hi, r_lo, start=False, stop=False, skip_group_check=share)
                return pe.matmul(o, l_hi, r_hi, start=False, stop=stop, skip_group_check=share)

            pe.wait_ge(p_const, 3)
            pe.wait_ge(d_b, 16 * 3)
            pe.transpose(bJ[0][:, 0:3 * H], b_rows[:, :], ident[0:3 * H, 0:3 * H]).then_inc(t_b, 1)
            pe.wait_ge(d_r, 32)
            for kt in range(KT):
                mm = pe.transpose(bJ[1][:, kt * NE:(kt + 1) * NE], rw_rows[:, kt * P:(kt + 1) * P], ident[0:NE, 0:NE])
            mm.then_inc(t_rw, 1)
            ln_tensor(pe, 0)
            pe.wait_ge(v_b, 1)
            pe.wait_ge(v_rw, 1)

            def proj_tile(pl, tile, number, pos, final=False):
                kind, m, hp, n = tile
                o = bJ[pos % 2]
                if pl is not None:
                    which, value = pl.freed(pos)
                    wait(pe, {"qk": v_qk, "v": v_v, "w": v_w}[which], value)
                elif pos >= 2:
                    wait(pe, v_qk, pos - 1)
                if kind in ("qk", "next"):
                    c = H0 if kind == "next" else H1
                    if n == 0 and m == Q:
                        wait(pe, p_wl, 1 if pl is None else pl.weights(c, 1 if kind == "next" else 0))
                    for kt in range(KT):
                        j = KT * m + kt
                        mm = mm3(o[:, :], w_hi[c][:, j, :], w_lo[c][:, j, :],
                                 hT_hi[:, kt, n * HALF:(n + 1) * HALF], hT_lo[:, kt, n * HALF:(n + 1) * HALF],
                                 kt == 0, kt == KT - 1)
                elif kind == "v":
                    if n == 0:
                        wait(pe, p_wl, pl.weights(VC, 0))
                    for i in range(2):
                        t = 2 * n + i
                        for kt in range(KT):
                            mm = mm3(o[:, i * D:(i + 1) * D], hT_hi[:, kt, t * P:(t + 1) * P], hT_lo[:, kt, t * P:(t + 1) * P],
                                     w_hi[VC][:, KT * kt:KT * kt + 2, :].rearrange("p a b -> p (a b)"),
                                     w_lo[VC][:, KT * kt:KT * kt + 2, :].rearrange("p a b -> p (a b)"),
                                     kt == 0, kt == KT - 1)
                else:
                    if n == 0:
                        wait(pe, p_wl, pl.weights(WC, 0) if final else (pl.g - 1) * 4 + 3 + 4)
                        wait(pe, v_o, pl.pair(PAIRS) if final else pl.pair(0))
                    for i in range(2):
                        t = 2 * n + i
                        for hh in range(2):
                            mm = mm3(o[:, i * D:(i + 1) * D], oT_hi[:, hh, t * P:(t + 1) * P], oT_lo[:, hh, t * P:(t + 1) * P],
                                     w_hi[WC][:, 2 * hh:2 * hh + 2, :].rearrange("p a b -> p (a b)"),
                                     w_lo[WC][:, 2 * hh:2 * hh + 2, :].rearrange("p a b -> p (a b)"),
                                     hh == 0, hh == 1)
                mm.then_inc(t_j, 1)

            def scores(pl, i):
                p = pl.pair(i)
                wait(pe, a_exp, p - 1 if not (pl.first and i < 2) else 0)
                hp, b = i // B, i % B
                if b in (0, 2):
                    wait(pe, v_qk, pl.g * 8 + 4 * hp + (2 if b == 0 else 4))
                for qt in range(2):
                    qs = slice(b * S + qt * P, b * S + qt * P + P)
                    ks = slice(b * S, b * S + S)
                    mm = mm3(bS[i % 2][:, qt * S:(qt + 1) * S], qk_hi[:, hp, Q, qs], qk_lo[:, hp, Q, qs],
                             qk_hi[:, hp, K, ks], qk_lo[:, hp, K, ks], True, True)
                mm.then_inc(t_sc, 1)

            def turn(pl, i):
                p = pl.pair(i)
                wait(pe, v_p, p + 1)
                wait(pe, v_pT, p - 1 if not (pl.first and i < 2) else 0)
                for kt in range(2):
                    for qt in range(2):
                        mm = pe.transpose(bP[i % 2][:, kt * S + qt * P:kt * S + qt * P + P],
                                          prob[:, i % 2, qt, kt * P:kt * P + P], ident[:, :])
                mm.then_inc(t_pT, 1)

            def attend(pl, i):
                p = pl.pair(i)
                wait(pe, v_pT, p + 1)
                wait(pe, v_o, p - 1 if not (pl.first and i < 2) else 0)
                if i == 0:
                    wait(pe, v_v, pl.g * 4 + 4)
                hp, b = (i % PAIRS) // B, i % B
                for kt in range(2):
                    mm = mm3(bO[i % 2][:, 0:S], v_hi[:, 2 * b + kt, hp, :], v_lo[:, 2 * b + kt, hp, :],
                             pT_hi[:, i % 2, kt, :], pT_lo[:, i % 2, kt, :], kt == 0, kt == 1)
                mm.then_inc(t_o, 1)

            pe.wait_ge(v_lnlo, 4)
            for pos, t in enumerate(PRO_TILES):
                proj_tile(None, t, pos, pos)

            def body(pl):
                for i in range(PAIRS + (2 if pl.last else 0)):
                    if i < PAIRS:
                        scores(pl, i)
                    if not (pl.first and i < 1) and i < PAIRS + 1:
                        turn(pl, i - 1)
                    if not (pl.first and i < 2):
                        attend(pl, i - 2)
                    for t, number, pos in pl.of_slot(i):
                        proj_tile(pl, t, number, pos)
                if pl.last:
                    for t, number, pos in pl.of_slot(PAIRS + 2):
                        proj_tile(pl, t, number, pos, final=True)

            over_groups(pe, body)

            pe.wait_ge(d_cw, 16)
            for e in range(NROUTE):
                if e == 2:
                    pe.wait_ge(v_v, 4 * G)
                for kt in range(KT):
                    for ft in range(KT):
                        mm = pe.transpose(bank[e][:, kt * D + ft * P:kt * D + ft * P + P],
                                          cw[:, e, ft, kt * P:kt * P + P], ident[:, :])
                mm.then_inc(t_c, 1)
            pe.wait_ge(v_c, NROUTE)
            ln_tensor(pe, 1)
            pe.wait_ge(v_lnlo, 8)

            for yb in Y_BANKS:
                pe.matmul(yb[:, :], zeros[0:1, 0:P], zeros[0:1, :], start=True, stop=True)

            def pre(e, s):
                half, ft = s // KT, s % KT
                wait(pe, v_t, e * 4 + s - 3 if not (isinstance(e, int) and e == 0) else 0)
                for kt in range(KT):
                    mm = mm3(Z_BANKS[s][:, :], cT_hi[:, e, kt, ft * P:ft * P + P], cT_lo[:, e, kt, ft * P:ft * P + P],
                             hT_hi[:, kt, half * HALF:(half + 1) * HALF], hT_lo[:, kt, half * HALF:(half + 1) * HALF],
                             kt == 0, kt == KT - 1)
                mm.then_inc(t_z, 1)

            def post(e, s):
                half, ft = s // KT, s % KT
                wait(pe, v_g, e * 4 + s + 1)
                for j in range(4):
                    yb = Y_BANKS[half * 2 + j // 2][:, (j % 2) * D:(j % 2) * D + D]
                    mm = mm3(yb, gu_hi[:, s % 2, j * P:(j + 1) * P], gu_lo[:, s % 2, j * P:(j + 1) * P],
                             cT_hi[:, e, ft, :], cT_lo[:, e, ft, :], False, e == NROUTE - 1 and ft == KT - 1, True)
                mm.then_inc(t_y, 1)

            for e in range(NROUTE):
                for s in range(4):
                    pre(e, s)
                    if (e, s) >= (0, 2):
                        post(e if s >= 2 else e - 1, (s - 2) % 4)
            for s in (2, 3):
                post(NROUTE - 1, s)

            ln_tensor(pe, 2)
            pe.wait_ge(a_hf, 2)
            pe.wait_ge(v_hf, 2)
            for t in range(NT):
                for kt in range(KT):
                    mm = pe.matmul(bank[6][:, t * NE:(t + 1) * NE], hT_f[:, kt, t * P:(t + 1) * P], rwT[:, kt, :],
                                   start=kt == 0, stop=kt == KT - 1)
            mm.then_inc(t_r, 1)

            def gate_up(n, e, xT_of):
                for kt in range(KT):
                    w = sgu[:, kt, :, :].rearrange("p a i -> p (a i)") if e is None else \
                        moe_w[:, :, :].rearrange("p e m -> p (e m)")[:, bass.ds(e * EW + kt * 2 * FI, 2 * FI)]
                    mm = pe.matmul(bG[n % 2][:, 0:2 * FI], xT_of(kt), w, start=kt == 0, stop=kt == KT - 1)
                mm.then_inc(t_gu, 1)

            def hidden_turn(n):
                pe.transpose(bH[n % 2][:, 0:SLOTS], hid[:, n % 2, :], ident[:, :]).then_inc(t_hT, 1)

            def down(n, e):
                w = sdn[:, :] if e is None else \
                    moe_w[:, :, :].rearrange("p e m -> p (e m)")[:, bass.ds(e * EW + 2 * D, D)]
                pe.matmul(bY[n % 2][:, 0:D], hidT[:, n % 2, :], w, start=True, stop=True).then_inc(t_dn, 1)

            pe.wait_ge(v_r, R_MEMBER)
            pe.wait_ge(p_const, 11)
            rank = bank[0]
            pe.matmul(rank[:, 0:NT * NE], before[:, :], member[:, :, :].rearrange("p t e -> p (t e)"),
                      start=True, stop=False, skip_group_check=True)
            for t in range(NT - 1):
                pe.matmul(rank[:, (t + 1) * NE:NT * NE].rearrange("p (t e) -> p t e", e=NE), ones[:, :],
                          member[:, t:t + 1, :].to_broadcast([P, NT - 1 - t, NE]),
                          start=False, stop=t == NT - 2, skip_group_check=True)
            for t in range(NT):
                mm = pe.matmul(bank[1][0:NE, 0:1], member[:, t, :], ones[:, 0:1], start=t == 0, stop=t == NT - 1)
            mm.then_inc(t_r, 1)
            pe.wait_ge(v_r, R_TILES)
            pe.matmul(bank[6][0:NE, 0:1], upto[:, :], tiles_b[:, 0:1], start=True, stop=True)
            pe.matmul(bank[7][:, 0:NE], tiles_b[:, :], before[0:NE, 0:NE], start=True, stop=True).then_inc(t_r, 1)
            pe.wait_ge(v_r, R_PAST)
            pe.matmul(bank[1][0:1, 0:TILES], ones[0:NE, 0:1], past[:, :], start=True, stop=True).then_inc(t_r, 1)

            for n in range(SH + 2):
                if n < SH:
                    if n == 0:
                        pe.wait_ge(d_sw, 48)
                    wait(pe, v_h, n - 1)
                    gate_up(n, None, lambda kt: hT_f[:, kt, n * P:(n + 1) * P])
                if 1 <= n <= SH:
                    pe.wait_ge(v_h, n)
                    wait(pe, a_hT, n - 2)
                    hidden_turn(n - 1)
                if n >= 2:
                    pe.wait_ge(a_hT, n - 1)
                    if n == 2:
                        pe.wait_ge(v_r, R_EXPERT)
                    wait(pe, v_sh, n - 3)
                    down(n - 2, None)

            pe.wait_ge(v_r, R_HOT)
            for c in range(CH):
                mm = pe.matmul(bank[0][:, 0:TILES], in_slot[:, c, :], in_tile[:, c, :], start=c == 0, stop=c == CH - 1)
            mm.then_inc(t_r, 1)

            def expert_of(j):
                apart(pe)
                return pe.value_load(expert[0:1, bass.ds(j, 1)], min_val=0, max_val=NE - 1)

            def row_turn(j, u, it):
                wait(pe, d_g[u], it * 16 + 16)
                wait(pe, v_x, j - 1)
                for kt in range(KT):
                    mm = pe.transpose(bX[u % 2][:, kt * SLOTS:(kt + 1) * SLOTS], xg[:, u, kt * P:(kt + 1) * P], ident[:, :])
                mm.then_inc(t_x, 1)

            def trip(it, first, last):
                for u in range(STEPS + (2 if last else 0)):
                    j = it * STEPS + u
                    if u < STEPS - 1:
                        row_turn(j + 1, u + 1, it)
                    elif u == STEPS - 1 and not last:
                        row_turn(j + 1, 0, it + 1)
                    if u < STEPS:
                        wait(pe, v_x, j + 1)
                        wait(pe, v_h, j - 1 + SH)
                        e = expert_of(j)
                        gate_up(u, e, lambda kt: xT[:, u % 2, kt * SLOTS:(kt + 1) * SLOTS])
                    if not (first and u < 1) and u < STEPS + 1:
                        wait(pe, v_h, j + SH)
                        wait(pe, a_hT, j - 2 + SH)
                        hidden_turn(u - 1 + STEPS)
                    if not (first and u < 2):
                        wait(pe, a_hT, j - 1 + SH)
                        wait(pe, a_y, 0 if first and u < 4 else j - 3)
                        down(u - 2 + STEPS, expert_of(j - 2))

            pe.wait_ge(v_r, R_SOURCE)
            pe.wait_ge(v_sh, SH)
            pe.wait_ge(d_m, 16 * 20)
            row_turn(0, 0, 0)
            trip(0, True, False)
            with pe.Fori(1, TRIPS - 1) as it:
                trip(it, False, False)
            trip(TRIPS - 1, False, True)

        @block.scalar
        def _(act):
            for n, nm in enumerate(("bq", "bk", "bv")):
                act.dma_start(b_rows[n * H:(n + 1) * H, :], a[nm].rearrange("(h d) -> h d", d=HD)).then_inc(d_b, 16)
            act.dma_start(bo_b[:, :], a["bo"].unsqueeze(0).to_broadcast([P, D])).then_inc(d_bo, 16)
            act.dma_start(ids[:, :], a["tok"].rearrange("b s -> (b s)").unsqueeze(0).to_broadcast([P, T])).then_inc(d_ids, 16)
            act.dma_start(rw_rows[:, :], a["router_w"]).then_inc(d_r, 16)
            act.dma_start(rb[:, :], a["bias"].unsqueeze(0).to_broadcast([P, NE])).then_inc(d_r, 16)
            act.dma_start(sgu[:, :, 0, :], a["sw_gate"].rearrange("(t p) i -> p t i", p=P)).then_inc(d_sw, 16)
            act.dma_start(sgu[:, :, 1, :], a["sw_up"].rearrange("(t p) i -> p t i", p=P)).then_inc(d_sw, 16)
            act.dma_start(sdn[:, :], a["sw_down"]).then_inc(d_sw, 16)
            act.dma_start(cw[:, :, :, :], a["ctx"].rearrange("e (t p) d -> p e t d", p=P)).then_inc(d_cw, 16)

            def weights_high(c, count):
                wait(act, p_wm, count)
                act.copy(w_hi[c][:, :, :], st_c[c][:, :, :]).then_inc(a_wh, 1)

            ln_scalar(act, 0)
            for n, c in enumerate((H0, VC, H1)):
                weights_high(c, n + 1)
            ln_high(act, 0)
            act.wait_ge(v_b, 1)

            def proj_high(pl, t, number, pos):
                kind, m, hp, n = t
                src = bJ[pos % 2]
                if kind == "w":
                    return
                wait(act, t_j, number + 1)
                if kind == "v":
                    if n == 0:
                        wait(act, t_o, pl.pair(0))
                    act.copy(v_hi[:, 2 * n:2 * n + 2, :, :].rearrange("p t h d -> p (t h d)"), src[:, :]).then_inc(a_v, 1)
                    return
                g_h = 0 if pl is None else (pl.g + (1 if kind == "next" else 0)) * 2 + hp
                if n == 0 and pl is not None:
                    wait(act, t_sc, pl.pair(B) if kind == "next" else pl.pair(0))
                apart(act)
                act.activation(qk_hi[:, hp, m, n * HALF:(n + 1) * HALF], src[:, :], ACT.Identity,
                               bias=b_col[:, bass.ds(g_h + m * H, 1)]).then_inc(a_qk, 1)

            for pos, t in enumerate(PRO_TILES):
                proj_high(None, t, pos, pos)

            def body(pl):
                for i in range(PAIRS + (2 if pl.last else 0)):
                    if not (pl.first and i < 1) and i < PAIRS + 1:
                        p = pl.pair(i - 1)
                        wait(act, t_pT, p + 1)
                        wait(act, t_o, p - 1 if not (pl.first and i - 1 < 2) else 0)
                        act.copy(pT_hi[:, (i - 1) % 2, :, :].rearrange("p a b -> p (a b)"), bP[(i - 1) % 2][:, :]).then_inc(a_pT, 1)
                    if i < PAIRS:
                        p = pl.pair(i)
                        wait(act, v_max, p + 1)
                        wait(act, t_pT, p - 1 if not (pl.first and i < 2) else 0)
                        for qt in range(2):
                            ex = act.activation(prob[:, i % 2, qt, :], bS[i % 2][:, qt * S:(qt + 1) * S], ACT.Exp,
                                                bias=nmax[:, i % 2, qt:qt + 1], scale=SCALE,
                                                accum_out=rsum[:, i % 2, qt:qt + 1])
                        ex.then_inc(a_exp, 1)
                    if not (pl.first and i < 2):
                        j = (i - 2) % PAIRS
                        hp, b = j // B, j % B
                        wait(act, t_o, pl.pair(i - 2) + 1)
                        if hp == 0 and not pl.first and 2 <= i < PAIRS:
                            wait(act, t_j, pl.w_tile_number(b) + 1)
                        head = pl.g * 2 + (hp if i >= 2 else hp - 2) + 2 * H
                        apart(act)
                        act.activation(oT_hi[:, hp, b * S:(b + 1) * S], bO[i % 2][:, 0:S], ACT.Identity,
                                       bias=b_col[:, bass.ds(head, 1)]).then_inc(a_o, 1)
                    for t, number, pos in pl.of_slot(i):
                        proj_high(pl, t, number, pos)
                    if i in (1, 3, 5, 7) and not (pl.last and i != 7):
                        c = {1: H0, 3: VC, 5: H1, 7: WC}[i]
                        if c == H0:
                            wait(act, t_j, pl.tiles[0][2])
                        elif c == VC:
                            wait(act, t_j, pl.tiles[5][2] + 1)
                        elif c == H1:
                            wait(act, t_j, [n for s, t, n, _ in pl.tiles if t[0] == "qk"][-1] + 1)
                        elif not pl.first:
                            wait(act, t_j, pl.w_tile_number(B - 1) + 1)
                        weights_high(c, pl.weights(c, 0 if c == WC else 1))

            over_groups(act, body)

            for e in range(NROUTE):
                act.wait_ge(t_c, e + 1)
                act.copy(cT_hi[:, e, :, :].rearrange("p a b -> p (a b)"), bank[e][:, :]).then_inc(a_c, 1)
            ln_scalar(act, 1)
            ln_high(act, 1)
            for n in range(NROUTE * 4):
                s = n % 4
                act.wait_ge(t_z, n + 1)
                wait(act, v_tm, n - 1)
                act.activation(gact[:, n % 2, :], Z_BANKS[s][:, :], ACT.Silu).then_inc(a_z, 1)
                act.wait_ge(v_tm, n + 1)
                wait(act, t_y, n - 1)
                act.copy(gu_hi[:, n % 2, :], gm[:, n % 2, :]).then_inc(a_g, 1)

            ln_scalar(act, 2)
            act.wait_ge(t_y, NROUTE * 4)
            for i in (0, 2):
                act.wait_ge(t_ln, 8 + i + 1)
                half, kt = i // KT, i % KT
                act.copy(hT_f[:, kt, half * HALF:(half + 1) * HALF], LN_BANKS[i][:, :]).then_inc(a_hf, 1)
            act.wait_ge(t_r, 1)
            act.activation(score[:, :, :].rearrange("p t e -> p (t e)"), bank[6][:, 0:NT * NE], ACT.Sigmoid).then_inc(a_r, 1)

            def silu(n, count):
                wait(act, t_gu, count + 1)
                wait(act, v_h, count - 1)
                act.activation(sg[:, n % 2, :], bG[n % 2][:, 0:FI], ACT.Silu).then_inc(a_s, 1)

            def hidden_copy(n, count):
                wait(act, t_hT, count + 1)
                wait(act, t_dn, count - 1)
                act.copy(hidT[:, n % 2, :], bH[n % 2][:, 0:SLOTS]).then_inc(a_hT, 1)

            for n in range(SH + 1):
                if n < SH:
                    silu(n, n)
                if n >= 1:
                    hidden_copy(n - 1, n - 1)

            def trip(it, first, last):
                for u in range(STEPS + (2 if last else 0)):
                    j = it * STEPS + u
                    if u < STEPS:
                        silu(u, j + SH)
                    if not (first and u < 1) and u < STEPS + 1:
                        hidden_copy(u - 1 + STEPS, j - 1 + SH)
                    if not (first and u < 2):
                        wait(act, t_dn, j - 1 + SH)
                        s = (u - 2) % STEPS
                        if not first:
                            wait(act, d_y[s], (it + 1 if u >= 2 else it) * 16)
                        act.copy(ysb[:, s, :], bY[u % 2][:, 0:D]).then_inc(a_y, 1)

            trip(0, True, False)
            with act.Fori(1, TRIPS - 1) as it:
                trip(it, False, False)
            trip(TRIPS - 1, False, True)

        @block.vector
        def _(dve):
            dve.wait_ge(d_x, 16)
            ln_vector(dve, 0, x_in)
            dve.wait_ge(t_b, 1)
            dve.tensor_copy(b_col[:, :], bJ[0][:, 0:3 * H]).then_inc(v_b, 1)
            dve.wait_ge(t_rw, 1)
            dve.tensor_copy(rwT[:, :, :].rearrange("p k e -> p (k e)"), bJ[1][:, 0:KT * NE]).then_inc(v_rw, 1)
            ln_low(dve, 0)
            dve.wait_ge(v_b, 1)

            def proj_low(pl, t, number, pos, final=False):
                kind, m, hp, n = t
                src = bJ[pos % 2]
                if kind == "w":
                    wait(dve, t_j, number + 1)
                    dst = x_acc[:, 2 * n:2 * n + 2, :]
                    if n == 0:
                        wait(dve, v_w, pl.w_done_count(0, final) - 1)
                    dve.tensor_tensor(dst, src[:, :].rearrange("p (a b) -> p a b", a=2), dst, ALU.add).then_inc(v_w, 1)
                elif kind == "v":
                    wait(dve, a_v, pl.v_count(n))
                    sl = v_lo[:, 2 * n:2 * n + 2, :, :].rearrange("p t h d -> p (t h d)")
                    hi = v_hi[:, 2 * n:2 * n + 2, :, :].rearrange("p t h d -> p (t h d)")
                    dve.tensor_tensor(sl, src[:, :], hi, ALU.subtract).then_inc(v_v, 1)
                else:
                    wait(dve, a_qk, pos + 1 if pl is None else pl.qk_count(t))
                    g_h = 0 if pl is None else (pl.g + (1 if kind == "next" else 0)) * 2 + hp
                    dve.scalar_tensor_tensor(out=qk_lo[:, hp, m, n * HALF:(n + 1) * HALF], in0=src[:, :],
                                             scalar=b_col[:, bass.ds(g_h + m * H, 1)],
                                             in1=qk_hi[:, hp, m, n * HALF:(n + 1) * HALF],
                                             op0=ALU.add, op1=ALU.subtract).then_inc(v_qk, 1)

            for pos, t in enumerate(PRO_TILES):
                proj_low(None, t, pos, pos)

            def body(pl):
                for i in range(PAIRS + (2 if pl.last else 0)):
                    if i < PAIRS:
                        p = pl.pair(i)
                        wait(dve, t_sc, p + 1)
                        dve.tensor_reduce(rmax[:, i % 2, :], bS[i % 2][:, :].rearrange("p (q k) -> p q k", q=2),
                                          AX.X, ALU.max).then_inc(v_m1, 1)
                        wait(dve, v_m1, p + 1)
                        wait(dve, a_exp, p - 1 if not (pl.first and i < 2) else 0)
                        dve.tensor_scalar(nmax[:, i % 2, :], rmax[:, i % 2, :], -SCALE, None, ALU.mult).then_inc(v_max, 1)
                    if not (pl.first and i < 1) and i < PAIRS + 1:
                        p = pl.pair(i - 1)
                        wait(dve, a_pT, p + 1)
                        j = (i - 1) % 2
                        dve.tensor_tensor(pT_lo[:, j, :, :].rearrange("p a b -> p (a b)"), bP[j][:, :],
                                          pT_hi[:, j, :, :].rearrange("p a b -> p (a b)"), ALU.subtract).then_inc(v_pT, 1)
                    if not (pl.first and i < 2):
                        j = (i - 2) % PAIRS
                        hp, b = j // B, j % B
                        wait(dve, a_o, pl.pair(i - 2) + 1)
                        head = pl.g * 2 + (hp if i >= 2 else hp - 2) + 2 * H
                        dve.scalar_tensor_tensor(out=oT_lo[:, hp, b * S:(b + 1) * S], in0=bO[i % 2][:, 0:S],
                                                 scalar=b_col[:, bass.ds(head, 1)], in1=oT_hi[:, hp, b * S:(b + 1) * S],
                                                 op0=ALU.add, op1=ALU.subtract).then_inc(v_o, 1)
                    if i < PAIRS:
                        wait(dve, a_exp, pl.pair(i) + 1)
                        dve.reciprocal(rinv[:, i % 2, :], rsum[:, i % 2, :]).then_inc(v_ri, 1)
                        wait(dve, v_ri, pl.pair(i) + 1)
                        for qt in range(2):
                            sc = dve.tensor_scalar(prob[:, i % 2, qt, :], prob[:, i % 2, qt, :],
                                                   rinv[:, i % 2, qt:qt + 1], None, ALU.mult)
                        sc.then_inc(v_p, 1)
                    for t, number, pos in pl.of_slot(i):
                        proj_low(pl, t, number, pos)
                if pl.last:
                    for t, number, pos in pl.of_slot(PAIRS + 2):
                        proj_low(pl, t, number, pos, final=True)

            over_groups(dve, body)
            dve.wait_ge(v_w, 4 * G + 1)
            ln_vector(dve, 1, x_acc)
            for e in range(NROUTE):
                dve.wait_ge(a_c, e + 1)
                dve.tensor_tensor(cT_lo[:, e, :, :].rearrange("p a b -> p (a b)"), bank[e][:, :],
                                  cT_hi[:, e, :, :].rearrange("p a b -> p (a b)"), ALU.subtract).then_inc(v_c, 1)
            ln_low(dve, 1)
            dve.wait_ge(p_mask, NROUTE + 2)
            for n in range(NROUTE * 4):
                e, s = n // 4, n % 4
                half = s // KT
                dve.wait_ge(a_z, n + 1)
                wait(dve, a_g, n - 1)
                dve.tensor_tensor(gm[:, n % 2, :], Z_BANKS[s][:, :], gact[:, n % 2, :], ALU.mult).then_inc(v_t, 1)
                dve.wait_ge(v_t, n + 1)
                dve.tensor_tensor(gm[:, n % 2, :], gm[:, n % 2, :], mask[:, e, half * HALF:(half + 1) * HALF], ALU.mult).then_inc(v_tm, 1)
                dve.wait_ge(a_g, n + 1)
                dve.tensor_tensor(gu_lo[:, n % 2, :], gm[:, n % 2, :], gu_hi[:, n % 2, :], ALU.subtract).then_inc(v_g, 1)
            for j in range(4):
                dve.wait_ge(t_y, NROUTE * 4)
                dst = x_acc[:, 2 * j:2 * j + 2, :]
                dve.tensor_tensor(dst, Y_BANKS[j][:, :].rearrange("p (a b) -> p a b", a=2), dst, ALU.add).then_inc(v_y, 1)

            dve.wait_ge(v_y, 4)
            ln_vector(dve, 2, x_acc)
            dve.wait_ge(t_y, NROUTE * 4)
            for i in (1, 3):
                dve.wait_ge(t_ln, 8 + i + 1)
                half, kt = i // KT, i % KT
                dve.tensor_copy(hT_f[:, kt, half * HALF:(half + 1) * HALF], LN_BANKS[i][:, :]).then_inc(v_hf, 1)

            done = [0]

            def own(ins):
                done[0] += 1
                ins.then_inc(v_own, 1)
                dve.wait_ge(v_own, done[0])

            dve.wait_ge(a_r, 1)
            dve.wait_ge(d_r, 32)
            own(dve.tensor_tensor(sel[:, :, :], score[:, :, :], rb[:, :].unsqueeze(1).to_broadcast([P, NT, NE]), ALU.add))
            for t in range(NT):
                ins = dve.max(top[:, t, :], sel[:, t, :])
            own(ins)
            for t in range(NT):
                ins = dve.max_index(topi[:, t, :], top[:, t, :], sel[:, t, :])
            own(ins)
            own(dve.tensor_copy(chosen[:, :, :], topi[:, :, 0:TOPK].rearrange("p t k -> p k t")))
            dve.wait_ge(p_const, 11)
            own(dve.tensor_tensor(hot[:, :, :, :].rearrange("p k t e -> p (k t) e"),
                                  chosen[:, :, :].rearrange("p k t -> p (k t)").unsqueeze(2).to_broadcast([P, CH, NE]),
                                  iota_e[:, :].unsqueeze(1).to_broadcast([P, CH, NE]), ALU.is_equal))
            with nc.allow_low_precision(reason="counts of at most 1 in bfloat16"):
                dve.tensor_reduce(member[:, :, :], hot[:, :, :, :].rearrange("p k t e -> p t e k"), AX.X, ALU.add).then_inc(v_r, 1)
            dve.wait_ge(t_r, 2)
            own(dve.tensor_copy(count[:, :], bank[1][0:NE, 0:1]))
            own(dve.tensor_scalar(over[:, :], iota_f[:, :], count[:, 0:1], None, ALU.is_lt))
            own(dve.tensor_reduce(tiles_e[:, :], over[:, :], AX.X, ALU.add))
            dve.tensor_scalar(tiles_b[:, :], ones[0:NE, :], tiles_e[:, 0:1], None, ALU.mult).then_inc(v_r, 1)
            dve.wait_ge(t_r, 3)
            own(dve.tensor_copy(end_e[:, :], bank[6][0:NE, 0:1]))
            dve.tensor_scalar(past[:, :], iota_t[0:NE, :], end_e[:, 0:1], None, ALU.is_ge).then_inc(v_r, 1)
            own(dve.tensor_scalar(base[:, :], bank[7][:, 0:NE], float(SLOTS), None, ALU.mult))
            own(dve.tensor_tensor(place[:, :, :], bank[0][:, 0:NT * NE].rearrange("p (t e) -> p t e", e=NE),
                                  base[:, :].unsqueeze(1).to_broadcast([P, NT, NE]), ALU.add))
            dve.wait_ge(t_r, 4)
            dve.tensor_scalar(expert[:, :], bank[1][0:1, 0:TILES], float(NE - 1), None, ALU.min).then_inc(v_r, 1)
            own(dve.tensor_tensor(work[:, :, :, :], hot[:, :, :, :],
                                  place[:, :, :].unsqueeze(1).to_broadcast([P, TOPK, NT, NE]), ALU.mult))
            own(dve.tensor_reduce(slot_f[:, :, :], work[:, :, :, :], AX.X, ALU.add))
            own(dve.tensor_copy(slot_i[:, :, :], slot_f[:, :, :]))
            flat = slot_i[:, :, :].rearrange("p k t -> p (k t)")
            dve.tensor_scalar(part_i[:, 0, :], flat, 7, None, ALU.logical_shift_right)
            own(dve.tensor_scalar(part_i[:, 1, :], flat, SLOTS - 1, None, ALU.bitwise_and))
            own(dve.tensor_copy(part_h[:, :, :], part_i[:, :, :]))
            dve.tensor_tensor(in_slot[:, :, :], part_h[:, 1, :].unsqueeze(2).to_broadcast([P, CH, SLOTS]),
                              iota_s[:, :].unsqueeze(1).to_broadcast([P, CH, SLOTS]), ALU.is_equal)
            own(dve.tensor_tensor(in_tile[:, :, :], part_h[:, 0, :].unsqueeze(2).to_broadcast([P, CH, TILES]),
                                  iota_t[:, :].unsqueeze(1).to_broadcast([P, CH, TILES]), ALU.is_equal))
            dve.tensor_tensor(in_tile[:, :, :], in_tile[:, :, :],
                              tok_id[:, :, :].rearrange("p k t -> p (k t)").unsqueeze(2).to_broadcast([P, CH, TILES]),
                              ALU.mult).then_inc(v_r, 1)
            own(dve.tensor_tensor(work[:, :, :, :], hot[:, :, :, :],
                                  score[:, :, :].unsqueeze(1).to_broadcast([P, TOPK, NT, NE]), ALU.mult))
            own(dve.tensor_reduce(gain[:, :, :], work[:, :, :, :], AX.X, ALU.add))
            own(dve.tensor_reduce(gsum[:, :], gain[:, :, :].rearrange("p k t -> p t k"), AX.X, ALU.add))
            own(dve.tensor_scalar(gsum[:, :], gsum[:, :], 1e-20, None, ALU.add))
            own(dve.reciprocal(gsum[:, :], gsum[:, :]))
            own(dve.tensor_tensor(gain[:, :, :], gain[:, :, :], gsum[:, :].unsqueeze(1).to_broadcast([P, TOPK, NT]), ALU.mult))

            def product(n, count):
                wait(dve, a_s, count + 1)
                wait(dve, t_hT, count - 1)
                dve.tensor_tensor(hid[:, n % 2, :], bG[n % 2][:, FI:2 * FI], sg[:, n % 2, :], ALU.mult).then_inc(v_h, 1)

            for n in range(SH + 2):
                if n < SH:
                    product(n, n)
                if n >= 2:
                    t = n - 2
                    dve.wait_ge(t_dn, t + 1)
                    dve.tensor_tensor(x_acc[:, t, :], bY[t % 2][:, 0:D], x_acc[:, t, :], ALU.add).then_inc(v_sh, 1)
            dve.wait_ge(t_r, 5)
            dve.tensor_copy(source[:, :], bank[0][:, 0:TILES]).then_inc(v_r, 1)

            def row_copy(j, u):
                wait(dve, t_x, j + 1)
                wait(dve, t_gu, j - 1 + SH)
                dve.tensor_copy(xT[:, u % 2, :], bX[u % 2][:, 0:D]).then_inc(v_x, 1)

            def trip(it, last):
                for u in range(STEPS):
                    j = it * STEPS + u
                    if u < STEPS - 1 or not last:
                        row_copy(j + 1, u + 1)
                    product(u, j + SH)

            row_copy(0, 0)
            with dve.Fori(0, TRIPS - 1) as it:
                trip(it, False)
            trip(TRIPS - 1, True)

            flat_gain = gain[:, :, :].rearrange("p k t -> p (k t)")

            def combine(k, first):
                for t in range(NT):
                    wait(dve, d_yg[t], k * 16 + 16)
                    if first:
                        wait(dve, v_sh, t + 1)
                    else:
                        wait(dve, v_cmb, (k - 1) * NT + t + 1)
                    dve.scalar_tensor_tensor(out=x_acc[:, t, :], in0=yg[:, t, :], scalar=flat_gain[:, bass.ds(k * NT + t, 1)],
                                             in1=x_acc[:, t, :], op0=ALU.mult, op1=ALU.add).then_inc(v_cmb, 1)

            combine(0, True)
            with dve.Fori(1, TOPK) as k:
                combine(k, False)


_INS = {"x": "x", "tok": "itok_BxS_13_99985", "ctx": "ctx_2048",
        **{n: f"L0_attn_{n}" for n in ("wq_codes", "wq_scales", "bq", "wk_codes", "wk_scales", "bk",
                                       "wv_codes", "wv_scales", "bv", "wo_codes", "wo_scales", "bo")},
        **{n: f"L0_ffn_{n}" for n in ("router_w", "bias", "w_gate", "w_up", "w_down",
                                      "sw_gate", "sw_up", "sw_down")}}


def kernel(**inputs):
    import numpy as _np
    import concourse.bacc as _bacc
    from concourse import mybir as _mybir
    from concourse.bass_utils import run_bass_kernel_spmd as _run

    nc = _bacc.Bacc("TRN2", target_bir_lowering=False, num_devices=1)
    arrays, args = {}, {}
    for short, name in _INS.items():
        arr = _np.ascontiguousarray(inputs[name])
        arrays[f"in_{short}"] = arr
        args[short] = nc.dram_tensor(f"in_{short}", arr.shape, _mybir.dt.from_np(arr.dtype), kind="ExternalInput").ap()
    out = nc.dram_tensor("out_0", (B, S, D), _mybir.dt.float32, kind="ExternalOutput").ap()
    decoder_layer(nc, args, out)
    r = _run(nc, [arrays], core_ids=[0])
    return r.results[0]["out_0"]
```

```python
from contextlib import ExitStack

import concourse.bass as bass
from concourse import mybir

F32 = mybir.dt.float32
F32R = mybir.dt.float32r
F16 = mybir.dt.float16
BF16 = mybir.dt.bfloat16
U32 = mybir.dt.uint32
I32 = mybir.dt.int32
ALU = mybir.AluOpType
ACT = mybir.ActivationFunctionType
AX = mybir.AxisListType

P = 128
T = 1024
D = 256
NT = T // P
KT = D // P
B, S = 4, 256
H, HD = 16, 128
FEAT = H * HD
QB = 32
G = H // 2
PAIRS = 2 * B
SCALE = float(HD) ** -0.5
EPS = 1e-5
NROUTE = 4
VOCAB = 12500
HALF = 512
NH = T // HALF
NE, TOPK, FI = 32, 4, 128

SLOTS = 128
TILES = (T * TOPK + NE * (SLOTS - 1)) // SLOTS + 1
STEPS = 8
TRIPS = TILES // STEPS
PACK = 4
assert TRIPS * STEPS == TILES == 64
CH = TOPK * NT
EW = 3 * D

Q, K, V, W = 0, 1, 2, 3
H0, VC, H1, WC = 0, 1, 2, 3


def wait(eng, sem, value):
    if isinstance(value, int) and value <= 0:
        return
    eng.wait_ge(sem, value)


def apart(eng):
    eng.nop(nofuse=True)


def slot_tiles(first, last):
    s = [[("qk", Q, 1, 0), ("w", W, 0, 0)],
         [("qk", K, 1, 0), ("w", W, 0, 1)],
         [("qk", Q, 1, 1), ("v", V, 0, 0)],
         [("v", V, 0, 1), ("w", W, 0, 2)],
         [("v", V, 0, 2), ("qk", K, 1, 1)],
         [("v", V, 0, 3), ("w", W, 0, 3)],
         [("next", Q, 0, 0), ("next", K, 0, 0)],
         [("next", Q, 0, 1), ("next", K, 0, 1)]]
    keep = lambda t: not (first and t[0] == "w") and not (last and t[0] == "next")
    return [[t if keep(t) else None for t in slot] for slot in s]


PREP_SLOTS = {1: H0, 5: VC, 6: H1, 7: WC}
TURN, ATTEND = 2, 3
DRAIN = ATTEND
PRO_TILES = [("next", Q, 0, 0), ("next", K, 0, 0), ("next", Q, 0, 1), ("next", K, 0, 1)]


class Plan:

    def __init__(self, g):
        self.g = g
        self.first = isinstance(g, int) and g == 0
        self.last = isinstance(g, int) and g == G - 1
        self.slots = slot_tiles(self.first, self.last)
        n = 0
        self.tiles = []
        start = 4 if self.first else 16 * g
        for i, slot in enumerate(self.slots):
            for place, t in enumerate(slot):
                if t is not None:
                    self.tiles.append((i, t, start + n, n, place))
                    n += 1
        if self.last:
            for b in range(B):
                self.tiles.append((PAIRS + b, ("w", W, 0, b), start + n, n, 1))
                n += 1

    def of_slot(self, i, place):
        if i < 0:
            return [] if self.first else [(("prev", K, 0, 1), None, 1, False)]
        return [(t, number, pos, s >= PAIRS) for s, t, number, pos, at in self.tiles if s == i and at == place]

    def pair(self, i):
        return self.g * PAIRS + i

    def qk_count(self, t):
        kind, m, hp, half = t
        at = {(Q, 0): 0, (K, 0): 1, (Q, 1): 2, (K, 1): 3}[(m, half)] + 1
        if kind == "next":
            return self.g * 8 + 8 + at
        if kind == "prev":
            return self.g * 8 + at
        return self.g * 8 + 4 + at

    def v_count(self, n):
        return self.g * 4 + n + 1

    def w_done_count(self, b, final):
        return (self.g * 4 if final else (self.g - 1) * 4) + b + 2

    def freed(self, pos):
        if pos >= 2:
            t = self.tiles[pos - 2][1]
            final = self.last and self.tiles[pos - 2][0] >= PAIRS
        else:
            t, final = ("prev", (Q, K)[pos], 0, 1), False
        kind, m, hp, n = t
        if kind in ("prev", "qk", "next"):
            return "qk", self.qk_count(t)
        if kind == "v":
            return "v", self.v_count(n)
        return "w", self.w_done_count(n, final)

    def w_tile_number(self, b):
        for s, t, number, pos, place in self.tiles:
            if t[0] == "w" and t[3] == b and s < PAIRS:
                return number

    def weights(self, chunk, ahead):
        if ahead == 0 and self.first and chunk != WC:
            return {H0: 1, VC: 2, H1: 3}[chunk]
        base = self.g * 4 + 3 if (ahead or chunk == WC) else (self.g - 1) * 4 + 3
        return base + {H0: 1, VC: 2, H1: 3, WC: 4}[chunk] - (3 if (self.last and chunk == WC and not ahead) else 0)


def over_groups(eng, body):
    body(Plan(0))
    with eng.Fori(1, G - 1) as g:
        body(Plan(g))
    body(Plan(G - 1))


def decoder_layer(nc, a, out):
    ctx = ExitStack()
    with ctx:
        def sb(name, shape, dt=F32):
            return ctx.enter_context(nc.sbuf_tensor(name, shape, dt))

        def sem(name):
            return ctx.enter_context(nc.semaphore(name))

        bank = [ctx.enter_context(nc.psum_tensor(f"bank{n}", [P, HALF], F32)) for n in range(8)]
        bS, bP, bO, bJ = bank[0:2], bank[2:4], bank[4:6], bank[6:8]

        Z_BANKS = bank[2:6]
        Y_BANKS = [bank[0], bank[1], bank[6], bank[7]]

        ident = sb("ident", [P, P])
        x_in = sb("x_in", [P, NT, D])
        h_row = sb("h_row", [P, NT, D])
        x_acc = sb("x_acc", [P, NT, D])
        bo_b = sb("bo_b", [P, D])
        b_rows = sb("b_rows", [3 * H, HD])
        b_col = sb("b_col", [P, 3 * H])
        rw_rows = sb("rw_rows", [NE, D])
        rwT = sb("rwT", [P, KT, NE])
        rb = sb("rb", [P, NE])
        sgu = sb("sgu", [P, KT, 2, FI])
        sdn = sb("sdn", [P, D])
        iota_e = sb("iota_e", [P, NE])
        iota_t = sb("iota_t", [P, TILES], F16)
        iota_s = sb("iota_s", [P, SLOTS], F16)
        powers = sb("powers", [1, TILES // PACK, PACK])
        iota_f = sb("iota_f", [NE, NT])
        tok_id = sb("tok_id", [P, TOPK, NT], F16)
        before = sb("before", [P, P], BF16)
        upto = sb("upto", [NE, NE], BF16)
        ones = sb("ones", [P, P], BF16)
        moe_at = nc.sbuf_base
        st_c = [sb(f"st_c{c}", [P, 4, P]) for c in range(4)]
        st_s = [sb(f"st_s{c}", [P, 4, P]) for c in range(4)]
        w_hi = [sb(f"w_hi{c}", [P, 4, P], F32R) for c in range(4)]
        w_lo = [sb(f"w_lo{c}", [P, 4, P], F32R) for c in range(4)]
        qk_hi = sb("qk_hi", [P, 2, 2, T], F32R)
        qk_lo = sb("qk_lo", [P, 2, 2, T], F32R)
        v_hi = sb("v_hi", [P, NT, 2, HD], F32R)
        v_lo = sb("v_lo", [P, NT, 2, HD], F32R)
        oT_hi = sb("oT_hi", [P, 2, T], F32R)
        oT_lo = sb("oT_lo", [P, 2, T], F32R)
        moe_w = nc.alloc_sbuf_tensor_at("moe_w", [P, NE, EW], F32, offset=moe_at)
        assert nc.sbuf_base >= moe_at + NE * EW * 4
        prob = sb("prob", [P, 4, 2, S])
        pT_hi = sb("pT_hi", [P, 2, 2, S], F32R)
        pT_lo = sb("pT_lo", [P, 2, 2, S], F32R)
        rmax = sb("rmax", [P, 2, 2])
        nmax = sb("nmax", [P, 2, 2])
        rsum = sb("rsum", [P, 2, 2])
        rinv = sb("rinv", [P, 2, 2])
        bn = sb("bn", [P, NT, 6])
        mv = sb("mv", [P, NT, 2])
        var = sb("var", [P, NT])
        sd = sb("sd", [P, NT])
        rstd = sb("rstd", [P, NT])
        nt1 = sb("nt1", [P, NT])
        ids = sb("ids", [P, T], I32)
        cw = sb("cw", [P, NROUTE, KT, D])
        hT_f = cw[:, :, :, :].rearrange("p (k a) t d -> p k (a t d)", k=KT)
        arena_at = nc.sbuf_base
        hT_hi = sb("hT_hi", [P, KT, T], F32R)
        hT_lo = sb("hT_lo", [P, KT, T], F32R)
        cT_hi = sb("cT_hi", [P, NROUTE, KT, D], F32R)
        cT_lo = sb("cT_lo", [P, NROUTE, KT, D], F32R)
        mask = sb("mask", [P, NROUTE, T])
        arena_end = nc.sbuf_base
        cursor = [arena_at]

        def later(name, shape, dt=F32):
            n = {F32: 4, I32: 4, U32: 4, F16: 2, BF16: 2}[dt]
            for m in shape[1:]:
                n *= m
            t = nc.alloc_sbuf_tensor_at(name, shape, dt, offset=cursor[0])
            cursor[0] += -(-n // 32) * 32
            assert cursor[0] <= arena_end
            return t

        score = later("score", [P, NT, NE])
        sel = later("sel", [P, NT, NE])
        top = later("top", [P, NT, 8])
        topi = later("topi", [P, NT, 8], U32)
        chosen = later("chosen", [P, TOPK, NT])
        hot = later("hot", [P, TOPK, NT, NE])
        work = later("work", [P, TOPK, NT, NE])
        member = later("member", [P, NT, NE], BF16)
        count = later("count", [NE, 1])
        over = later("over", [NE, NT])
        tiles_e = later("tiles_e", [NE, 1])
        tiles_b = later("tiles_b", [NE, P], BF16)
        end_e = later("end_e", [NE, 1])
        past = later("past", [NE, TILES], BF16)
        expert = later("expert", [1, TILES])
        packed = later("packed", [1, TILES // PACK], I32)
        base = later("base", [P, NE])
        place = later("place", [P, NT, NE])
        slot_f = later("slot_f", [P, TOPK, NT])
        slot_i = later("slot_i", [P, TOPK, NT], I32)
        part_i = later("part_i", [P, 2, CH], I32)
        part_h = later("part_h", [P, 2, CH], F16)
        in_tile = later("in_tile", [P, CH, TILES], F16)
        in_slot_at = cursor[0]
        in_slot = later("in_slot", [P, CH, SLOTS], F16)
        gain = later("gain", [P, TOPK, NT])
        gsum = later("gsum", [P, NT])
        source = later("source", [P, TILES], I32)
        src = later("src", [P, STEPS], I32)
        xg = later("xg", [P, STEPS, D])
        xT = later("xT", [P, 2, D])
        sg = later("sg", [P, 2, FI])
        hid = later("hid", [P, 2, FI])
        hidT = later("hidT", [P, 2, SLOTS])
        ysb = later("ysb", [P, STEPS, D])
        cursor[0] = in_slot_at
        yg = later("yg", [P, NT, D])
        gact = x_in[:, 0:4, :].rearrange("p (a t) d -> p a (t d)", a=2)
        gm = prob[:, 0:2, :, :].rearrange("p a q k -> p a (q k)")
        gu_hi = pT_hi[:, :, :, :].rearrange("p a q k -> p a (q k)")
        gu_lo = pT_lo[:, :, :, :].rearrange("p a q k -> p a (q k)")
        zeros = sb("zeros", [1, HALF])

        d_x, d_b, d_bo, d_ids, d_cw = sem("d_x"), sem("d_b"), sem("d_bo"), sem("d_ids"), sem("d_cw")
        d_w = [sem(f"d_w{c}") for c in range(4)]
        d_out = sem("d_out")
        p_const = sem("p_const")
        p_mask = sem("p_mask")
        p_wm = sem("p_wm")
        a_wh = sem("a_wh")
        p_wl = sem("p_wl")
        v_ln = sem("v_ln")
        a_sd = sem("a_sd")
        t_ln, a_ln, v_lnlo = sem("t_ln"), sem("a_ln"), sem("v_lnlo")
        t_b, v_b = sem("t_b"), sem("v_b")
        t_sc = sem("t_sc")
        v_m1, v_max = sem("v_m1"), sem("v_max")
        a_exp = sem("a_exp")
        v_ri, v_p = sem("v_ri"), sem("v_p")
        t_pT, a_pT, v_pT = sem("t_pT"), sem("a_pT"), sem("v_pT")
        t_o, a_o, v_o = sem("t_o"), sem("a_o"), sem("v_o")
        t_j = sem("t_j")
        a_qk, v_qk = sem("a_qk"), sem("v_qk")
        a_v, v_v = sem("a_v"), sem("v_v")
        v_w = sem("v_w")
        t_c, a_c, v_c = sem("t_c"), sem("a_c"), sem("v_c")
        t_z, a_z = sem("t_z"), sem("a_z")
        v_t, v_tm, a_g, v_g = sem("v_t"), sem("v_tm"), sem("a_g"), sem("v_g")
        t_y, v_y = sem("t_y"), sem("v_y")
        d_r, d_sw, d_h = sem("d_r"), sem("d_sw"), sem("d_h")
        d_m = sem("d_m")
        t_rw, v_rw = sem("t_rw"), sem("v_rw")
        a_hf, v_hf = sem("a_hf"), sem("v_hf")
        t_r, a_r, v_r = sem("t_r"), sem("a_r"), sem("v_r")
        t_gu, a_s, v_h = sem("t_gu"), sem("a_s"), sem("v_h")
        t_hT, a_hT, t_dn = sem("t_hT"), sem("a_hT"), sem("t_dn")
        v_sh, a_y = sem("v_sh"), sem("a_y")
        t_x, v_x = sem("t_x"), sem("v_x")
        d_g = [sem(f"d_g{u}") for u in range(STEPS)]
        d_y = [sem(f"d_y{u}") for u in range(STEPS)]
        d_yg = [sem(f"d_yg{t}") for t in range(NT)]
        v_own = sem("v_own")
        p_src, v_cmb = sem("p_src"), sem("v_cmb")

        bX, bG, bH, bY = bank[0:2], bank[2:4], bank[4:6], bank[6:8]
        SH = NT

        h_dram = nc.dram_tensor("h_dram", (T, D), F32, kind="Internal").ap()
        y_dram = nc.dram_tensor("y_dram", (TILES * SLOTS, D), F32, kind="Internal").ap()
        x_rows = a["x"].rearrange("b s d -> (b s) d").rearrange("(t p) d -> p t d", p=P)
        out_rows = out.rearrange("b s d -> (b s) d").rearrange("(t p) d -> p t d", p=P)
        codes = [a[f"w{n}_codes"].rearrange("(t p) n -> p t n", p=P) for n in "qkv"]
        scales = [a[f"w{n}_scales"] for n in "qkv"]
        wo_codes = a["wo_codes"].rearrange("(h p) n -> p h n", p=P)

        def load_chunk(eng, c, g):
            def spread(rows):
                return rows.unsqueeze(1).to_broadcast([rows.shape[0], QB, rows.shape[1]])
            if c in (H0, H1):
                col = g * (2 * HD) + (0 if c == H0 else HD)
                for j, m in enumerate((Q, K)):
                    eng.dma_start(st_c[c][:, KT * j:KT * j + KT, :], codes[m][:, :, bass.ds(col, HD)]).then_inc(d_w[c], 16)
                    for kt in range(KT):
                        eng.dma_start(st_s[c][:, KT * j + kt, :],
                                      spread(scales[m][kt * 4:kt * 4 + 4, bass.ds(col, HD)])).then_inc(d_w[c], 16)
            elif c == VC:
                col = g * (2 * HD)
                dst_c = st_c[c][:, :, :].rearrange("p (t n) e -> p t (n e)", t=KT)
                dst_s = st_s[c][:, :, :].rearrange("p (t n) e -> p t (n e)", t=KT)
                eng.dma_start(dst_c, codes[V][:, :, bass.ds(col, 2 * HD)]).then_inc(d_w[c], 16)
                for kt in range(KT):
                    eng.dma_start(dst_s[:, kt, :],
                                  spread(scales[V][kt * 4:kt * 4 + 4, bass.ds(col, 2 * HD)])).then_inc(d_w[c], 16)
            else:
                dst_c = st_c[c][:, :, :].rearrange("p (h n) e -> p h (n e)", h=2)
                dst_s = st_s[c][:, :, :].rearrange("p (h n) e -> p h (n e)", h=2)
                eng.dma_start(dst_c, wo_codes[:, bass.ds(g * 2, 2), :]).then_inc(d_w[c], 16)
                for hp in range(2):
                    eng.dma_start(dst_s[:, hp, :],
                                  spread(a["wo_scales"][bass.ds(g * 8 + hp * 4, 4), :])).then_inc(d_w[c], 16)

        DMAS = {H0: 6, VC: 3, H1: 6, WC: 3}

        LN_STEPS = 2 * NT + 1 + 5 + NT
        R_MEMBER, R_TILES, R_PAST, R_EXPERT, R_HOT, R_SOURCE = 1, 2, 3, 4, 5, 6

        block = ctx.enter_context(nc.Block())

        @block.sync
        def _(sp):
            sp.dma_start(x_in[:, :, :], x_rows).then_inc(d_x, 16)
            for c in (H0, VC, H1):
                load_chunk(sp, c, 0)
            load_chunk(sp, WC, 0)
            for c, n in ((H0, 1), (VC, 2), (H1, 3)):
                sp.wait_ge(p_wl, n)
                load_chunk(sp, c, 1)

            def reload(g, chunks):
                for c in chunks:
                    sp.wait_ge(p_wl, g * 4 + 3 + {H0: 1, VC: 2, H1: 3, WC: 4}[c])
                    load_chunk(sp, c, g + (1 if c == WC else 2))

            reload(0, (H0, VC, H1, WC))
            with sp.Fori(1, G - 2) as g:
                reload(g, (H0, VC, H1, WC))
            reload(G - 2, (WC,))
            sp.wait_ge(v_w, 4 * G + 1)
            EB = NE // 4
            for q in range(4):
                es = slice(q * EB, (q + 1) * EB)
                gate = a["w_gate"][es, :, :].rearrange("e (t p) i -> p e t i", p=P)
                up = a["w_up"][es, :, :].rearrange("e (t p) i -> p e t i", p=P)
                down = a["w_down"][es, :, :].rearrange("e p d -> p e d")
                gu = moe_w[:, es, 0:2 * D].rearrange("p e (t m) -> p e t m", t=KT)
                for t in range(KT):
                    sp.dma_start(gu[:, :, t, 0:FI], gate[:, :, t, :]).then_inc(d_m, 16)
                    sp.dma_start(gu[:, :, t, FI:2 * FI], up[:, :, t, :]).then_inc(d_m, 16)
                sp.dma_start(moe_w[:, es, 2 * D:EW], down).then_inc(d_m, 16)
            sp.wait_ge(v_ln, 3 * LN_STEPS)
            sp.dma_start(h_dram.rearrange("(t p) d -> p t d", p=P), h_row[:, :, :]).then_inc(d_h, 16)

            for u in range(STEPS):
                sp.sem_inc(d_y[u], 16)
            def store(it):
                for u in range(STEPS):
                    sp.wait_ge(a_y, it * STEPS + u + 1)
                    sp.dma_start(y_dram[bass.ds((it * STEPS + u) * SLOTS, SLOTS), :], ysb[:, u, :]).then_inc(d_y[u], 16)

            with sp.Fori(0, TRIPS) as it:
                store(it)
            for t in range(0, NT, 2):
                sp.wait_ge(v_cmb, (TOPK - 1) * NT + t + 2)
                sp.dma_start(out_rows[:, t:t + 2, :], x_acc[:, t:t + 2, :]).then_inc(d_out, 16)
            sp.wait_ge(d_out, 16 * (NT // 2))

        @block.gpsimd
        def _(pool):
            def prep(c, wm, load_count, free=None):
                wait(pool, d_w[c], load_count)
                pool.tensor_tensor(st_c[c][:, :, :], st_c[c][:, :, :], st_s[c][:, :, :], ALU.mult).then_inc(p_wm, 1)
                wait(pool, p_wm, wm)
                wait(pool, a_wh, wm)
                pool.tensor_tensor(w_lo[c][:, :, :], st_c[c][:, :, :], w_hi[c][:, :, :], ALU.subtract).then_inc(p_wl, 1)

            pool.memset(ident[:, :], 0.0).then_inc(p_const, 1)
            pool.memset(zeros[:, :], 0.0).then_inc(p_const, 1)
            pool.wait_ge(p_const, 2)
            pool.affine_select(out=ident[:, :], in_=ident[:, :], compare_op=ALU.not_equal, fill=1.0,
                               base=0, pattern=[[-1, P]], channel_multiplier=1).then_inc(p_const, 1)
            for n, c in enumerate((H0, VC, H1)):
                prep(c, n + 1, 16 * DMAS[c])
            pool.wait_ge(d_x, 16)
            pool.wait_ge(d_bo, 16)
            pool.tensor_tensor(x_acc[:, :, :], x_in[:, :, :],
                               bo_b[:, :].unsqueeze(1).to_broadcast([P, NT, D]), ALU.add).then_inc(v_w, 1)
            pool.wait_ge(d_ids, 16)
            per = VOCAB // NROUTE
            for e in range(NROUTE):
                pool.tensor_scalar(mask[:, e, :], ids[:, :], float(per * e) if e else float(per), None,
                                   ALU.is_ge if e else ALU.is_lt).then_inc(p_mask, 1)
            pool.wait_ge(p_mask, NROUTE)
            for e in range(1, NROUTE - 1):
                pool.tensor_tensor(mask[:, e, :], mask[:, e, :], mask[:, e + 1, :], ALU.subtract).then_inc(p_mask, 1)

            pool.iota(iota_e[:, :], pattern=[[1, NE]], base=0, channel_multiplier=0,
                      allow_small_or_imprecise_dtypes=True).then_inc(p_const, 1)
            pool.iota(iota_t[:, :], pattern=[[1, TILES]], base=0, channel_multiplier=0,
                      allow_small_or_imprecise_dtypes=True).then_inc(p_const, 1)
            pool.iota(iota_s[:, :], pattern=[[1, SLOTS]], base=0, channel_multiplier=0,
                      allow_small_or_imprecise_dtypes=True).then_inc(p_const, 1)
            pool.iota(iota_f[:, :], pattern=[[SLOTS, NT]], base=0, channel_multiplier=0,
                      allow_small_or_imprecise_dtypes=True).then_inc(p_const, 1)
            pool.iota(tok_id[:, :, :], pattern=[[0, TOPK], [P, NT]], base=0, channel_multiplier=1,
                      allow_small_or_imprecise_dtypes=True).then_inc(p_const, 1)
            pool.memset(ones[:, :], 1.0).then_inc(p_const, 1)
            for i in range(PACK):
                pool.memset(powers[:, :, i:i + 1], float(NE ** i)).then_inc(p_const, 1)
            pool.wait_ge(p_const, 9 + PACK)
            pool.affine_select(out=before[:, :], in_=ones[:, :], compare_op=ALU.is_gt, fill=0.0,
                               base=0, pattern=[[1, P]], channel_multiplier=-1).then_inc(p_const, 1)
            pool.affine_select(out=upto[:, :], in_=ones[0:NE, 0:NE], compare_op=ALU.is_ge, fill=0.0,
                               base=0, pattern=[[1, NE]], channel_multiplier=-1).then_inc(p_const, 1)

            def body(pl):
                g = pl.g
                for c in ((WC,) if pl.last else (H0, VC, H1, WC)):
                    ahead = 0 if c == WC else 1
                    prep(c, pl.weights(c, ahead), (g + ahead) * (16 * DMAS[c]) + 16 * DMAS[c])

            over_groups(pool, body)

            pool.wait_ge(d_h, 16)
            pool.wait_ge(v_r, R_SOURCE)

            def gathers(it, first):
                for u in range(STEPS):
                    wait(pool, t_x, 0 if first else (it - 1) * STEPS + (u + PACK if u % PACK == 0 else u + 1))
                    if u % PACK == 0:
                        pool.tensor_copy(src[:, u:u + PACK], source[:, bass.ds(it * STEPS + u, PACK)]).then_inc(p_src, 1)
                        wait(pool, p_src, it * (STEPS // PACK) + u // PACK + 1)
                    apart(pool)
                    pool.indirect_dma_start(out=xg[:, u, :], out_offset=None, in_=h_dram,
                                            in_offset=bass.IndirectOffsetOnAxis(ap=src[:, u:u + 1], axis=0)).then_inc(d_g[u], 16)

            gathers(0, True)
            with pool.Fori(1, TRIPS) as it:
                gathers(it, False)

            for u in range(STEPS):
                pool.wait_ge(d_y[u], 16 * TRIPS + 16)

            for k in range(TOPK):
                for t in range(NT):
                    wait(pool, v_cmb, (k - 1) * NT + t + 1)
                    pool.indirect_dma_start(out=yg[:, t, :], out_offset=None, in_=y_dram,
                                            in_offset=bass.IndirectOffsetOnAxis(ap=slot_i[:, k, t:t + 1], axis=0)).then_inc(d_yg[t], 16)


        def ln_vector(dve, n, src):
            base = n * LN_STEPS
            for t in range(NT):
                dve.bn_stats(bn[:, t, :], src[:, t, :]).then_inc(v_ln, 1)
            for t in range(NT):
                dve.wait_ge(v_ln, base + t + 1)
                dve.bn_aggr(mv[:, t, :], bn[:, t, :]).then_inc(v_ln, 1)
            dve.wait_ge(v_ln, base + 2 * NT)
            dve.tensor_scalar(var[:, :], mv[:, :, 1], EPS, None, ALU.add).then_inc(v_ln, 1)
            dve.wait_ge(a_sd, n + 1)
            k = base + 2 * NT + 1
            dve.reciprocal(rstd[:, :], sd[:, :]).then_inc(v_ln, 1)
            dve.wait_ge(v_ln, k + 1)
            dve.tensor_tensor(nt1[:, :], rstd[:, :], rstd[:, :], ALU.mult).then_inc(v_ln, 1)
            dve.wait_ge(v_ln, k + 2)
            dve.tensor_tensor(nt1[:, :], nt1[:, :], var[:, :], ALU.mult).then_inc(v_ln, 1)
            dve.wait_ge(v_ln, k + 3)
            dve.tensor_scalar(nt1[:, :], nt1[:, :], -0.5, 1.5, ALU.mult, ALU.add).then_inc(v_ln, 1)
            dve.wait_ge(v_ln, k + 4)
            dve.tensor_tensor(rstd[:, :], rstd[:, :], nt1[:, :], ALU.mult).then_inc(v_ln, 1)
            dve.wait_ge(v_ln, k + 5)
            for t in range(NT):
                dve.tensor_scalar(h_row[:, t, :], src[:, t, :], mv[:, t, 0:1], rstd[:, t:t + 1],
                                  ALU.subtract, ALU.mult).then_inc(v_ln, 1)

        def ln_scalar(act, n):
            act.wait_ge(v_ln, n * LN_STEPS + 2 * NT + 1)
            act.activation(sd[:, :], var[:, :], ACT.Sqrt).then_inc(a_sd, 1)

        LN_BANKS = [bank[2], bank[3], bank[4], bank[5]]

        def ln_tensor(pe, n):
            for half in range(NH):
                for kt in range(KT):
                    b = LN_BANKS[half * KT + kt]
                    for j in range(4):
                        t = half * 4 + j
                        pe.wait_ge(v_ln, n * LN_STEPS + LN_STEPS - NT + t + 1)
                        mm = pe.transpose(b[:, j * P:j * P + P], h_row[:, t, kt * P:kt * P + P], ident[:, :])
                    mm.then_inc(t_ln, 1)

        def ln_high(act, n):
            for i in range(4):
                act.wait_ge(t_ln, 4 * n + i + 1)
                half, kt = i // KT, i % KT
                act.copy(hT_hi[:, kt, half * HALF:(half + 1) * HALF], LN_BANKS[i][:, :]).then_inc(a_ln, 1)

        def ln_low(dve, n):
            for i in range(4):
                dve.wait_ge(a_ln, 4 * n + i + 1)
                half, kt = i // KT, i % KT
                sl = slice(half * HALF, (half + 1) * HALF)
                dve.tensor_tensor(hT_lo[:, kt, sl], LN_BANKS[i][:, :], hT_hi[:, kt, sl], ALU.subtract).then_inc(v_lnlo, 1)

        @block.tensor
        def _(pe):
            def mm3(o, l_hi, l_lo, r_hi, r_lo, start, stop, share=False):
                pe.matmul(o, l_lo, r_hi, start=start, stop=False, skip_group_check=share)
                pe.matmul(o, l_hi, r_lo, start=False, stop=False, skip_group_check=share)
                return pe.matmul(o, l_hi, r_hi, start=False, stop=stop, skip_group_check=share)

            pe.wait_ge(p_const, 3)
            pe.wait_ge(d_b, 16 * 3)
            pe.transpose(bJ[0][:, 0:3 * H], b_rows[:, :], ident[0:3 * H, 0:3 * H]).then_inc(t_b, 1)
            pe.wait_ge(d_r, 32)
            for kt in range(KT):
                mm = pe.transpose(bJ[1][:, kt * NE:(kt + 1) * NE], rw_rows[:, kt * P:(kt + 1) * P], ident[0:NE, 0:NE])
            mm.then_inc(t_rw, 1)
            ln_tensor(pe, 0)
            pe.wait_ge(v_b, 1)
            pe.wait_ge(v_rw, 1)

            def proj_tile(pl, tile, number, pos, final=False):
                kind, m, hp, n = tile
                o = bJ[pos % 2]
                if pl is not None:
                    which, value = pl.freed(pos)
                    wait(pe, {"qk": v_qk, "v": v_v, "w": v_w}[which], value)
                elif pos >= 2:
                    wait(pe, v_qk, pos - 1)
                if kind in ("qk", "next"):
                    c = H0 if kind == "next" else H1
                    if n == 0 and m == Q:
                        wait(pe, p_wl, 1 if pl is None else pl.weights(c, 1 if kind == "next" else 0))
                    for kt in range(KT):
                        j = KT * m + kt
                        mm = mm3(o[:, :], w_hi[c][:, j, :], w_lo[c][:, j, :],
                                 hT_hi[:, kt, n * HALF:(n + 1) * HALF], hT_lo[:, kt, n * HALF:(n + 1) * HALF],
                                 kt == 0, kt == KT - 1)
                elif kind == "v":
                    if n == 0:
                        wait(pe, p_wl, pl.weights(VC, 0))
                    for i in range(2):
                        t = 2 * n + i
                        for kt in range(KT):
                            mm = mm3(o[:, i * D:(i + 1) * D], hT_hi[:, kt, t * P:(t + 1) * P], hT_lo[:, kt, t * P:(t + 1) * P],
                                     w_hi[VC][:, KT * kt:KT * kt + 2, :].rearrange("p a b -> p (a b)"),
                                     w_lo[VC][:, KT * kt:KT * kt + 2, :].rearrange("p a b -> p (a b)"),
                                     kt == 0, kt == KT - 1)
                else:
                    if n == 0:
                        wait(pe, p_wl, pl.weights(WC, 0) if final else (pl.g - 1) * 4 + 3 + 4)
                    wait(pe, v_o, pl.pair(PAIRS if final else 0) - B + n + 1)
                    for i in range(2):
                        t = 2 * n + i
                        for hh in range(2):
                            mm = mm3(o[:, i * D:(i + 1) * D], oT_hi[:, hh, t * P:(t + 1) * P], oT_lo[:, hh, t * P:(t + 1) * P],
                                     w_hi[WC][:, 2 * hh:2 * hh + 2, :].rearrange("p a b -> p (a b)"),
                                     w_lo[WC][:, 2 * hh:2 * hh + 2, :].rearrange("p a b -> p (a b)"),
                                     hh == 0, hh == 1)
                mm.then_inc(t_j, 1)

            def scores(pl, i):
                p = pl.pair(i)
                wait(pe, a_exp, p - 1 if not (pl.first and i < 2) else 0)
                hp, b = i // B, i % B
                if b in (0, 2):
                    wait(pe, v_qk, pl.g * 8 + 4 * hp + (2 if b == 0 else 4))
                for qt in range(2):
                    qs = slice(b * S + qt * P, b * S + qt * P + P)
                    ks = slice(b * S, b * S + S)
                    mm = mm3(bS[i % 2][:, qt * S:(qt + 1) * S], qk_hi[:, hp, Q, qs], qk_lo[:, hp, Q, qs],
                             qk_hi[:, hp, K, ks], qk_lo[:, hp, K, ks], True, True)
                mm.then_inc(t_sc, 1)

            def turn(pl, i):
                p = pl.pair(i)
                wait(pe, v_p, p + 1)
                wait(pe, v_pT, p - 1 if not (pl.first and 0 <= i < 2) else 0)
                for kt in range(2):
                    for qt in range(2):
                        mm = pe.transpose(bP[i % 2][:, kt * S + qt * P:kt * S + qt * P + P],
                                          prob[:, i % 4, qt, kt * P:kt * P + P], ident[:, :])
                mm.then_inc(t_pT, 1)

            def attend(pl, i):
                p = pl.pair(i)
                wait(pe, v_pT, p + 1)
                wait(pe, v_o, p - 1 if not (pl.first and 0 <= i < 2) else 0)
                hp, b = (i % PAIRS) // B, i % B
                if 0 <= i < B:
                    wait(pe, v_v, pl.v_count(b))
                for kt in range(2):
                    mm = mm3(bO[i % 2][:, 0:S], v_hi[:, 2 * b + kt, hp, :], v_lo[:, 2 * b + kt, hp, :],
                             pT_hi[:, i % 2, kt, :], pT_lo[:, i % 2, kt, :], kt == 0, kt == 1)
                mm.then_inc(t_o, 1)

            pe.wait_ge(v_lnlo, 4)
            for pos, t in enumerate(PRO_TILES):
                proj_tile(None, t, pos, pos)

            def body(pl):
                for i in range(PAIRS + (DRAIN + 1 if pl.last else 0)):
                    if i < PAIRS:
                        scores(pl, i)
                    for tile in pl.of_slot(i, 0):
                        proj_tile(pl, *tile)
                    if not (pl.first and i < TURN) and i < PAIRS + TURN:
                        turn(pl, i - TURN)
                    if not (pl.first and i < ATTEND) and i < PAIRS + ATTEND:
                        attend(pl, i - ATTEND)
                    for tile in pl.of_slot(i, 1):
                        proj_tile(pl, *tile)

            over_groups(pe, body)

            pe.wait_ge(d_cw, 16)
            for e in range(NROUTE):
                if e == 2:
                    pe.wait_ge(v_v, 4 * G)
                for kt in range(KT):
                    for ft in range(KT):
                        mm = pe.transpose(bank[e][:, kt * D + ft * P:kt * D + ft * P + P],
                                          cw[:, e, ft, kt * P:kt * P + P], ident[:, :])
                mm.then_inc(t_c, 1)
            pe.wait_ge(v_c, NROUTE)
            ln_tensor(pe, 1)
            pe.wait_ge(v_lnlo, 8)

            for yb in Y_BANKS:
                pe.matmul(yb[:, :], zeros[0:1, 0:P], zeros[0:1, :], start=True, stop=True)

            def pre(e, s):
                half, ft = s // KT, s % KT
                wait(pe, v_t, e * 4 + s - 3 if not (isinstance(e, int) and e == 0) else 0)
                for kt in range(KT):
                    mm = mm3(Z_BANKS[s][:, :], cT_hi[:, e, kt, ft * P:ft * P + P], cT_lo[:, e, kt, ft * P:ft * P + P],
                             hT_hi[:, kt, half * HALF:(half + 1) * HALF], hT_lo[:, kt, half * HALF:(half + 1) * HALF],
                             kt == 0, kt == KT - 1)
                mm.then_inc(t_z, 1)

            def post(e, s):
                half, ft = s // KT, s % KT
                wait(pe, v_g, e * 4 + s + 1)
                for j in range(4):
                    yb = Y_BANKS[half * 2 + j // 2][:, (j % 2) * D:(j % 2) * D + D]
                    mm = mm3(yb, gu_hi[:, s % 2, j * P:(j + 1) * P], gu_lo[:, s % 2, j * P:(j + 1) * P],
                             cT_hi[:, e, ft, :], cT_lo[:, e, ft, :], False, e == NROUTE - 1 and ft == KT - 1, True)
                mm.then_inc(t_y, 1)

            for e in range(NROUTE):
                for s in range(4):
                    pre(e, s)
                    if (e, s) >= (0, 2):
                        post(e if s >= 2 else e - 1, (s - 2) % 4)
            for s in (2, 3):
                post(NROUTE - 1, s)

            ln_tensor(pe, 2)
            pe.wait_ge(a_hf, 2)
            pe.wait_ge(v_hf, 2)
            for t in range(NT):
                for kt in range(KT):
                    mm = pe.matmul(bank[6][:, t * NE:(t + 1) * NE], hT_f[:, kt, t * P:(t + 1) * P], rwT[:, kt, :],
                                   start=kt == 0, stop=kt == KT - 1)
            mm.then_inc(t_r, 1)

            def gate_up(n, e, xT_of):
                for kt in range(KT):
                    w = sgu[:, kt, :, :].rearrange("p a i -> p (a i)") if e is None else \
                        moe_w[:, :, :].rearrange("p e m -> p (e m)")[:, bass.ds(e * EW + kt * 2 * FI, 2 * FI)]
                    mm = pe.matmul(bG[n % 2][:, 0:2 * FI], xT_of(kt), w, start=kt == 0, stop=kt == KT - 1)
                mm.then_inc(t_gu, 1)

            def hidden_turn(n):
                pe.transpose(bH[n % 2][:, 0:SLOTS], hid[:, n % 2, :], ident[:, :]).then_inc(t_hT, 1)

            def down(n, e):
                w = sdn[:, :] if e is None else \
                    moe_w[:, :, :].rearrange("p e m -> p (e m)")[:, bass.ds(e * EW + 2 * D, D)]
                pe.matmul(bY[n % 2][:, 0:D], hidT[:, n % 2, :], w, start=True, stop=True).then_inc(t_dn, 1)

            pe.wait_ge(v_r, R_MEMBER)
            pe.wait_ge(p_const, 11 + PACK)
            rank = bank[0]
            pe.matmul(rank[:, 0:NT * NE], before[:, :], member[:, :, :].rearrange("p t e -> p (t e)"),
                      start=True, stop=False, skip_group_check=True)
            for t in range(NT - 1):
                pe.matmul(rank[:, (t + 1) * NE:NT * NE].rearrange("p (t e) -> p t e", e=NE), ones[:, :],
                          member[:, t:t + 1, :].to_broadcast([P, NT - 1 - t, NE]),
                          start=False, stop=t == NT - 2, skip_group_check=True)
            for t in range(NT):
                mm = pe.matmul(bank[1][0:NE, 0:1], member[:, t, :], ones[:, 0:1], start=t == 0, stop=t == NT - 1)
            mm.then_inc(t_r, 1)
            pe.wait_ge(v_r, R_TILES)
            pe.matmul(bank[6][0:NE, 0:1], upto[:, :], tiles_b[:, 0:1], start=True, stop=True)
            pe.matmul(bank[7][:, 0:NE], tiles_b[:, :], before[0:NE, 0:NE], start=True, stop=True).then_inc(t_r, 1)
            pe.wait_ge(v_r, R_PAST)
            pe.matmul(bank[1][0:1, 0:TILES], ones[0:NE, 0:1], past[:, :], start=True, stop=True).then_inc(t_r, 1)

            for n in range(SH + 2):
                if n < SH:
                    if n == 0:
                        pe.wait_ge(d_sw, 48)
                    wait(pe, v_h, n - 1)
                    gate_up(n, None, lambda kt: hT_f[:, kt, n * P:(n + 1) * P])
                if 1 <= n <= SH:
                    pe.wait_ge(v_h, n)
                    wait(pe, a_hT, n - 2)
                    hidden_turn(n - 1)
                if n >= 2:
                    pe.wait_ge(a_hT, n - 1)
                    if n == 2:
                        pe.wait_ge(v_r, R_EXPERT)
                    wait(pe, v_sh, n - 3)
                    down(n - 2, None)

            pe.wait_ge(v_r, R_HOT)
            for c in range(CH):
                mm = pe.matmul(bank[0][:, 0:TILES], in_slot[:, c, :], in_tile[:, c, :], start=c == 0, stop=c == CH - 1)
            mm.then_inc(t_r, 1)

            def experts(word):
                apart(pe)
                v = pe.value_load(packed[0:1, bass.ds(word, 1)], min_val=0, max_val=NE ** PACK - 1)
                return [pe.snap((v // (NE ** i)) % NE) for i in range(PACK)]

            def row_turn(j, u, it):
                wait(pe, d_g[u], it * 16 + 16)
                wait(pe, v_x, j - 1)
                for kt in range(KT):
                    mm = pe.transpose(bX[u % 2][:, kt * SLOTS:(kt + 1) * SLOTS], xg[:, u, kt * P:(kt + 1) * P], ident[:, :])
                mm.then_inc(t_x, 1)

            def trip(it, first, last):
                words = STEPS // PACK
                es = [0] * PACK if first else experts(it * words - 1)
                for u in range(STEPS + (2 if last else 0)):
                    j = it * STEPS + u
                    if u < STEPS and u % PACK == 0:
                        es += experts(it * words + u // PACK)
                    if u < STEPS - 1:
                        row_turn(j + 1, u + 1, it)
                    elif u == STEPS - 1 and not last:
                        row_turn(j + 1, 0, it + 1)
                    if u < STEPS:
                        wait(pe, v_x, j + 1)
                        wait(pe, v_h, j - 1 + SH)
                        gate_up(u, es[PACK + u], lambda kt: xT[:, u % 2, kt * SLOTS:(kt + 1) * SLOTS])
                    if not (first and u < 1) and u < STEPS + 1:
                        wait(pe, v_h, j + SH)
                        wait(pe, a_hT, j - 2 + SH)
                        hidden_turn(u - 1 + STEPS)
                    if not (first and u < 2):
                        wait(pe, a_hT, j - 1 + SH)
                        wait(pe, a_y, 0 if first and u < 4 else j - 3)
                        down(u - 2 + STEPS, es[PACK + u - 2])

            pe.wait_ge(v_r, R_SOURCE)
            pe.wait_ge(v_sh, SH)
            pe.wait_ge(d_m, 16 * 20)
            row_turn(0, 0, 0)
            trip(0, True, False)
            with pe.Fori(1, TRIPS - 1) as it:
                trip(it, False, False)
            trip(TRIPS - 1, False, True)

        @block.scalar
        def _(act):
            for n, nm in enumerate(("bq", "bk", "bv")):
                act.dma_start(b_rows[n * H:(n + 1) * H, :], a[nm].rearrange("(h d) -> h d", d=HD)).then_inc(d_b, 16)
            act.dma_start(bo_b[:, :], a["bo"].unsqueeze(0).to_broadcast([P, D])).then_inc(d_bo, 16)
            act.dma_start(ids[:, :], a["tok"].rearrange("b s -> (b s)").unsqueeze(0).to_broadcast([P, T])).then_inc(d_ids, 16)
            act.dma_start(rw_rows[:, :], a["router_w"]).then_inc(d_r, 16)
            act.dma_start(rb[:, :], a["bias"].unsqueeze(0).to_broadcast([P, NE])).then_inc(d_r, 16)
            act.dma_start(sgu[:, :, 0, :], a["sw_gate"].rearrange("(t p) i -> p t i", p=P)).then_inc(d_sw, 16)
            act.dma_start(sgu[:, :, 1, :], a["sw_up"].rearrange("(t p) i -> p t i", p=P)).then_inc(d_sw, 16)
            act.dma_start(sdn[:, :], a["sw_down"]).then_inc(d_sw, 16)
            act.dma_start(cw[:, :, :, :], a["ctx"].rearrange("e (t p) d -> p e t d", p=P)).then_inc(d_cw, 16)

            def weights_high(c, count):
                wait(act, p_wm, count)
                act.copy(w_hi[c][:, :, :], st_c[c][:, :, :]).then_inc(a_wh, 1)

            ln_scalar(act, 0)
            for n, c in enumerate((H0, VC, H1)):
                weights_high(c, n + 1)
            ln_high(act, 0)
            act.wait_ge(v_b, 1)

            def proj_high(pl, t, number, pos):
                kind, m, hp, n = t
                src = bJ[pos % 2]
                if kind == "w":
                    return
                wait(act, t_j, number + 1)
                if kind == "v":
                    if n == 0:
                        wait(act, t_o, pl.pair(0))
                    act.copy(v_hi[:, 2 * n:2 * n + 2, :, :].rearrange("p t h d -> p (t h d)"), src[:, :]).then_inc(a_v, 1)
                    return
                g_h = 0 if pl is None else (pl.g + (1 if kind == "next" else 0)) * 2 + hp
                if n == 0 and pl is not None:
                    wait(act, t_sc, pl.pair(B) if kind == "next" else pl.pair(0))
                apart(act)
                act.activation(qk_hi[:, hp, m, n * HALF:(n + 1) * HALF], src[:, :], ACT.Identity,
                               bias=b_col[:, bass.ds(g_h + m * H, 1)]).then_inc(a_qk, 1)

            for pos, t in enumerate(PRO_TILES):
                proj_high(None, t, pos, pos)

            def body(pl):
                for i in range(PAIRS + (DRAIN + 1 if pl.last else 0)):
                    if i < PAIRS:
                        p = pl.pair(i)
                        wait(act, v_max, p + 1)
                        wait(act, t_pT, p - 3 if not (pl.first and i < 4) else 0)
                        for qt in range(2):
                            ex = act.activation(prob[:, i % 4, qt, :], bS[i % 2][:, qt * S:(qt + 1) * S], ACT.Exp,
                                                bias=nmax[:, i % 2, qt:qt + 1], scale=SCALE,
                                                accum_out=rsum[:, i % 2, qt:qt + 1])
                        ex.then_inc(a_exp, 1)
                    for t, number, pos, final in pl.of_slot(i, 0):
                        proj_high(pl, t, number, pos)
                    if not (pl.first and i < TURN) and i < PAIRS + TURN:
                        j = i - TURN
                        wait(act, t_pT, pl.pair(j) + 1)
                        wait(act, t_o, pl.pair(j) - 1 if not (pl.first and j < 2) else 0)
                        act.copy(pT_hi[:, j % 2, :, :].rearrange("p a b -> p (a b)"), bP[j % 2][:, :]).then_inc(a_pT, 1)
                    if not (pl.first and i < ATTEND) and i < PAIRS + ATTEND:
                        j = i - ATTEND
                        hp, b = (j % PAIRS) // B, j % B
                        wait(act, t_o, pl.pair(j) + 1)
                        if hp == 0 and not pl.first and 0 <= j < PAIRS:
                            wait(act, t_j, pl.w_tile_number(b) + 1)
                        head = pl.g * 2 + (hp if j >= 0 else hp - 2) + 2 * H
                        apart(act)
                        act.activation(oT_hi[:, hp, b * S:(b + 1) * S], bO[j % 2][:, 0:S], ACT.Identity,
                                       bias=b_col[:, bass.ds(head, 1)]).then_inc(a_o, 1)
                    for t, number, pos, final in pl.of_slot(i, 1):
                        proj_high(pl, t, number, pos)
                    if i in PREP_SLOTS and not (pl.last and i != 7):
                        c = PREP_SLOTS[i]
                        if c == H0:
                            wait(act, t_j, pl.tiles[0][2])
                        elif c != WC or not pl.first:
                            kind = {VC: "v", H1: "qk", WC: "w"}[c]
                            wait(act, t_j, [tile[2] for tile in pl.tiles if tile[1][0] == kind and tile[0] < PAIRS][-1] + 1)
                        weights_high(c, pl.weights(c, 0 if c == WC else 1))

            over_groups(act, body)

            for e in range(NROUTE):
                act.wait_ge(t_c, e + 1)
                act.copy(cT_hi[:, e, :, :].rearrange("p a b -> p (a b)"), bank[e][:, :]).then_inc(a_c, 1)
            ln_scalar(act, 1)
            ln_high(act, 1)
            for n in range(NROUTE * 4):
                s = n % 4
                act.wait_ge(t_z, n + 1)
                wait(act, v_tm, n - 1)
                act.activation(gact[:, n % 2, :], Z_BANKS[s][:, :], ACT.Silu).then_inc(a_z, 1)
                act.wait_ge(v_tm, n + 1)
                wait(act, t_y, n - 1)
                act.copy(gu_hi[:, n % 2, :], gm[:, n % 2, :]).then_inc(a_g, 1)

            ln_scalar(act, 2)
            act.wait_ge(t_y, NROUTE * 4)
            for i in (0, 2):
                act.wait_ge(t_ln, 8 + i + 1)
                half, kt = i // KT, i % KT
                act.copy(hT_f[:, kt, half * HALF:(half + 1) * HALF], LN_BANKS[i][:, :]).then_inc(a_hf, 1)
            act.wait_ge(t_r, 1)
            act.activation(score[:, :, :].rearrange("p t e -> p (t e)"), bank[6][:, 0:NT * NE], ACT.Sigmoid).then_inc(a_r, 1)

            def silu(n, count):
                wait(act, t_gu, count + 1)
                wait(act, v_h, count - 1)
                act.activation(sg[:, n % 2, :], bG[n % 2][:, 0:FI], ACT.Silu).then_inc(a_s, 1)

            def hidden_copy(n, count):
                wait(act, t_hT, count + 1)
                wait(act, t_dn, count - 1)
                act.copy(hidT[:, n % 2, :], bH[n % 2][:, 0:SLOTS]).then_inc(a_hT, 1)

            for n in range(SH + 1):
                if n < SH:
                    silu(n, n)
                if n >= 1:
                    hidden_copy(n - 1, n - 1)

            def trip(it, first, last):
                for u in range(STEPS + (2 if last else 0)):
                    j = it * STEPS + u
                    if u < STEPS:
                        silu(u, j + SH)
                    if not (first and u < 1) and u < STEPS + 1:
                        hidden_copy(u - 1 + STEPS, j - 1 + SH)
                    if not (first and u < 2):
                        wait(act, t_dn, j - 1 + SH)
                        s = (u - 2) % STEPS
                        if not first:
                            wait(act, d_y[s], (it + 1 if u >= 2 else it) * 16)
                        act.copy(ysb[:, s, :], bY[u % 2][:, 0:D]).then_inc(a_y, 1)

            trip(0, True, False)
            with act.Fori(1, TRIPS - 1) as it:
                trip(it, False, False)
            trip(TRIPS - 1, False, True)

        @block.vector
        def _(dve):
            dve.wait_ge(d_x, 16)
            ln_vector(dve, 0, x_in)
            dve.wait_ge(t_b, 1)
            dve.tensor_copy(b_col[:, :], bJ[0][:, 0:3 * H]).then_inc(v_b, 1)
            dve.wait_ge(t_rw, 1)
            dve.tensor_copy(rwT[:, :, :].rearrange("p k e -> p (k e)"), bJ[1][:, 0:KT * NE]).then_inc(v_rw, 1)
            ln_low(dve, 0)
            dve.wait_ge(v_b, 1)

            def proj_low(pl, t, number, pos, final=False):
                kind, m, hp, n = t
                src = bJ[pos % 2]
                if kind == "w":
                    wait(dve, t_j, number + 1)
                    dst = x_acc[:, 2 * n:2 * n + 2, :]
                    if n == 0:
                        wait(dve, v_w, pl.w_done_count(0, final) - 1)
                    dve.tensor_tensor(dst, src[:, :].rearrange("p (a b) -> p a b", a=2), dst, ALU.add).then_inc(v_w, 1)
                elif kind == "v":
                    wait(dve, a_v, pl.v_count(n))
                    sl = v_lo[:, 2 * n:2 * n + 2, :, :].rearrange("p t h d -> p (t h d)")
                    hi = v_hi[:, 2 * n:2 * n + 2, :, :].rearrange("p t h d -> p (t h d)")
                    dve.tensor_tensor(sl, src[:, :], hi, ALU.subtract).then_inc(v_v, 1)
                else:
                    wait(dve, a_qk, pos + 1 if pl is None else pl.qk_count(t))
                    g_h = 0 if pl is None else (pl.g + (1 if kind == "next" else 0)) * 2 + hp
                    dve.scalar_tensor_tensor(out=qk_lo[:, hp, m, n * HALF:(n + 1) * HALF], in0=src[:, :],
                                             scalar=b_col[:, bass.ds(g_h + m * H, 1)],
                                             in1=qk_hi[:, hp, m, n * HALF:(n + 1) * HALF],
                                             op0=ALU.add, op1=ALU.subtract).then_inc(v_qk, 1)

            for pos, t in enumerate(PRO_TILES):
                proj_low(None, t, pos, pos)

            def body(pl):
                for i in range(PAIRS + (DRAIN + 2 if pl.last else 0)):
                    if i < PAIRS:
                        p = pl.pair(i)
                        wait(dve, t_sc, p + 1)
                        dve.tensor_reduce(rmax[:, i % 2, :], bS[i % 2][:, :].rearrange("p (q k) -> p q k", q=2),
                                          AX.X, ALU.max).then_inc(v_m1, 1)
                        wait(dve, v_m1, p + 1)
                        wait(dve, a_exp, p - 1 if not (pl.first and i < 2) else 0)
                        dve.tensor_scalar(nmax[:, i % 2, :], rmax[:, i % 2, :], -SCALE, None, ALU.mult).then_inc(v_max, 1)
                    for tile in pl.of_slot(i - 1, 1):
                        proj_low(pl, *tile)
                    if not (pl.first and i < 1) and i < PAIRS + 1:
                        j = i - 1
                        wait(dve, a_exp, pl.pair(j) + 1)
                        dve.reciprocal(rinv[:, j % 2, :], rsum[:, j % 2, :]).then_inc(v_ri, 1)
                        wait(dve, v_ri, pl.pair(j) + 1)
                        for qt in range(2):
                            sc = dve.tensor_scalar(prob[:, j % 4, qt, :], prob[:, j % 4, qt, :],
                                                   rinv[:, j % 2, qt:qt + 1], None, ALU.mult)
                        sc.then_inc(v_p, 1)
                    for tile in pl.of_slot(i, 0):
                        proj_low(pl, *tile)
                    if not (pl.first and i < TURN) and i < PAIRS + TURN:
                        j = i - TURN
                        wait(dve, a_pT, pl.pair(j) + 1)
                        dve.tensor_tensor(pT_lo[:, j % 2, :, :].rearrange("p a b -> p (a b)"), bP[j % 2][:, :],
                                          pT_hi[:, j % 2, :, :].rearrange("p a b -> p (a b)"), ALU.subtract).then_inc(v_pT, 1)
                    if not (pl.first and i < ATTEND) and i < PAIRS + ATTEND:
                        j = i - ATTEND
                        hp, b = (j % PAIRS) // B, j % B
                        wait(dve, a_o, pl.pair(j) + 1)
                        head = pl.g * 2 + (hp if j >= 0 else hp - 2) + 2 * H
                        dve.scalar_tensor_tensor(out=oT_lo[:, hp, b * S:(b + 1) * S], in0=bO[j % 2][:, 0:S],
                                                 scalar=b_col[:, bass.ds(head, 1)], in1=oT_hi[:, hp, b * S:(b + 1) * S],
                                                 op0=ALU.add, op1=ALU.subtract).then_inc(v_o, 1)

            over_groups(dve, body)
            dve.wait_ge(v_w, 4 * G + 1)
            ln_vector(dve, 1, x_acc)
            for e in range(NROUTE):
                dve.wait_ge(a_c, e + 1)
                dve.tensor_tensor(cT_lo[:, e, :, :].rearrange("p a b -> p (a b)"), bank[e][:, :],
                                  cT_hi[:, e, :, :].rearrange("p a b -> p (a b)"), ALU.subtract).then_inc(v_c, 1)
            ln_low(dve, 1)
            dve.wait_ge(p_mask, NROUTE + 2)
            for n in range(NROUTE * 4):
                e, s = n // 4, n % 4
                half = s // KT
                dve.wait_ge(a_z, n + 1)
                wait(dve, a_g, n - 1)
                dve.tensor_tensor(gm[:, n % 2, :], Z_BANKS[s][:, :], gact[:, n % 2, :], ALU.mult).then_inc(v_t, 1)
                dve.wait_ge(v_t, n + 1)
                dve.tensor_tensor(gm[:, n % 2, :], gm[:, n % 2, :], mask[:, e, half * HALF:(half + 1) * HALF], ALU.mult).then_inc(v_tm, 1)
                dve.wait_ge(a_g, n + 1)
                dve.tensor_tensor(gu_lo[:, n % 2, :], gm[:, n % 2, :], gu_hi[:, n % 2, :], ALU.subtract).then_inc(v_g, 1)
            for j in range(4):
                dve.wait_ge(t_y, NROUTE * 4)
                dst = x_acc[:, 2 * j:2 * j + 2, :]
                dve.tensor_tensor(dst, Y_BANKS[j][:, :].rearrange("p (a b) -> p a b", a=2), dst, ALU.add).then_inc(v_y, 1)

            dve.wait_ge(v_y, 4)
            ln_vector(dve, 2, x_acc)
            dve.wait_ge(t_y, NROUTE * 4)
            for i in (1, 3):
                dve.wait_ge(t_ln, 8 + i + 1)
                half, kt = i // KT, i % KT
                dve.tensor_copy(hT_f[:, kt, half * HALF:(half + 1) * HALF], LN_BANKS[i][:, :]).then_inc(v_hf, 1)

            done = [0]

            def own(ins):
                done[0] += 1
                ins.then_inc(v_own, 1)
                dve.wait_ge(v_own, done[0])

            dve.wait_ge(a_r, 1)
            dve.wait_ge(d_r, 32)
            own(dve.tensor_tensor(sel[:, :, :], score[:, :, :], rb[:, :].unsqueeze(1).to_broadcast([P, NT, NE]), ALU.add))
            for t in range(NT):
                ins = dve.max(top[:, t, :], sel[:, t, :])
            own(ins)
            for t in range(NT):
                ins = dve.max_index(topi[:, t, :], top[:, t, :], sel[:, t, :])
            own(ins)
            own(dve.tensor_copy(chosen[:, :, :], topi[:, :, 0:TOPK].rearrange("p t k -> p k t")))
            dve.wait_ge(p_const, 11 + PACK)
            own(dve.tensor_tensor(hot[:, :, :, :].rearrange("p k t e -> p (k t) e"),
                                  chosen[:, :, :].rearrange("p k t -> p (k t)").unsqueeze(2).to_broadcast([P, CH, NE]),
                                  iota_e[:, :].unsqueeze(1).to_broadcast([P, CH, NE]), ALU.is_equal))
            with nc.allow_low_precision(reason="counts of at most 1 in bfloat16"):
                dve.tensor_reduce(member[:, :, :], hot[:, :, :, :].rearrange("p k t e -> p t e k"), AX.X, ALU.add).then_inc(v_r, 1)
            dve.wait_ge(t_r, 2)
            own(dve.tensor_copy(count[:, :], bank[1][0:NE, 0:1]))
            own(dve.tensor_scalar(over[:, :], iota_f[:, :], count[:, 0:1], None, ALU.is_lt))
            own(dve.tensor_reduce(tiles_e[:, :], over[:, :], AX.X, ALU.add))
            dve.tensor_scalar(tiles_b[:, :], ones[0:NE, :], tiles_e[:, 0:1], None, ALU.mult).then_inc(v_r, 1)
            dve.wait_ge(t_r, 3)
            own(dve.tensor_copy(end_e[:, :], bank[6][0:NE, 0:1]))
            dve.tensor_scalar(past[:, :], iota_t[0:NE, :], end_e[:, 0:1], None, ALU.is_ge).then_inc(v_r, 1)
            own(dve.tensor_scalar(base[:, :], bank[7][:, 0:NE], float(SLOTS), None, ALU.mult))
            own(dve.tensor_tensor(place[:, :, :], bank[0][:, 0:NT * NE].rearrange("p (t e) -> p t e", e=NE),
                                  base[:, :].unsqueeze(1).to_broadcast([P, NT, NE]), ALU.add))
            dve.wait_ge(t_r, 4)
            own(dve.tensor_scalar(expert[:, :], bank[1][0:1, 0:TILES], float(NE - 1), None, ALU.min))
            own(dve.tensor_tensor(expert[:, :].rearrange("p (w i) -> p w i", i=PACK), expert[:, :].rearrange("p (w i) -> p w i", i=PACK),
                                  powers[:, :, :], ALU.mult))
            with nc.allow_low_precision(reason="integers under 2 ** 20"):
                dve.tensor_reduce(packed[:, :], expert[:, :].rearrange("p (w i) -> p w i", i=PACK), AX.X, ALU.add).then_inc(v_r, 1)
            own(dve.tensor_tensor(work[:, :, :, :], hot[:, :, :, :],
                                  place[:, :, :].unsqueeze(1).to_broadcast([P, TOPK, NT, NE]), ALU.mult))
            own(dve.tensor_reduce(slot_f[:, :, :], work[:, :, :, :], AX.X, ALU.add))
            own(dve.tensor_copy(slot_i[:, :, :], slot_f[:, :, :]))
            flat = slot_i[:, :, :].rearrange("p k t -> p (k t)")
            dve.tensor_scalar(part_i[:, 0, :], flat, 7, None, ALU.logical_shift_right)
            own(dve.tensor_scalar(part_i[:, 1, :], flat, SLOTS - 1, None, ALU.bitwise_and))
            own(dve.tensor_copy(part_h[:, :, :], part_i[:, :, :]))
            dve.tensor_tensor(in_slot[:, :, :], part_h[:, 1, :].unsqueeze(2).to_broadcast([P, CH, SLOTS]),
                              iota_s[:, :].unsqueeze(1).to_broadcast([P, CH, SLOTS]), ALU.is_equal)
            own(dve.tensor_tensor(in_tile[:, :, :], part_h[:, 0, :].unsqueeze(2).to_broadcast([P, CH, TILES]),
                                  iota_t[:, :].unsqueeze(1).to_broadcast([P, CH, TILES]), ALU.is_equal))
            dve.tensor_tensor(in_tile[:, :, :], in_tile[:, :, :],
                              tok_id[:, :, :].rearrange("p k t -> p (k t)").unsqueeze(2).to_broadcast([P, CH, TILES]),
                              ALU.mult).then_inc(v_r, 1)
            own(dve.tensor_tensor(work[:, :, :, :], hot[:, :, :, :],
                                  score[:, :, :].unsqueeze(1).to_broadcast([P, TOPK, NT, NE]), ALU.mult))
            own(dve.tensor_reduce(gain[:, :, :], work[:, :, :, :], AX.X, ALU.add))
            own(dve.tensor_reduce(gsum[:, :], gain[:, :, :].rearrange("p k t -> p t k"), AX.X, ALU.add))
            own(dve.tensor_scalar(gsum[:, :], gsum[:, :], 1e-20, None, ALU.add))
            own(dve.reciprocal(gsum[:, :], gsum[:, :]))
            own(dve.tensor_tensor(gain[:, :, :], gain[:, :, :], gsum[:, :].unsqueeze(1).to_broadcast([P, TOPK, NT]), ALU.mult))

            def product(n, count):
                wait(dve, a_s, count + 1)
                wait(dve, t_hT, count - 1)
                dve.tensor_tensor(hid[:, n % 2, :], bG[n % 2][:, FI:2 * FI], sg[:, n % 2, :], ALU.mult).then_inc(v_h, 1)

            for n in range(SH + 2):
                if n < SH:
                    product(n, n)
                if n >= 2:
                    t = n - 2
                    dve.wait_ge(t_dn, t + 1)
                    dve.tensor_tensor(x_acc[:, t, :], bY[t % 2][:, 0:D], x_acc[:, t, :], ALU.add).then_inc(v_sh, 1)
            dve.wait_ge(t_r, 5)
            dve.tensor_copy(source[:, :], bank[0][:, 0:TILES]).then_inc(v_r, 1)

            def row_copy(j, u):
                wait(dve, t_x, j + 1)
                wait(dve, t_gu, j - 1 + SH)
                dve.tensor_copy(xT[:, u % 2, :], bX[u % 2][:, 0:D]).then_inc(v_x, 1)

            def trip(it, last):
                for u in range(STEPS):
                    j = it * STEPS + u
                    if u < STEPS - 1 or not last:
                        row_copy(j + 1, u + 1)
                    product(u, j + SH)

            row_copy(0, 0)
            with dve.Fori(0, TRIPS - 1) as it:
                trip(it, False)
            trip(TRIPS - 1, True)

            for k in range(TOPK):
                for t in range(NT):
                    dve.wait_ge(d_yg[t], k * 16 + 16)
                    if k == 0:
                        dve.wait_ge(v_sh, t + 1)
                    else:
                        dve.wait_ge(v_cmb, (k - 1) * NT + t + 1)
                    dve.scalar_tensor_tensor(out=x_acc[:, t, :], in0=yg[:, t, :], scalar=gain[:, k, t:t + 1],
                                             in1=x_acc[:, t, :], op0=ALU.mult, op1=ALU.add).then_inc(v_cmb, 1)


_INS = {"x": "x", "tok": "itok_BxS_13_99985", "ctx": "ctx_2048",
        **{n: f"L0_attn_{n}" for n in ("wq_codes", "wq_scales", "bq", "wk_codes", "wk_scales", "bk",
                                       "wv_codes", "wv_scales", "bv", "wo_codes", "wo_scales", "bo")},
        **{n: f"L0_ffn_{n}" for n in ("router_w", "bias", "w_gate", "w_up", "w_down",
                                      "sw_gate", "sw_up", "sw_down")}}


def kernel(**inputs):
    import numpy as _np
    import concourse.bacc as _bacc
    from concourse import mybir as _mybir
    from concourse.bass_utils import run_bass_kernel_spmd as _run

    nc = _bacc.Bacc("TRN2", target_bir_lowering=False, num_devices=1)
    arrays, args = {}, {}
    for short, name in _INS.items():
        arr = _np.ascontiguousarray(inputs[name])
        arrays[f"in_{short}"] = arr
        args[short] = nc.dram_tensor(f"in_{short}", arr.shape, _mybir.dt.from_np(arr.dtype), kind="ExternalInput").ap()
    out = nc.dram_tensor("out_0", (B, S, D), _mybir.dt.float32, kind="ExternalOutput").ap()
    decoder_layer(nc, args, out)
    r = _run(nc, [arrays], core_ids=[0])
    return r.results[0]["out_0"]
```

```python
from contextlib import ExitStack

import concourse.bass as bass
from concourse import mybir

F32 = mybir.dt.float32
F32R = mybir.dt.float32r
F16 = mybir.dt.float16
BF16 = mybir.dt.bfloat16
U32 = mybir.dt.uint32
I32 = mybir.dt.int32
ALU = mybir.AluOpType
ACT = mybir.ActivationFunctionType
AX = mybir.AxisListType

P = 128
T = 1024
D = 256
NT = T // P
KT = D // P
B, S = 4, 256
H, HD = 16, 128
QB = 32
G = H // 2
PAIRS = 2 * B
SCALE = float(HD) ** -0.5
EPS = 1e-5
NROUTE = 4
VOCAB = 12500
HALF = 512
NE, TOPK, FI = 32, 4, 128

SLOTS = 128
TILES = (T * TOPK + NE * (SLOTS - 1)) // SLOTS + 1
STEPS = 8
TRIPS = TILES // STEPS
LAST = 3
PART = 4
assert TRIPS * STEPS == TILES == 64 and STEPS == 2 * PART
CH = TOPK * NT
EW = 3 * D

Q, K, V, W = 0, 1, 2, 3
H0, VC, H1, WC = 0, 1, 2, 3


def wait(eng, sem, value):
    if isinstance(value, int) and value <= 0:
        return
    eng.wait_ge(sem, value)


def apart(eng):
    eng.nop(nofuse=True)


def slot_tiles(first, last):
    s = [[("qk", Q, 1, 0), ("w", W, 0, 0)],
         [("qk", K, 1, 0), ("w", W, 0, 1)],
         [("qk", Q, 1, 1), ("v", V, 0, 0)],
         [("v", V, 0, 1), ("w", W, 0, 2)],
         [("v", V, 0, 2), ("qk", K, 1, 1)],
         [("v", V, 0, 3), ("w", W, 0, 3)],
         [("next", Q, 0, 0), ("next", K, 0, 0)],
         [("next", Q, 0, 1), ("next", K, 0, 1)]]
    def tile(t):
        if first and t[0] == "w":
            return ("ctx", None, 0, t[3])
        return None if last and t[0] == "next" else t
    return [[tile(t) for t in slot] for slot in s]


PREP_SLOTS = {1: H0, 5: VC, 6: H1, 7: WC}
TURN, ATTEND = 2, 3
DRAIN = ATTEND
PRO_TILES = [("next", Q, 0, 0), ("next", K, 0, 0), ("next", Q, 0, 1), ("next", K, 0, 1)]


class Plan:

    def __init__(self, g):
        self.g = g
        self.first = isinstance(g, int) and g == 0
        self.last = isinstance(g, int) and g == G - 1
        self.slots = slot_tiles(self.first, self.last)
        n = 0
        self.tiles = []
        start = 4 + 16 * g
        for i, slot in enumerate(self.slots):
            for place, t in enumerate(slot):
                if t is not None:
                    self.tiles.append((i, t, start + n, n, place))
                    n += 1
        if self.last:
            for b in range(B):
                self.tiles.append((PAIRS + b, ("w", W, 0, b), start + n, n, 1))
                n += 1

    def of_slot(self, i, place):
        if i < 0:
            return [] if self.first else [(("prev", K, 0, 1), None, 1, False)]
        return [(t, number, pos, s >= PAIRS) for s, t, number, pos, at in self.tiles if s == i and at == place]

    def pair(self, i):
        return self.g * PAIRS + i

    def qk_count(self, t):
        kind, m, hp, half = t
        at = {(Q, 0): 0, (K, 0): 1, (Q, 1): 2, (K, 1): 3}[(m, half)] + 1
        if kind == "next":
            return self.g * 8 + 8 + at
        if kind == "prev":
            return self.g * 8 + at
        return self.g * 8 + 4 + at

    def v_count(self, n):
        return self.g * 4 + n + 1

    def w_done_count(self, b, final):
        return (self.g * 4 if final else (self.g - 1) * 4) + b + 2

    def freed(self, pos):
        if pos >= 2:
            t = self.tiles[pos - 2][1]
            final = self.last and self.tiles[pos - 2][0] >= PAIRS
        else:
            t, final = ("prev", (Q, K)[pos], 0, 1), False
        kind, m, hp, n = t
        if kind in ("prev", "qk", "next"):
            return "qk", self.qk_count(t)
        if kind == "v":
            return "v", self.v_count(n)
        if kind == "ctx":
            return "ctx", n + 1
        return "w", self.w_done_count(n, final)

    def w_tile_number(self, b):
        for s, t, number, pos, place in self.tiles:
            if t[0] == "w" and t[3] == b and s < PAIRS:
                return number

    def weights(self, chunk, ahead):
        if ahead == 0 and self.first and chunk != WC:
            return {H0: 1, H1: 2, VC: 3}[chunk]
        base = self.g * 4 + 3 if (ahead or chunk == WC) else (self.g - 1) * 4 + 3
        return base + {H0: 1, VC: 2, H1: 3, WC: 4}[chunk] - (3 if (self.last and chunk == WC and not ahead) else 0)


def over_groups(eng, body):
    body(Plan(0))
    with eng.Fori(1, G - 1) as g:
        body(Plan(g))
    body(Plan(G - 1))


def decoder_layer(nc, a, out):
    ctx = ExitStack()
    with ctx:
        def sb(name, shape, dt=F32):
            return ctx.enter_context(nc.sbuf_tensor(name, shape, dt))

        def sem(name):
            return ctx.enter_context(nc.semaphore(name))

        bank = [ctx.enter_context(nc.psum_tensor(f"bank{n}", [P, HALF], F32)) for n in range(8)]
        bS, bP, bO, bJ = bank[0:2], bank[2:4], bank[4:6], bank[6:8]

        Z_BANKS = bank[2:6]
        ENDS = [bank[0:2], bank[6:8]]

        ident = sb("ident", [P, P])
        yg_at = [nc.sbuf_base]
        x_in = sb("x_in", [P, NT, D])
        h_row = sb("h_row", [P, NT, D])
        x_acc = sb("x_acc", [P, NT, D])
        bo_b = sb("bo_b", [P, D])
        b_rows = sb("b_rows", [3 * H, HD])
        b_col = sb("b_col", [P, 3 * H])
        rw_rows = sb("rw_rows", [NE, D])
        rwT = sb("rwT", [P, KT, NE])
        rb = sb("rb", [P, NE])
        sgu = sb("sgu", [P, KT, 2, FI])
        sdn = sb("sdn", [P, D])
        iota_t = sb("iota_t", [P, TILES], F16)
        iota_f = sb("iota_f", [NE, NT])
        before = sb("before", [P, P], BF16)
        upto = sb("upto", [NE, NE], BF16)
        ones = sb("ones", [P, P], BF16)
        moe_at = nc.sbuf_base
        st_c = [sb(f"st_c{c}", [P, 4, P]) for c in range(4)]
        st_s = [sb(f"st_s{c}", [P, 4, P]) for c in range(4)]
        w_hi = [sb(f"w_hi{c}", [P, 4, P], F32R) for c in range(4)]
        w_lo = [sb(f"w_lo{c}", [P, 4, P], F32R) for c in range(4)]
        qk_hi = sb("qk_hi", [P, 2, 2, T], F32R)
        qk_lo = sb("qk_lo", [P, 2, 2, T], F32R)
        v_hi = sb("v_hi", [P, NT, 2, HD], F32R)
        v_lo = sb("v_lo", [P, NT, 2, HD], F32R)
        oT_hi = sb("oT_hi", [P, 2, T], F32R)
        oT_lo = sb("oT_lo", [P, 2, T], F32R)
        moe_w = nc.alloc_sbuf_tensor_at("moe_w", [P, NE, EW], F32, offset=moe_at)
        assert nc.sbuf_base >= moe_at + NE * EW * 4
        yg_at.append(nc.sbuf_base)
        prob = sb("prob", [P, 4, 2, S])
        pT_hi = sb("pT_hi", [P, 2, 2, S], F32R)
        pT_lo = sb("pT_lo", [P, 2, 2, S], F32R)
        yg = [nc.alloc_sbuf_tensor_at(f"yg{n}", [P, 2, NT, D], F32, offset=at) for n, at in enumerate(yg_at)]
        rmax = sb("rmax", [P, 2, 2])
        nmax = sb("nmax", [P, 2, 2])
        rsum = sb("rsum", [P, 2, 2])
        rinv = sb("rinv", [P, 2, 2])
        bn = sb("bn", [P, NT, 6])
        mv = sb("mv", [P, NT, 2])
        var = sb("var", [P, NT])
        sd = sb("sd", [P, NT])
        rstd = sb("rstd", [P, NT])
        nt1 = sb("nt1", [P, NT])
        ids = sb("ids", [P, T], I32)
        xg_at = nc.sbuf_base
        cw = sb("cw", [P, NROUTE, KT, D])
        hT_f = cw[:, :, :, :].rearrange("p (k a) t d -> p k (a t d)", k=KT)
        sg = sb("sg", [P, 2, FI])
        hid = sb("hid", [P, 2, FI])
        hidT = sb("hidT", [P, 2, SLOTS])
        arena_at = nc.sbuf_base
        hT_hi = sb("hT_hi", [P, KT, T], F32R)
        hT_lo = sb("hT_lo", [P, KT, T], F32R)
        cT_hi = sb("cT_hi", [P, NROUTE, KT, D], F32R)
        cT_lo = sb("cT_lo", [P, NROUTE, KT, D], F32R)
        mask = sb("mask", [P, NROUTE, T])
        arena_end = nc.sbuf_base
        cursor = [arena_at]

        def later(name, shape, dt=F32):
            n = {F32: 4, I32: 4, U32: 4, F16: 2, BF16: 2}[dt]
            for m in shape[1:]:
                n *= m
            t = nc.alloc_sbuf_tensor_at(name, shape, dt, offset=cursor[0])
            cursor[0] += -(-n // 32) * 32
            assert cursor[0] <= arena_end
            return t

        score = later("score", [P, NT, NE])
        sel = later("sel", [P, NT, NE])
        top = later("top", [P, NT, 8])
        topi = later("topi", [P, NT, 8], U32)
        chosen = later("chosen", [P, TOPK, NT], F16)
        many_at = cursor[0]
        iota_e = later("iota_e", [P, NE, CH], F16)
        iota_s = later("iota_s", [P, SLOTS, CH], F16)
        iota_tc = later("iota_tc", [P, TILES, CH], F16)
        tok_id = later("tok_id", [P, TILES, CH], F16)
        hot = later("hot", [P, NE, TOPK, NT], F16)
        two = later("two", [P, NE, 2, NT], F16)
        work = later("work", [P, NE, TOPK, NT])
        member = later("member", [P, NT, NE], BF16)
        count = later("count", [NE, 1])
        over = later("over", [NE, NT])
        tiles_e = later("tiles_e", [NE, 1])
        tiles_b = later("tiles_b", [NE, P], BF16)
        end_e = later("end_e", [NE, 1])
        past = later("past", [NE, TILES], BF16)
        expert = later("expert", [1, TILES])
        column_of = later("column_of", [1, TILES], I32)
        used = later("used", [1, 1], I32)
        base = later("base", [P, NE])
        place = later("place", [P, NE, NT])
        slot_f = later("slot_f", [P, TOPK, NT])
        slot_i = later("slot_i", [P, TOPK, NT], I32)
        part_i = later("part_i", [P, 2, CH], I32)
        part_h = later("part_h", [P, 2, CH], F16)
        gain = later("gain", [P, TOPK, NT])
        gsum = later("gsum", [P, NT])
        source = later("source", [P, TILES], I32)
        src = later("src", [P, STEPS], I32)
        one_hot_at = cursor[0]
        in_tile = later("in_tile", [P, TILES, CH], F16)
        in_slot = later("in_slot", [P, SLOTS, CH], F16)
        cursor[0] = many_at
        xT = later("xT", [P, 2, D])
        xg = later("xg", [P, STEPS, D])
        ysb = later("ysb", [P, STEPS, D])
        xg_last = [nc.alloc_sbuf_tensor_at(f"xg_last{n}", [P, STEPS, D], F32, offset=at)
                   for n, at in enumerate((xg_at, one_hot_at, one_hot_at + STEPS * D * 4))]
        assert LAST == len(xg_last) and one_hot_at + 2 * STEPS * D * 4 <= arena_end
        gact = x_in[:, :, :].rearrange("p (a t) d -> p a (t d)", a=4)
        gm = prob[:, :, :, :].rearrange("p a q k -> p a (q k)")
        gu_hi = pT_hi[:, :, :, :].rearrange("p a q k -> p a (q k)")
        gu_lo = pT_lo[:, :, :, :].rearrange("p a q k -> p a (q k)")
        zeros = sb("zeros", [1, P], BF16)

        d_x = [sem(f"d_x{half}") for half in range(2)]
        d_b, d_bo, d_ids, d_cw = sem("d_b"), sem("d_bo"), sem("d_ids"), sem("d_cw")
        d_w = [sem(f"d_w{c}") for c in range(4)]
        d_out = sem("d_out")
        p_const = sem("p_const")
        p_mask = sem("p_mask")
        p_many = sem("p_many")
        p_wm = sem("p_wm")
        a_wh = sem("a_wh")
        p_wl = sem("p_wl")
        v_ln = sem("v_ln")
        a_sd = sem("a_sd")
        t_ln, a_ln, v_lnlo = sem("t_ln"), sem("a_ln"), sem("v_lnlo")
        t_b, v_b = sem("t_b"), sem("v_b")
        t_sc = sem("t_sc")
        v_m1, v_max = sem("v_m1"), sem("v_max")
        a_exp = sem("a_exp")
        v_ri, v_p = sem("v_ri"), sem("v_p")
        t_pT, a_pT, v_pT = sem("t_pT"), sem("a_pT"), sem("v_pT")
        t_o, a_o, v_o = sem("t_o"), sem("a_o"), sem("v_o")
        t_j = sem("t_j")
        a_qk, v_qk = sem("a_qk"), sem("v_qk")
        a_v, v_v = sem("a_v"), sem("v_v")
        v_w = sem("v_w")
        a_c, v_c = sem("a_c"), sem("v_c")
        t_z, a_z = sem("t_z"), sem("a_z")
        p_gm, v_t = sem("p_gm"), sem("v_t")
        a_g, v_g = sem("a_g"), sem("v_g")
        t_y, v_y = sem("t_y"), sem("v_y")
        d_r, d_sw, d_h = sem("d_r"), sem("d_sw"), sem("d_h")
        d_m = sem("d_m")
        t_rw, v_rw = sem("t_rw"), sem("v_rw")
        a_hf, v_hf = sem("a_hf"), sem("v_hf")
        t_r, a_r, v_r = sem("t_r"), sem("a_r"), sem("v_r")
        t_gu, a_s, v_h = sem("t_gu"), sem("a_s"), sem("v_h")
        t_hT, a_hT, t_dn = sem("t_hT"), sem("a_hT"), sem("t_dn")
        v_sh, a_y = sem("v_sh"), sem("a_y")
        t_x, v_x = sem("t_x"), sem("v_x")
        d_g = [sem(f"d_g{u}") for u in range(STEPS)]
        d_y = [sem(f"d_y{u}") for u in range(STEPS)]
        d_spare = sem("d_spare")
        d_gl = [sem(f"d_gl{n}") for n in range(LAST * STEPS)]
        d_yg = [[sem(f"d_yg{t}_{pair}") for pair in range(2)] for t in range(NT)]
        v_own = sem("v_own")
        p_src, v_cmb = sem("p_src"), sem("v_cmb")

        bX, bG, bH, bY = bank[0:2], bank[2:4], bank[4:6], bank[6:8]
        SH = NT

        h_dram = nc.dram_tensor("h_dram", (T, D), F32, kind="Internal").ap()
        y_dram = nc.dram_tensor("y_dram", (TILES * SLOTS, D), F32, kind="Internal").ap()
        x_rows = a["x"].rearrange("b s d -> (b s) d").rearrange("(t p) d -> p t d", p=P)
        out_rows = out.rearrange("b s d -> (b s) d").rearrange("(t p) d -> p t d", p=P)
        codes = [a[f"w{n}_codes"].rearrange("(t p) n -> p t n", p=P) for n in "qkv"]
        scales = [a[f"w{n}_scales"] for n in "qkv"]
        wo_codes = a["wo_codes"].rearrange("(h p) n -> p h n", p=P)

        def load_chunk(eng, c, g, parts=(Q, K)):
            def spread(rows):
                return rows.unsqueeze(1).to_broadcast([rows.shape[0], QB, rows.shape[1]])
            if c in (H0, H1):
                col = g * (2 * HD) + (0 if c == H0 else HD)
                for m in parts:
                    j = (Q, K).index(m)
                    eng.dma_start(st_c[c][:, KT * j:KT * j + KT, :], codes[m][:, :, bass.ds(col, HD)]).then_inc(d_w[c], 16)
                    for kt in range(KT):
                        eng.dma_start(st_s[c][:, KT * j + kt, :],
                                      spread(scales[m][kt * 4:kt * 4 + 4, bass.ds(col, HD)])).then_inc(d_w[c], 16)
            elif c == VC:
                col = g * (2 * HD)
                dst_c = st_c[c][:, :, :].rearrange("p (t n) e -> p t (n e)", t=KT)
                dst_s = st_s[c][:, :, :].rearrange("p (t n) e -> p t (n e)", t=KT)
                eng.dma_start(dst_c, codes[V][:, :, bass.ds(col, 2 * HD)]).then_inc(d_w[c], 16)
                for kt in range(KT):
                    eng.dma_start(dst_s[:, kt, :],
                                  spread(scales[V][kt * 4:kt * 4 + 4, bass.ds(col, 2 * HD)])).then_inc(d_w[c], 16)
            else:
                dst_c = st_c[c][:, :, :].rearrange("p (h n) e -> p h (n e)", h=2)
                dst_s = st_s[c][:, :, :].rearrange("p (h n) e -> p h (n e)", h=2)
                eng.dma_start(dst_c, wo_codes[:, bass.ds(g * 2, 2), :]).then_inc(d_w[c], 16)
                for hp in range(2):
                    eng.dma_start(dst_s[:, hp, :],
                                  spread(a["wo_scales"][bass.ds(g * 8 + hp * 4, 4), :])).then_inc(d_w[c], 16)

        DMAS = {H0: 6, VC: 3, H1: 6, WC: 3}

        HT = NT // 2
        LN_STEPS = 2 * HT + 1 + 5 + HT
        R_MEMBER, R_TILES, R_PAST, R_HOT, R_EXPERT, R_SOURCE = 1, 2, 3, 4, 5, 6

        combine_order = [(n // (2 * TOPK) * 2 + n % 2, n // 2 % TOPK) for n in range(NT * TOPK)]

        BEHIND = 3
        RSTEPS = 2 * NROUTE * KT

        def routed(n):
            return n // (NROUTE * KT), n // KT % NROUTE, n % KT

        block = ctx.enter_context(nc.Block())

        @block.sync
        def _(sp):
            def load_x(eng, half):
                ts = slice(half * HT, (half + 1) * HT)
                eng.dma_start(x_in[:, ts, :], x_rows[:, ts, :]).then_inc(d_x[half], 16)

            load_x(sp, 0)
            load_chunk(sp, H0, 0, (Q,))
            load_x(sp, 1)
            load_chunk(sp, H1, 0)
            load_chunk(sp, VC, 0)
            sp.dma_start(cw[:, :, :, :], a["ctx"].rearrange("e (t p) d -> p e t d", p=P)).then_inc(d_cw, 16)
            load_chunk(sp, WC, 0)
            sp.dma_start(bo_b[:, :], a["bo"].unsqueeze(0).to_broadcast([P, D])).then_inc(d_bo, 16)
            sp.dma_start(ids[:, :], a["tok"].rearrange("b s -> (b s)").unsqueeze(0).to_broadcast([P, T])).then_inc(d_ids, 16)
            sp.dma_start(rw_rows[:, :], a["router_w"]).then_inc(d_r, 16)
            sp.dma_start(rb[:, :], a["bias"].unsqueeze(0).to_broadcast([P, NE])).then_inc(d_r, 16)
            sp.dma_start(sgu[:, :, 0, :], a["sw_gate"].rearrange("(t p) i -> p t i", p=P)).then_inc(d_sw, 16)
            sp.dma_start(sgu[:, :, 1, :], a["sw_up"].rearrange("(t p) i -> p t i", p=P)).then_inc(d_sw, 16)
            sp.dma_start(sdn[:, :], a["sw_down"]).then_inc(d_sw, 16)
            for c, n in ((H0, 1), (H1, 2), (VC, 3)):
                sp.wait_ge(p_wl, n)
                load_chunk(sp, c, 1)

            def reload(g, chunks):
                for c in chunks:
                    sp.wait_ge(p_wl, g * 4 + 3 + {H0: 1, VC: 2, H1: 3, WC: 4}[c])
                    load_chunk(sp, c, g + (1 if c == WC else 2))

            reload(0, (H0, VC, H1, WC))
            with sp.Fori(1, G - 2) as g:
                reload(g, (H0, VC, H1, WC))
            reload(G - 2, (WC,))
            spare = y_dram[T * TOPK:TILES * SLOTS, :].rearrange("(n r) d -> n r d", r=T)
            for n in range(TILES * SLOTS // T - TOPK):
                sp.dma_start(spare[n], a["x"].rearrange("b s d -> (b s) d")).then_inc(d_spare, 16)
            sp.wait_ge(v_w, 4 * G + 1)
            EB = NE // 4
            for q in range(4):
                es = slice(q * EB, (q + 1) * EB)
                gate = a["w_gate"][es, :, :].rearrange("e (t p) i -> p e t i", p=P)
                up = a["w_up"][es, :, :].rearrange("e (t p) i -> p e t i", p=P)
                down = a["w_down"][es, :, :].rearrange("e p d -> p e d")
                gu = moe_w[:, es, 0:2 * D].rearrange("p e (t m) -> p e t m", t=KT)
                for t in range(KT):
                    sp.dma_start(gu[:, :, t, 0:FI], gate[:, :, t, :]).then_inc(d_m, 16)
                    sp.dma_start(gu[:, :, t, FI:2 * FI], up[:, :, t, :]).then_inc(d_m, 16)
                sp.dma_start(moe_w[:, es, 2 * D:EW], down).then_inc(d_m, 16)
            for half in range(2):
                ts = slice(half * HT, (half + 1) * HT)
                sp.wait_ge(v_ln, (4 + half + 1) * LN_STEPS)
                sp.dma_start(h_dram.rearrange("(t p) d -> p t d", p=P)[:, ts, :], h_row[:, ts, :]).then_inc(d_h, 16)

            sp.wait_ge(d_spare, 16 * (TILES * SLOTS // T - TOPK))
            for u in range(STEPS):
                sp.sem_inc(d_y[u], 16)
            def store(it):
                for u in range(STEPS):
                    sp.wait_ge(a_y, it * STEPS + u + 1)
                    sp.dma_start(y_dram[bass.ds((it * STEPS + u) * SLOTS, SLOTS), :], ysb[:, u, :]).then_inc(d_y[u], 16)

            with sp.Fori(0, TRIPS) as it:
                store(it)
            for t in range(0, NT, 2):
                sp.wait_ge(v_cmb, (t + 2) * TOPK)
                sp.dma_start(out_rows[:, t:t + 2, :], x_acc[:, t:t + 2, :]).then_inc(d_out, 16)
            sp.wait_ge(d_out, 16 * (NT // 2))
            for u in range(STEPS):
                sp.wait_ge(d_y[u], 16 * (TRIPS + 1))

        @block.gpsimd
        def _(pool):
            def prep(c, wm, load_count, free=None):
                wait(pool, d_w[c], load_count)
                pool.tensor_tensor(st_c[c][:, :, :], st_c[c][:, :, :], st_s[c][:, :, :], ALU.mult).then_inc(p_wm, 1)
                wait(pool, p_wm, wm)
                wait(pool, a_wh, wm)
                pool.tensor_tensor(w_lo[c][:, :, :], st_c[c][:, :, :], w_hi[c][:, :, :], ALU.subtract).then_inc(p_wl, 1)

            pool.memset(ident[:, :], 0.0).then_inc(p_const, 1)
            pool.memset(zeros[:, :], 0.0).then_inc(p_const, 1)
            pool.wait_ge(p_const, 2)
            pool.affine_select(out=ident[:, :], in_=ident[:, :], compare_op=ALU.not_equal, fill=1.0,
                               base=0, pattern=[[-1, P]], channel_multiplier=1).then_inc(p_const, 1)
            for n, nm in enumerate(("bq", "bk", "bv")):
                pool.dma_start(b_rows[n * H:(n + 1) * H, :], a[nm].rearrange("(h d) -> h d", d=HD)).then_inc(d_b, 16)
            for n, c in enumerate((H0, H1, VC)):
                prep(c, n + 1, 16 * DMAS[c])
            def add_bias():
                for half in range(2):
                    pool.wait_ge(d_x[half], 16)
                pool.wait_ge(d_bo, 16)
                pool.tensor_tensor(x_acc[:, :, :], x_in[:, :, :],
                                   bo_b[:, :].unsqueeze(1).to_broadcast([P, NT, D]), ALU.add).then_inc(v_w, 1)

            def masks():
                pool.wait_ge(d_ids, 16)
                per = VOCAB // NROUTE
                for e in range(NROUTE):
                    pool.tensor_scalar(mask[:, e, :], ids[:, :], float(per * e) if e else float(per), None,
                                       ALU.is_ge if e else ALU.is_lt).then_inc(p_mask, 1)
                pool.wait_ge(p_mask, NROUTE)
                for e in range(1, NROUTE - 1):
                    pool.tensor_tensor(mask[:, e, :], mask[:, e, :], mask[:, e + 1, :], ALU.subtract).then_inc(p_mask, 1)

            def constants():
                pool.iota(iota_t[:, :], pattern=[[1, TILES]], base=0, channel_multiplier=0,
                          allow_small_or_imprecise_dtypes=True).then_inc(p_const, 1)
                pool.iota(iota_f[:, :], pattern=[[SLOTS, NT]], base=0, channel_multiplier=0,
                          allow_small_or_imprecise_dtypes=True).then_inc(p_const, 1)
                pool.memset(ones[:, :], 1.0).then_inc(p_const, 1)
                pool.wait_ge(p_const, 6)
                pool.affine_select(out=before[:, :], in_=ones[:, :], compare_op=ALU.is_gt, fill=0.0,
                                   base=0, pattern=[[1, P]], channel_multiplier=-1).then_inc(p_const, 1)
                pool.affine_select(out=upto[:, :], in_=ones[0:NE, 0:NE], compare_op=ALU.is_ge, fill=0.0,
                                   base=0, pattern=[[1, NE]], channel_multiplier=-1).then_inc(p_const, 1)

            def body(pl):
                g = pl.g
                if pl.last:
                    masks()
                for c in ((WC,) if pl.last else (H0, VC, H1, WC)):
                    ahead = 0 if c == WC else 1
                    prep(c, pl.weights(c, ahead), (g + ahead) * (16 * DMAS[c]) + 16 * DMAS[c])
                    if pl.first and c == H0:
                        add_bias()
                    if pl.first and c == WC:
                        constants()

            over_groups(pool, body)

            pool.wait_ge(p_mask, 2 * NROUTE - 2)
            for n in range(RSTEPS):
                half, e, ft = routed(n)
                pool.wait_ge(a_z, n + 1)
                pool.tensor_tensor(gact[:, n % 4, :], gact[:, n % 4, :], mask[:, e, half * HALF:(half + 1) * HALF],
                                   ALU.mult).then_inc(p_gm, 1)
            pool.wait_ge(t_y, RSTEPS)
            pool.iota(iota_e[:, :, :], pattern=[[1, NE], [0, CH]], base=0, channel_multiplier=0,
                      allow_small_or_imprecise_dtypes=True).then_inc(p_many, 1)
            pool.iota(iota_s[:, :, :], pattern=[[1, SLOTS], [0, CH]], base=0, channel_multiplier=0,
                      allow_small_or_imprecise_dtypes=True).then_inc(p_many, 1)
            pool.iota(iota_tc[:, :, :], pattern=[[1, TILES], [0, CH]], base=0, channel_multiplier=0,
                      allow_small_or_imprecise_dtypes=True).then_inc(p_many, 1)
            pool.iota(tok_id[:, :, :].rearrange("p s (k t) -> p s k t", k=TOPK), pattern=[[0, TILES], [0, TOPK], [P, NT]],
                      base=0, channel_multiplier=1, allow_small_or_imprecise_dtypes=True).then_inc(p_many, 1)

            pool.wait_ge(d_h, 32)
            pool.wait_ge(v_r, R_SOURCE)

            def gathers(it, first):
                for u in range(STEPS):
                    index = source[:, u:u + 1]
                    if not first:
                        wait(pool, t_x, (it - 1) * STEPS + (u + PART if u % PART == 0 else u + 1))
                        if u % PART == 0:
                            pool.tensor_copy(src[:, u:u + PART], source[:, bass.ds(it * STEPS + u, PART)]).then_inc(p_src, 1)
                            wait(pool, p_src, (it - 1) * (STEPS // PART) + u // PART + 1)
                        apart(pool)
                        index = src[:, u:u + 1]
                    pool.indirect_dma_start(out=xg[:, u, :], out_offset=None, in_=h_dram,
                                            in_offset=bass.IndirectOffsetOnAxis(ap=index, axis=0)).then_inc(d_g[u], 16)

            gathers(0, True)
            with pool.Fori(1, TRIPS - LAST) as it:
                gathers(it, False)
            pool.wait_ge(t_gu, SH)
            for n in range(LAST * STEPS):
                index = source[:, (TRIPS - LAST) * STEPS + n:(TRIPS - LAST) * STEPS + n + 1]
                pool.indirect_dma_start(out=xg_last[n // STEPS][:, n % STEPS, :], out_offset=None, in_=h_dram,
                                        in_offset=bass.IndirectOffsetOnAxis(ap=index, axis=0)).then_inc(d_gl[n], 16)

            tiles = pool.value_load(used[0:1, 0:1], min_val=1, max_val=TILES)
            for u in range(STEPS):
                pool.wait_ge(d_y[u], (tiles + (STEPS - 1 - u)) // STEPS * 16 + 16)
            apart(pool)
            for t, k in combine_order:
                pool.indirect_dma_start(out=yg[k // 2][:, k % 2, t, :], out_offset=None, in_=y_dram,
                                        in_offset=bass.IndirectOffsetOnAxis(ap=slot_i[:, k, t:t + 1], axis=0)
                                        ).then_inc(d_yg[t][k // 2], 16)


        def ln_vector(dve, n, half, src):
            base = (2 * n + half) * LN_STEPS
            tiles = range(half * HT, (half + 1) * HT)
            hs = slice(half * HT, (half + 1) * HT)

            def statistics():
                for t in tiles:
                    dve.bn_stats(bn[:, t, :], src[:, t, :]).then_inc(v_ln, 1)

            def variances():
                for i, t in enumerate(tiles):
                    dve.wait_ge(v_ln, base + i + 1)
                    dve.bn_aggr(mv[:, t, :], bn[:, t, :]).then_inc(v_ln, 1)
                dve.wait_ge(v_ln, base + 2 * HT)
                dve.tensor_scalar(var[:, hs], mv[:, hs, 1], EPS, None, ALU.add).then_inc(v_ln, 1)

            def reciprocals():
                dve.wait_ge(a_sd, 2 * n + half + 1)
                k = base + 2 * HT + 1
                dve.reciprocal(rstd[:, hs], sd[:, hs]).then_inc(v_ln, 1)
                dve.wait_ge(v_ln, k + 1)
                dve.tensor_tensor(nt1[:, hs], rstd[:, hs], rstd[:, hs], ALU.mult).then_inc(v_ln, 1)
                dve.wait_ge(v_ln, k + 2)
                dve.tensor_tensor(nt1[:, hs], nt1[:, hs], var[:, hs], ALU.mult).then_inc(v_ln, 1)
                dve.wait_ge(v_ln, k + 3)
                dve.tensor_scalar(nt1[:, hs], nt1[:, hs], -0.5, 1.5, ALU.mult, ALU.add).then_inc(v_ln, 1)
                dve.wait_ge(v_ln, k + 4)
                dve.tensor_tensor(rstd[:, hs], rstd[:, hs], nt1[:, hs], ALU.mult).then_inc(v_ln, 1)
                dve.wait_ge(v_ln, k + 5)

            def rows():
                for t in tiles:
                    dve.tensor_scalar(h_row[:, t, :], src[:, t, :], mv[:, t, 0:1], rstd[:, t:t + 1],
                                      ALU.subtract, ALU.mult).then_inc(v_ln, 1)

            return statistics, variances, reciprocals, rows

        def ln_scalar(act, n, half):
            act.wait_ge(v_ln, (2 * n + half) * LN_STEPS + 2 * HT + 1)
            hs = slice(half * HT, (half + 1) * HT)
            act.activation(sd[:, hs], var[:, hs], ACT.Sqrt).then_inc(a_sd, 1)

        def ln_tensor(pe, n, half, banks):
            for kt in range(KT):
                for i in range(HT):
                    t = half * HT + i
                    pe.wait_ge(v_ln, (2 * n + half + 1) * LN_STEPS - HT + i + 1)
                    mm = pe.transpose(banks[kt][:, i * P:i * P + P], h_row[:, t, kt * P:kt * P + P], ident[:, :])
                mm.then_inc(t_ln, 1)

        def ln_high(act, n, half, banks):
            for kt in range(KT):
                act.wait_ge(t_ln, 4 * n + 2 * half + kt + 1)
                act.copy(hT_hi[:, kt, half * HALF:(half + 1) * HALF], banks[kt][:, :]).then_inc(a_ln, 1)

        def ln_low(dve, n, half, banks):
            sl = slice(half * HALF, (half + 1) * HALF)
            for kt in range(KT):
                dve.wait_ge(a_ln, 4 * n + 2 * half + kt + 1)
                dve.tensor_tensor(hT_lo[:, kt, sl], banks[kt][:, :], hT_hi[:, kt, sl], ALU.subtract).then_inc(v_lnlo, 1)

        FIRST = [bank[2:4], bank[4:6]]

        @block.tensor
        def _(pe):
            def mm3(o, l_hi, l_lo, r_hi, r_lo, start, stop, share=False):
                pe.matmul(o, l_lo, r_hi, start=start, stop=False, skip_group_check=share)
                pe.matmul(o, l_hi, r_lo, start=False, stop=False, skip_group_check=share)
                return pe.matmul(o, l_hi, r_hi, start=False, stop=stop, skip_group_check=share)

            pe.wait_ge(p_const, 3)
            pe.wait_ge(d_b, 16 * 3)
            pe.transpose(bJ[0][:, 0:3 * H], b_rows[:, :], ident[0:3 * H, 0:3 * H]).then_inc(t_b, 1)
            ln_tensor(pe, 0, 0, FIRST[0])
            pe.wait_ge(v_b, 1)

            def proj_tile(pl, tile, number, pos, final=False):
                kind, m, hp, n = tile
                o = bJ[pos % 2]
                if pl is not None:
                    which, value = pl.freed(pos)
                    wait(pe, {"qk": v_qk, "v": v_v, "w": v_w, "ctx": v_c}[which], value)
                elif pos >= 2:
                    wait(pe, v_qk, pos - 1)
                if kind == "ctx":
                    pe.wait_ge(d_cw, 16)
                    for kt in range(KT):
                        for ft in range(KT):
                            mm = pe.transpose(o[:, kt * D + ft * P:kt * D + ft * P + P],
                                              cw[:, n, ft, kt * P:kt * P + P], ident[:, :])
                elif kind in ("qk", "next"):
                    c = H0 if kind == "next" else H1
                    if n == 0 and m == Q:
                        wait(pe, p_wl, 1 if pl is None else pl.weights(c, 1 if kind == "next" else 0))
                    for kt in range(KT):
                        j = KT * m + kt
                        mm = mm3(o[:, :], w_hi[c][:, j, :], w_lo[c][:, j, :],
                                 hT_hi[:, kt, n * HALF:(n + 1) * HALF], hT_lo[:, kt, n * HALF:(n + 1) * HALF],
                                 kt == 0, kt == KT - 1)
                elif kind == "v":
                    if n == 0:
                        wait(pe, p_wl, pl.weights(VC, 0))
                    for i in range(2):
                        t = 2 * n + i
                        for kt in range(KT):
                            mm = mm3(o[:, i * D:(i + 1) * D], hT_hi[:, kt, t * P:(t + 1) * P], hT_lo[:, kt, t * P:(t + 1) * P],
                                     w_hi[VC][:, KT * kt:KT * kt + 2, :].rearrange("p a b -> p (a b)"),
                                     w_lo[VC][:, KT * kt:KT * kt + 2, :].rearrange("p a b -> p (a b)"),
                                     kt == 0, kt == KT - 1)
                else:
                    if n == 0:
                        wait(pe, p_wl, pl.weights(WC, 0) if final else (pl.g - 1) * 4 + 3 + 4)
                    wait(pe, v_o, pl.pair(PAIRS if final else 0) - B + n + 1)
                    for i in range(2):
                        t = 2 * n + i
                        for hh in range(2):
                            mm = mm3(o[:, i * D:(i + 1) * D], oT_hi[:, hh, t * P:(t + 1) * P], oT_lo[:, hh, t * P:(t + 1) * P],
                                     w_hi[WC][:, 2 * hh:2 * hh + 2, :].rearrange("p a b -> p (a b)"),
                                     w_lo[WC][:, 2 * hh:2 * hh + 2, :].rearrange("p a b -> p (a b)"),
                                     hh == 0, hh == 1)
                mm.then_inc(t_j, 1)

            def scores(pl, i):
                p = pl.pair(i)
                wait(pe, a_exp, p - 1 if not (pl.first and i < 2) else 0)
                hp, b = i // B, i % B
                if b in (0, 2):
                    wait(pe, v_qk, pl.g * 8 + 4 * hp + (2 if b == 0 else 4))
                for qt in range(2):
                    qs = slice(b * S + qt * P, b * S + qt * P + P)
                    ks = slice(b * S, b * S + S)
                    mm = mm3(bS[i % 2][:, qt * S:(qt + 1) * S], qk_hi[:, hp, Q, qs], qk_lo[:, hp, Q, qs],
                             qk_hi[:, hp, K, ks], qk_lo[:, hp, K, ks], True, True)
                mm.then_inc(t_sc, 1)

            def turn(pl, i):
                p = pl.pair(i)
                wait(pe, v_p, p + 1)
                wait(pe, v_pT, p - 1 if not (pl.first and 0 <= i < 2) else 0)
                for kt in range(2):
                    for qt in range(2):
                        mm = pe.transpose(bP[i % 2][:, kt * S + qt * P:kt * S + qt * P + P],
                                          prob[:, i % 4, qt, kt * P:kt * P + P], ident[:, :])
                mm.then_inc(t_pT, 1)

            def attend(pl, i):
                p = pl.pair(i)
                wait(pe, v_pT, p + 1)
                wait(pe, v_o, p - 1 if not (pl.first and 0 <= i < 2) else 0)
                hp, b = (i % PAIRS) // B, i % B
                if 0 <= i < B:
                    wait(pe, v_v, pl.v_count(b))
                for kt in range(2):
                    mm = mm3(bO[i % 2][:, 0:S], v_hi[:, 2 * b + kt, hp, :], v_lo[:, 2 * b + kt, hp, :],
                             pT_hi[:, i % 2, kt, :], pT_lo[:, i % 2, kt, :], kt == 0, kt == 1)
                mm.then_inc(t_o, 1)

            for pos, t in enumerate(PRO_TILES):
                if pos == 1:
                    ln_tensor(pe, 0, 1, FIRST[1])
                pe.wait_ge(v_lnlo, 2 + 2 * t[3])
                proj_tile(None, t, pos, pos)

            def body(pl):
                for i in range(PAIRS + (DRAIN + 1 if pl.last else 0)):
                    if i < PAIRS:
                        scores(pl, i)
                    for tile in pl.of_slot(i, 0):
                        proj_tile(pl, *tile)
                    if not (pl.first and i < TURN) and i < PAIRS + TURN:
                        turn(pl, i - TURN)
                    if not (pl.first and i < ATTEND) and i < PAIRS + ATTEND:
                        attend(pl, i - ATTEND)
                    for tile in pl.of_slot(i, 1):
                        proj_tile(pl, *tile)

            over_groups(pe, body)

            def zero(half):
                for yb in ENDS[half]:
                    pe.matmul(yb[:, :], zeros[:, :], zeros[:, 0:1].to_broadcast([1, HALF]), start=True, stop=True)

            def pre(n):
                half, e, ft = routed(n)
                wait(pe, v_t, n - 3)
                for kt in range(KT):
                    mm = mm3(Z_BANKS[n % 4][:, :], cT_hi[:, e, kt, ft * P:ft * P + P], cT_lo[:, e, kt, ft * P:ft * P + P],
                             hT_hi[:, kt, half * HALF:(half + 1) * HALF], hT_lo[:, kt, half * HALF:(half + 1) * HALF],
                             kt == 0, kt == KT - 1)
                mm.then_inc(t_z, 1)

            def post(n):
                half, e, ft = routed(n)
                pe.wait_ge(v_g, n + 1)
                for j in range(4):
                    yb = ENDS[half][j // 2][:, (j % 2) * D:(j % 2) * D + D]
                    mm = mm3(yb, gu_hi[:, n % 2, j * P:(j + 1) * P], gu_lo[:, n % 2, j * P:(j + 1) * P],
                             cT_hi[:, e, ft, :], cT_lo[:, e, ft, :], False, e == NROUTE - 1 and ft == KT - 1, True)
                mm.then_inc(t_y, 1)

            pe.wait_ge(d_r, 32)
            pe.wait_ge(v_o, G * PAIRS)
            for kt in range(KT):
                mm = pe.transpose(bank[5][:, kt * NE:(kt + 1) * NE], rw_rows[:, kt * P:(kt + 1) * P], ident[0:NE, 0:NE])
            mm.then_inc(t_rw, 1)
            pe.wait_ge(v_c, NROUTE)
            ln_tensor(pe, 1, 0, ENDS[0])
            for n in range(RSTEPS + BEHIND):
                if n % (RSTEPS // 2) == 0 and n < RSTEPS:
                    pe.wait_ge(v_lnlo, 6 if n == 0 else 8)
                if n == 3:
                    pe.wait_ge(v_rw, 1)
                if n < RSTEPS:
                    pre(n)
                if n in (1, RSTEPS // 2 + 1):
                    zero(0 if n == 1 else 1)
                if n == 2:
                    ln_tensor(pe, 1, 1, ENDS[1])
                if n >= BEHIND:
                    post(n - BEHIND)

            def gate_up(n, e, xT_of):
                for kt in range(KT):
                    w = sgu[:, kt, :, :].rearrange("p a i -> p (a i)") if e is None else \
                        moe_w[:, :, :].rearrange("p e m -> p (e m)")[:, bass.ds(e + kt * 2 * FI, 2 * FI)]
                    mm = pe.matmul(bG[n % 2][:, 0:2 * FI], xT_of(kt), w, start=kt == 0, stop=kt == KT - 1)
                mm.then_inc(t_gu, 1)

            def hidden_turn(n):
                pe.transpose(bH[n % 2][:, 0:SLOTS], hid[:, n % 2, :], ident[:, :]).then_inc(t_hT, 1)

            def down(n, e):
                w = moe_w[:, :, :].rearrange("p e m -> p (e m)")[:, bass.ds(e + 2 * D, D)]
                pe.matmul(bY[n % 2][:, 0:D], hidT[:, n % 2, :], w, start=True, stop=True).then_inc(t_dn, 1)

            def shared_gate_up(n):
                wait(pe, v_h, n - 1)
                gate_up(n, None, lambda kt: hT_f[:, kt, n * P:(n + 1) * P])

            def shared_turn(n):
                pe.wait_ge(v_h, n + 1)
                wait(pe, a_hT, n - 1)
                hidden_turn(n)

            def shared_down(n):
                pe.wait_ge(a_hT, n + 1)
                wait(pe, v_sh, n - 1)
                pe.matmul(bY[n % 2][:, 0:D], hidT[:, n % 2, :], sdn[:, :], start=True, stop=True).then_inc(t_dn, 1)

            def logits(half):
                for t in range(half * HT, (half + 1) * HT):
                    for kt in range(KT):
                        mm = pe.matmul(bank[0][:, t * NE:(t + 1) * NE], hT_f[:, kt, t * P:(t + 1) * P], rwT[:, kt, :],
                                       start=kt == 0, stop=kt == KT - 1)
                return mm

            ln_tensor(pe, 2, 0, ENDS[0])
            pe.wait_ge(a_hf, 2)
            pe.wait_ge(v_t, RSTEPS)
            pe.wait_ge(d_sw, 48)
            shared_gate_up(0)
            shared_gate_up(1)
            logits(0)
            ln_tensor(pe, 2, 1, ENDS[1])
            shared_turn(0)
            shared_turn(1)
            shared_gate_up(2)
            pe.wait_ge(a_hf, 3)
            pe.wait_ge(v_hf, 1)
            logits(1).then_inc(t_r, 1)
            shared_gate_up(3)
            shared_down(0)
            shared_down(1)
            for n in range(2, SH - 3):
                shared_turn(n)
                shared_gate_up(n + 2)
                shared_down(n)

            pe.wait_ge(v_r, R_MEMBER)
            pe.wait_ge(p_const, 8)
            for t in range(NT):
                mm = pe.matmul(bank[1][0:NE, 0:1], member[:, t, :], ones[:, 0:1], start=t == 0, stop=t == NT - 1)
            mm.then_inc(t_r, 1)
            rank = bank[0]
            pe.matmul(rank[:, 0:NT * NE], before[:, :], member[:, :, :].rearrange("p t e -> p (t e)"),
                      start=True, stop=False, skip_group_check=True)
            for t in range(NT - 1):
                pe.matmul(rank[:, (t + 1) * NE:NT * NE].rearrange("p (t e) -> p t e", e=NE), ones[:, :],
                          member[:, t:t + 1, :].to_broadcast([P, NT - 1 - t, NE]),
                          start=False, stop=t == NT - 2, skip_group_check=True)
            shared_turn(SH - 3)
            shared_gate_up(SH - 1)
            shared_turn(SH - 2)
            pe.wait_ge(v_r, R_TILES)
            pe.matmul(bank[1][0:NE, 0:1], upto[:, :], tiles_b[:, 0:1], start=True, stop=True)
            pe.matmul(bank[1][:, NE:2 * NE], tiles_b[:, :], before[0:NE, 0:NE], start=True, stop=True).then_inc(t_r, 1)
            shared_turn(SH - 1)
            shared_down(SH - 3)
            shared_down(SH - 2)
            pe.wait_ge(v_r, R_PAST)
            pe.matmul(bank[2][0:1, 0:TILES], ones[0:NE, 0:1], past[:, :], start=True, stop=True)
            pe.matmul(bank[2][0:1, TILES:TILES + 1], ones[0:NE, 0:1], tiles_b[:, 0:1], start=True, stop=True).then_inc(t_r, 1)


            pe.wait_ge(v_r, R_HOT)
            for c in range(CH):
                mm = pe.matmul(bank[0][:, 0:TILES], in_slot[:, :, c], in_tile[:, :, c], start=c == 0, stop=c == CH - 1)
            mm.then_inc(t_r, 1)
            shared_down(SH - 1)

            at = [pe.alloc_register(f"at{i}") for i in range(STEPS)]

            def load_columns(part, first):
                apart(pe)
                pe.reg_load(at[first:first + PART], column_of[0:1, bass.ds(part * PART, PART)])

            def column(tile):
                return pe.snap(at[tile % STEPS], min_val=0, max_val=(NE - 1) * EW)

            def row_turn(j, u, it):
                if isinstance(it, int) and it >= TRIPS - LAST:
                    n = j - (TRIPS - LAST) * STEPS
                    pe.wait_ge(d_gl[n], 16)
                    rows = xg_last[n // STEPS][:, n % STEPS, :]
                else:
                    wait(pe, d_g[u], it * 16 + 16)
                    rows = xg[:, u, :]
                wait(pe, v_x, j - 1)
                for kt in range(KT):
                    mm = pe.transpose(bX[u % 2][:, kt * SLOTS:(kt + 1) * SLOTS], rows[:, kt * P:(kt + 1) * P], ident[:, :])
                mm.then_inc(t_x, 1)

            def trip(it, first, last):
                for u in range(STEPS + (2 if last else 0)):
                    j = it * STEPS + u
                    if u == 2:
                        load_columns(it * 2 + 1, PART)
                    if u == PART + 2 and not last:
                        load_columns(it * 2 + 2, 0)
                    if u < STEPS - 1:
                        row_turn(j + 1, u + 1, it)
                    elif u == STEPS - 1 and not last:
                        row_turn(j + 1, 0, it + 1)
                    if u < STEPS:
                        wait(pe, v_x, j + 1)
                        wait(pe, v_h, j - 1 + SH)
                        gate_up(u, column(u), lambda kt: xT[:, u % 2, kt * SLOTS:(kt + 1) * SLOTS])
                    if not (first and u < 1) and u < STEPS + 1:
                        wait(pe, v_h, j + SH)
                        wait(pe, a_hT, j - 2 + SH)
                        hidden_turn(u - 1 + STEPS)
                    if not (first and u < 2):
                        wait(pe, a_hT, j - 1 + SH)
                        wait(pe, a_y, 0 if first and u < 4 else j - 3)
                        down(u - 2 + STEPS, column(u - 2))

            pe.wait_ge(v_r, R_SOURCE)
            pe.wait_ge(v_sh, SH)
            pe.wait_ge(d_m, 16 * 20)
            load_columns(0, 0)
            row_turn(0, 0, 0)
            trip(0, True, False)
            with pe.Fori(1, TRIPS - LAST - 1) as it:
                trip(it, False, False)
            for it in range(TRIPS - LAST - 1, TRIPS):
                trip(it, False, it == TRIPS - 1)

        @block.scalar
        def _(act):
            load_chunk(act, H0, 0, (K,))

            def weights_high(c, count):
                wait(act, p_wm, count)
                act.copy(w_hi[c][:, :, :], st_c[c][:, :, :]).then_inc(a_wh, 1)

            ln_scalar(act, 0, 0)
            weights_high(H0, 1)
            ln_high(act, 0, 0, FIRST[0])
            ln_scalar(act, 0, 1)
            weights_high(H1, 2)
            act.wait_ge(v_b, 1)

            def proj_high(pl, t, number, pos):
                kind, m, hp, n = t
                src = bJ[pos % 2]
                if kind == "w":
                    return
                wait(act, t_j, number + 1)
                if kind == "ctx":
                    act.copy(cT_hi[:, n, :, :].rearrange("p a b -> p (a b)"), src[:, :]).then_inc(a_c, 1)
                    return
                if kind == "v":
                    if n == 0:
                        wait(act, t_o, pl.pair(0))
                    act.copy(v_hi[:, 2 * n:2 * n + 2, :, :].rearrange("p t h d -> p (t h d)"), src[:, :]).then_inc(a_v, 1)
                    return
                g_h = 0 if pl is None else (pl.g + (1 if kind == "next" else 0)) * 2 + hp
                if n == 0 and pl is not None:
                    wait(act, t_sc, pl.pair(B) if kind == "next" else pl.pair(0))
                apart(act)
                act.activation(qk_hi[:, hp, m, n * HALF:(n + 1) * HALF], src[:, :], ACT.Identity,
                               bias=b_col[:, bass.ds(g_h + m * H, 1)]).then_inc(a_qk, 1)

            for pos, t in enumerate(PRO_TILES):
                if pos == 1:
                    ln_high(act, 0, 1, FIRST[1])
                proj_high(None, t, pos, pos)
            weights_high(VC, 3)

            def body(pl):
                for i in range(PAIRS + (DRAIN + 1 if pl.last else 0)):
                    if i < PAIRS:
                        p = pl.pair(i)
                        wait(act, v_max, p + 1)
                        wait(act, t_pT, p - 3 if not (pl.first and i < 4) else 0)
                        for qt in range(2):
                            ex = act.activation(prob[:, i % 4, qt, :], bS[i % 2][:, qt * S:(qt + 1) * S], ACT.Exp,
                                                bias=nmax[:, i % 2, qt:qt + 1], scale=SCALE,
                                                accum_out=rsum[:, i % 2, qt:qt + 1])
                        ex.then_inc(a_exp, 1)
                    for t, number, pos, final in pl.of_slot(i, 0):
                        proj_high(pl, t, number, pos)
                    if not (pl.first and i < TURN) and i < PAIRS + TURN:
                        j = i - TURN
                        wait(act, t_pT, pl.pair(j) + 1)
                        wait(act, t_o, pl.pair(j) - 1 if not (pl.first and j < 2) else 0)
                        act.copy(pT_hi[:, j % 2, :, :].rearrange("p a b -> p (a b)"), bP[j % 2][:, :]).then_inc(a_pT, 1)
                    if not (pl.first and i < ATTEND) and i < PAIRS + ATTEND:
                        j = i - ATTEND
                        hp, b = (j % PAIRS) // B, j % B
                        wait(act, t_o, pl.pair(j) + 1)
                        if hp == 0 and not pl.first and 0 <= j < PAIRS:
                            wait(act, t_j, pl.w_tile_number(b) + 1)
                        head = pl.g * 2 + (hp if j >= 0 else hp - 2) + 2 * H
                        apart(act)
                        act.activation(oT_hi[:, hp, b * S:(b + 1) * S], bO[j % 2][:, 0:S], ACT.Identity,
                                       bias=b_col[:, bass.ds(head, 1)]).then_inc(a_o, 1)
                    for t, number, pos, final in pl.of_slot(i, 1):
                        proj_high(pl, t, number, pos)
                    if (i in PREP_SLOTS and not pl.last) or (i == PAIRS - 2 and pl.last):
                        c = WC if pl.last else PREP_SLOTS[i]
                        if c == H0:
                            wait(act, t_j, pl.tiles[0][2])
                        elif c != WC or not pl.first:
                            kind = {VC: "v", H1: "qk", WC: "w"}[c]
                            wait(act, t_j, [tile[2] for tile in pl.tiles if tile[1][0] == kind and tile[0] < PAIRS][-1] + 1)
                        weights_high(c, pl.weights(c, 0 if c == WC else 1))

            over_groups(act, body)

            ln_scalar(act, 1, 0)
            ln_high(act, 1, 0, ENDS[0])
            ln_scalar(act, 1, 1)

            def routed_high(n):
                act.wait_ge(v_t, n + 1)
                wait(act, t_y, n - 1)
                act.copy(gu_hi[:, n % 2, :], gm[:, n % 4, :]).then_inc(a_g, 1)

            for n in range(RSTEPS):
                act.wait_ge(t_z, n + 1)
                wait(act, v_t, n - 3)
                act.activation(gact[:, n % 4, :], Z_BANKS[n % 4][:, :], ACT.Silu).then_inc(a_z, 1)
                if n >= 1:
                    routed_high(n - 1)
                if n == 3:
                    ln_high(act, 1, 1, ENDS[1])
            ln_scalar(act, 2, 0)
            routed_high(RSTEPS - 1)

            def rows_copy(half, kt):
                act.wait_ge(t_ln, 8 + 2 * half + kt + 1)
                act.copy(hT_f[:, kt, half * HALF:(half + 1) * HALF], ENDS[half][kt][:, :]).then_inc(a_hf, 1)

            def silu(n, count):
                wait(act, t_gu, count + 1)
                wait(act, v_h, count - 1)
                act.activation(sg[:, n % 2, :], bG[n % 2][:, 0:FI], ACT.Silu).then_inc(a_s, 1)

            def hidden_copy(n, count):
                wait(act, t_hT, count + 1)
                wait(act, t_dn, count - 1)
                act.copy(hidT[:, n % 2, :], bH[n % 2][:, 0:SLOTS]).then_inc(a_hT, 1)

            rows_copy(0, 0)
            rows_copy(0, 1)
            ln_scalar(act, 2, 1)
            silu(0, 0)
            silu(1, 1)
            rows_copy(1, 0)
            hidden_copy(0, 0)
            hidden_copy(1, 1)
            silu(2, 2)
            act.wait_ge(t_r, 1)
            act.activation(score[:, :, :].rearrange("p t e -> p (t e)"), bank[0][:, 0:NT * NE], ACT.Sigmoid).then_inc(a_r, 1)
            silu(3, 3)
            for n in range(2, SH):
                hidden_copy(n, n)
                if n + 2 < SH:
                    silu(n + 2, n + 2)

            def trip(it, first, last):
                for u in range(STEPS + (2 if last else 0)):
                    j = it * STEPS + u
                    if u < STEPS:
                        silu(u, j + SH)
                    if not (first and u < 1) and u < STEPS + 1:
                        hidden_copy(u - 1 + STEPS, j - 1 + SH)
                    if not (first and u < 2):
                        wait(act, t_dn, j - 1 + SH)
                        s = (u - 2) % STEPS
                        if not first:
                            wait(act, d_y[s], (it + 1 if u >= 2 else it) * 16)
                        act.copy(ysb[:, s, :], bY[u % 2][:, 0:D]).then_inc(a_y, 1)

            trip(0, True, False)
            with act.Fori(1, TRIPS - 1) as it:
                trip(it, False, False)
            trip(TRIPS - 1, False, True)

        @block.vector
        def _(dve):
            dve.wait_ge(d_x[0], 16)
            for part in ln_vector(dve, 0, 0, x_in):
                part()
            dve.wait_ge(t_b, 1)
            dve.tensor_copy(b_col[:, :], bJ[0][:, 0:3 * H]).then_inc(v_b, 1)
            dve.wait_ge(d_x[1], 16)
            statistics, variances, reciprocals, rows = ln_vector(dve, 0, 1, x_in)
            statistics()
            variances()
            ln_low(dve, 0, 0, FIRST[0])
            reciprocals()
            rows()
            dve.wait_ge(v_b, 1)

            def proj_low(pl, t, number, pos, final=False):
                kind, m, hp, n = t
                src = bJ[pos % 2]
                if kind == "w":
                    wait(dve, t_j, number + 1)
                    dst = x_acc[:, 2 * n:2 * n + 2, :]
                    if n == 0:
                        wait(dve, v_w, pl.w_done_count(0, final) - 1)
                    dve.tensor_tensor(dst, src[:, :].rearrange("p (a b) -> p a b", a=2), dst, ALU.add).then_inc(v_w, 1)
                elif kind == "ctx":
                    dve.wait_ge(a_c, n + 1)
                    dve.tensor_tensor(cT_lo[:, n, :, :].rearrange("p a b -> p (a b)"), src[:, :],
                                      cT_hi[:, n, :, :].rearrange("p a b -> p (a b)"), ALU.subtract).then_inc(v_c, 1)
                elif kind == "v":
                    wait(dve, a_v, pl.v_count(n))
                    sl = v_lo[:, 2 * n:2 * n + 2, :, :].rearrange("p t h d -> p (t h d)")
                    hi = v_hi[:, 2 * n:2 * n + 2, :, :].rearrange("p t h d -> p (t h d)")
                    dve.tensor_tensor(sl, src[:, :], hi, ALU.subtract).then_inc(v_v, 1)
                else:
                    wait(dve, a_qk, pos + 1 if pl is None else pl.qk_count(t))
                    g_h = 0 if pl is None else (pl.g + (1 if kind == "next" else 0)) * 2 + hp
                    dve.scalar_tensor_tensor(out=qk_lo[:, hp, m, n * HALF:(n + 1) * HALF], in0=src[:, :],
                                             scalar=b_col[:, bass.ds(g_h + m * H, 1)],
                                             in1=qk_hi[:, hp, m, n * HALF:(n + 1) * HALF],
                                             op0=ALU.add, op1=ALU.subtract).then_inc(v_qk, 1)

            for pos, t in enumerate(PRO_TILES):
                if pos == 1:
                    ln_low(dve, 0, 1, FIRST[1])
                proj_low(None, t, pos, pos)

            def body(pl):
                for i in range(PAIRS + (DRAIN + 2 if pl.last else 0)):
                    if i < PAIRS:
                        p = pl.pair(i)
                        wait(dve, t_sc, p + 1)
                        dve.tensor_reduce(rmax[:, i % 2, :], bS[i % 2][:, :].rearrange("p (q k) -> p q k", q=2),
                                          AX.X, ALU.max).then_inc(v_m1, 1)
                        wait(dve, v_m1, p + 1)
                        wait(dve, a_exp, p - 1 if not (pl.first and i < 2) else 0)
                        dve.tensor_scalar(nmax[:, i % 2, :], rmax[:, i % 2, :], -SCALE, None, ALU.mult).then_inc(v_max, 1)
                    for tile in pl.of_slot(i - 1, 1):
                        proj_low(pl, *tile)
                    if not (pl.first and i < 1) and i < PAIRS + 1:
                        j = i - 1
                        wait(dve, a_exp, pl.pair(j) + 1)
                        dve.reciprocal(rinv[:, j % 2, :], rsum[:, j % 2, :]).then_inc(v_ri, 1)
                        wait(dve, v_ri, pl.pair(j) + 1)
                        for qt in range(2):
                            sc = dve.tensor_scalar(prob[:, j % 4, qt, :], prob[:, j % 4, qt, :],
                                                   rinv[:, j % 2, qt:qt + 1], None, ALU.mult)
                        sc.then_inc(v_p, 1)
                    for tile in pl.of_slot(i, 0):
                        proj_low(pl, *tile)
                    if not (pl.first and i < TURN) and i < PAIRS + TURN:
                        j = i - TURN
                        wait(dve, a_pT, pl.pair(j) + 1)
                        dve.tensor_tensor(pT_lo[:, j % 2, :, :].rearrange("p a b -> p (a b)"), bP[j % 2][:, :],
                                          pT_hi[:, j % 2, :, :].rearrange("p a b -> p (a b)"), ALU.subtract).then_inc(v_pT, 1)
                    if not (pl.first and i < ATTEND) and i < PAIRS + ATTEND:
                        j = i - ATTEND
                        hp, b = (j % PAIRS) // B, j % B
                        wait(dve, a_o, pl.pair(j) + 1)
                        head = pl.g * 2 + (hp if j >= 0 else hp - 2) + 2 * H
                        dve.scalar_tensor_tensor(out=oT_lo[:, hp, b * S:(b + 1) * S], in0=bO[j % 2][:, 0:S],
                                                 scalar=b_col[:, bass.ds(head, 1)], in1=oT_hi[:, hp, b * S:(b + 1) * S],
                                                 op0=ALU.add, op1=ALU.subtract).then_inc(v_o, 1)
                    if pl.last and i == PAIRS + 2:
                        dve.wait_ge(v_w, 4 * G - 1)
                        for part in ln_vector(dve, 1, 0, x_acc):
                            part()

            over_groups(dve, body)
            statistics, variances, reciprocals, rows = ln_vector(dve, 1, 1, x_acc)
            dve.wait_ge(v_w, 4 * G + 1)
            ln_low(dve, 1, 0, ENDS[0])
            statistics()
            variances()
            reciprocals()
            rows()
            dve.wait_ge(t_rw, 1)
            dve.tensor_copy(rwT[:, :, :].rearrange("p k e -> p (k e)"), bank[5][:, 0:KT * NE]).then_inc(v_rw, 1)

            def routed_low(n):
                dve.wait_ge(a_g, n + 1)
                dve.tensor_tensor(gu_lo[:, n % 2, :], gm[:, n % 4, :], gu_hi[:, n % 2, :], ALU.subtract).then_inc(v_g, 1)

            def add_routed(half):
                dve.wait_ge(t_y, (half + 1) * RSTEPS // 2)
                for j in range(2):
                    t = half * HT + 2 * j
                    dve.tensor_tensor(x_acc[:, t:t + 2, :], ENDS[half][j][:, :].rearrange("p (a b) -> p a b", a=2),
                                      x_acc[:, t:t + 2, :], ALU.add).then_inc(v_y, 1)
                dve.wait_ge(v_y, 2 * half + 2)

            statistics, variances, reciprocals, rows = ln_vector(dve, 2, 0, x_acc)
            between = {4: lambda: ln_low(dve, 1, 1, ENDS[1]), 12: lambda: add_routed(0), 13: statistics, 14: variances}
            for n in range(RSTEPS):
                if n >= 1:
                    routed_low(n - 1)
                dve.wait_ge(p_gm, n + 1)
                dve.tensor_tensor(gm[:, n % 4, :], Z_BANKS[n % 4][:, :], gact[:, n % 4, :], ALU.mult).then_inc(v_t, 1)
                if n in between:
                    between[n]()
            reciprocals()
            routed_low(RSTEPS - 1)
            rows()
            add_routed(1)
            statistics, variances, reciprocals, rows = ln_vector(dve, 2, 1, x_acc)
            for part in (statistics, variances, reciprocals, rows):
                part()

            def product(n, count):
                wait(dve, a_s, count + 1)
                wait(dve, t_hT, count - 1)
                dve.tensor_tensor(hid[:, n % 2, :], bG[n % 2][:, FI:2 * FI], sg[:, n % 2, :], ALU.mult).then_inc(v_h, 1)

            def add_shared(t):
                dve.wait_ge(t_dn, t + 1)
                dve.tensor_tensor(x_acc[:, t, :], bY[t % 2][:, 0:D], x_acc[:, t, :], ALU.add).then_inc(v_sh, 1)

            product(0, 0)
            product(1, 1)
            dve.wait_ge(t_ln, 12)
            dve.tensor_copy(hT_f[:, 1, HALF:2 * HALF], ENDS[1][1][:, :]).then_inc(v_hf, 1)
            product(2, 2)

            done = [0]

            def own(ins):
                done[0] += 1
                ins.then_inc(v_own, 1)
                dve.wait_ge(v_own, done[0])

            dve.wait_ge(a_r, 1)
            dve.wait_ge(d_r, 32)
            own(dve.tensor_tensor(sel[:, :, :], score[:, :, :], rb[:, :].unsqueeze(1).to_broadcast([P, NT, NE]), ALU.add))
            for t in range(NT):
                ins = dve.max(top[:, t, :], sel[:, t, :])
            own(ins)
            product(3, 3)
            for t in range(NT):
                ins = dve.max_index(topi[:, t, :], top[:, t, :], sel[:, t, :])
            own(ins)
            add_shared(0)
            own(dve.tensor_copy(chosen[:, :, :], topi[:, :, 0:TOPK].rearrange("p t k -> p k t")))
            product(4, 4)
            dve.wait_ge(p_many, 1)
            own(dve.tensor_tensor(hot[:, :, :, :].rearrange("p e k t -> p e (k t)"), iota_e[:, :, :],
                                  chosen[:, :, :].rearrange("p k t -> p (k t)").unsqueeze(1).to_broadcast([P, NE, CH]),
                                  ALU.is_equal))
            add_shared(1)
            own(dve.tensor_tensor(two[:, :, :, :], hot[:, :, 0:2, :], hot[:, :, 2:4, :], ALU.add))
            product(5, 5)
            dve.tensor_tensor(member[:, :, :].rearrange("p t e -> p e t"), two[:, :, 0, :], two[:, :, 1, :],
                              ALU.add).then_inc(v_r, 1)
            add_shared(2)
            product(6, 6)
            dve.wait_ge(p_const, 8)
            dve.wait_ge(t_r, 2)
            own(dve.tensor_copy(count[:, :], bank[1][0:NE, 0:1]))
            own(dve.tensor_scalar(over[:, :], iota_f[:, :], count[:, 0:1], None, ALU.is_lt))
            own(dve.tensor_reduce(tiles_e[:, :], over[:, :], AX.X, ALU.add))
            dve.tensor_scalar(tiles_b[:, :], ones[0:NE, :], tiles_e[:, 0:1], None, ALU.mult).then_inc(v_r, 1)
            product(7, 7)
            add_shared(3)
            dve.wait_ge(t_r, 3)
            own(dve.tensor_copy(end_e[:, :], bank[1][0:NE, 0:1]))
            dve.tensor_scalar(past[:, :], iota_t[0:NE, :], end_e[:, 0:1], None, ALU.is_ge).then_inc(v_r, 1)
            own(dve.tensor_scalar(base[:, :], bank[1][:, NE:2 * NE], float(SLOTS), None, ALU.mult))
            own(dve.tensor_tensor(place[:, :, :].rearrange("p e t -> p t e"),
                                  bank[0][:, 0:NT * NE].rearrange("p (t e) -> p t e", e=NE),
                                  base[:, :].unsqueeze(1).to_broadcast([P, NT, NE]), ALU.add))
            add_shared(4)
            own(dve.tensor_tensor(work[:, :, :, :], hot[:, :, :, :],
                                  place[:, :, :].unsqueeze(2).to_broadcast([P, NE, TOPK, NT]), ALU.mult))
            own(dve.tensor_reduce(slot_f[:, :, :], work[:, :, :, :].rearrange("p e k t -> p k t e"), AX.X, ALU.add))
            own(dve.tensor_copy(slot_i[:, :, :], slot_f[:, :, :]))
            flat = slot_i[:, :, :].rearrange("p k t -> p (k t)")
            dve.tensor_scalar(part_i[:, 0, :], flat, 7, None, ALU.logical_shift_right)
            own(dve.tensor_scalar(part_i[:, 1, :], flat, SLOTS - 1, None, ALU.bitwise_and))
            own(dve.tensor_copy(part_h[:, :, :], part_i[:, :, :]))
            dve.wait_ge(p_many, 4)
            dve.tensor_tensor(in_slot[:, :, :], iota_s[:, :, :], part_h[:, 1, :].unsqueeze(1).to_broadcast([P, SLOTS, CH]),
                              ALU.is_equal)
            own(dve.tensor_tensor(in_tile[:, :, :], iota_tc[:, :, :], part_h[:, 0, :].unsqueeze(1).to_broadcast([P, TILES, CH]),
                                  ALU.is_equal))
            dve.tensor_tensor(in_tile[:, :, :], in_tile[:, :, :], tok_id[:, :, :], ALU.mult).then_inc(v_r, 1)
            dve.wait_ge(t_r, 4)
            dve.tensor_copy(used[:, :], bank[2][0:1, TILES:TILES + 1])
            own(dve.tensor_scalar(expert[:, :], bank[2][0:1, 0:TILES], float(NE - 1), None, ALU.min))
            dve.tensor_scalar(column_of[:, :], expert[:, :], float(EW), None, ALU.mult).then_inc(v_r, 1)
            add_shared(5)
            dve.wait_ge(t_r, 5)
            dve.tensor_copy(source[:, :], bank[0][:, 0:TILES]).then_inc(v_r, 1)
            for t in (6, 7):
                add_shared(t)
            def row_copy(j, u):
                wait(dve, t_x, j + 1)
                wait(dve, t_gu, j - 1 + SH)
                dve.tensor_copy(xT[:, u % 2, :], bX[u % 2][:, 0:D]).then_inc(v_x, 1)

            own(dve.tensor_tensor(work[:, :, :, :], hot[:, :, :, :],
                                  score[:, :, :].rearrange("p t e -> p e t").unsqueeze(2).to_broadcast([P, NE, TOPK, NT]),
                                  ALU.mult))
            own(dve.tensor_reduce(gain[:, :, :], work[:, :, :, :].rearrange("p e k t -> p k t e"), AX.X, ALU.add))
            row_copy(0, 0)
            own(dve.tensor_reduce(gsum[:, :], gain[:, :, :].rearrange("p k t -> p t k"), AX.X, ALU.add))
            own(dve.tensor_scalar(gsum[:, :], gsum[:, :], 1e-20, None, ALU.add))
            own(dve.reciprocal(gsum[:, :], gsum[:, :]))
            own(dve.tensor_tensor(gain[:, :, :], gain[:, :, :], gsum[:, :].unsqueeze(1).to_broadcast([P, TOPK, NT]), ALU.mult))

            def trip(it, last):
                for u in range(STEPS):
                    j = it * STEPS + u
                    if u < STEPS - 1 or not last:
                        row_copy(j + 1, u + 1)
                    product(u, j + SH)

            with dve.Fori(0, TRIPS - 1) as it:
                trip(it, False)
            trip(TRIPS - 1, True)

            dve.wait_ge(v_sh, NT)
            for n, (t, k) in enumerate(combine_order):
                dve.wait_ge(d_yg[t][k // 2], TOPK // 2 * 16)
                wait(dve, v_cmb, n - 1 if k else 0)
                dve.scalar_tensor_tensor(out=x_acc[:, t, :], in0=yg[k // 2][:, k % 2, t, :], scalar=gain[:, k, t:t + 1],
                                         in1=x_acc[:, t, :], op0=ALU.mult, op1=ALU.add).then_inc(v_cmb, 1)


_INS = {"x": "x", "tok": "itok_BxS_13_99985", "ctx": "ctx_2048",
        **{n: f"L0_attn_{n}" for n in ("wq_codes", "wq_scales", "bq", "wk_codes", "wk_scales", "bk",
                                       "wv_codes", "wv_scales", "bv", "wo_codes", "wo_scales", "bo")},
        **{n: f"L0_ffn_{n}" for n in ("router_w", "bias", "w_gate", "w_up", "w_down",
                                      "sw_gate", "sw_up", "sw_down")}}


def kernel(**inputs):
    import numpy as _np
    import concourse.bacc as _bacc
    from concourse import mybir as _mybir
    from concourse.bass_utils import run_bass_kernel_spmd as _run

    nc = _bacc.Bacc("TRN2", target_bir_lowering=False, num_devices=1)
    arrays, args = {}, {}
    for short, name in _INS.items():
        arr = _np.ascontiguousarray(inputs[name])
        arrays[f"in_{short}"] = arr
        args[short] = nc.dram_tensor(f"in_{short}", arr.shape, _mybir.dt.from_np(arr.dtype), kind="ExternalInput").ap()
    out = nc.dram_tensor("out_0", (B, S, D), _mybir.dt.float32, kind="ExternalOutput").ap()
    decoder_layer(nc, args, out)
    r = _run(nc, [arrays], core_ids=[0])
    return r.results[0]["out_0"]
```
